# Optimizing a Trainium2 kernel written in Bass

```python
import numpy as np
import jax
import jax.numpy as jnp

def _softmax(x, axis=-1):
    return jax.nn.softmax(x, axis=axis)

def _gelu(x):
    return jax.nn.gelu(x, approximate=True)

def _silu(x):
    return jax.nn.silu(x)

def _sigmoid(x):
    return jax.nn.sigmoid(x)

def _layernorm(x, axis=-1, eps=1e-05):
    m = jnp.mean(x, axis=axis, keepdims=True)
    v = jnp.var(x, axis=axis, keepdims=True)
    return (x - m) / jnp.sqrt(v + eps)

def _scatter_add(tgt, idx, src, axis=0):
    return tgt.at[idx].add(src)

def _segment_sum(src, seg, n):
    return jax.ops.segment_sum(src, seg, n)
kernel_name = 'mk_decoder_postln_d2_seqx_r8_9cb6c8'

def setup_inputs(seed: int=0):
    np.random.seed(seed)
    _w = jnp.asarray

    def _rec_inputs():
        import jax
        import jax.numpy as jnp
        _rk = jax.random.key(seed)
        x = -0.0002928 + 1 * jax.random.normal(jax.random.fold_in(_rk, 1), (8, 256, 128), jnp.float32)
        _lenS = 256 - jax.random.randint(jax.random.fold_in(_rk, 7), (8,), 0, max(1, 256 // 4) + 1, jnp.int32)
        _lenS2 = 1601 - jax.random.randint(jax.random.fold_in(_rk, 8), (8,), 0, max(1, 1601 // 4) + 1, jnp.int32)
        _ctx_512P = jax.random.normal(jax.random.fold_in(_rk, 11), (8, 16, 64), jnp.float32)
        _ctx_512c = jax.random.dirichlet(jax.random.fold_in(_rk, 511), 0.3 * jnp.ones((16,), jnp.float32), (8, 1601))
        _ctx_512t = jnp.einsum('bsk,bkd->bsd', _ctx_512c, _ctx_512P)
        _ctx_512t = _ctx_512t * jax.lax.rsqrt(jnp.mean(jnp.square(_ctx_512t)) + 1e-12) * 0.953939
        ctx_512 = 0.00222621 + 0.99962 * (_ctx_512t + 0.3 * jax.random.normal(jax.random.fold_in(_rk, 611), (8, 1601, 64), jnp.float32))
        return (x, ctx_512)
    x, ctx_512 = _rec_inputs()

    def _L0_attn_setup():
        import jax, jax.numpy as jnp
        import numpy as np
        import math
        D_MODEL, D_C, D_R, NH = (128, 128, 32, 16)
        HD = D_MODEL // NH
        B, T = (2, 256)

        def _rope_tables(T, d_R):
            inv_freq = 1.0 / 10000.0 ** (jnp.arange(0, d_R, 2, dtype=jnp.float32) / d_R)
            t = jnp.arange(T, dtype=jnp.float32)
            freqs = jnp.outer(t, inv_freq)
            return (jnp.cos(freqs), jnp.sin(freqs))

        def _rotary_apply(x, cos, sin):
            d = x.shape[-1]
            x1, x2 = (x[..., :d // 2], x[..., d // 2:])
            return jnp.concatenate([x1 * cos - x2 * sin, x2 * cos + x1 * sin], axis=-1)
        key = jax.random.key(seed)
        ks = jax.random.split(key, 8)
        s = lambda fan_in: 1.0 / math.sqrt(fan_in)
        return {'x': jax.random.normal(ks[0], (B, T, D_MODEL), jnp.float32), 'W_kv_down': jax.random.normal(ks[1], (D_MODEL, D_C), jnp.float32) * s(D_MODEL), 'W_k_up': jax.random.normal(ks[2], (D_C, D_MODEL), jnp.float32) * s(D_C), 'W_v_up': jax.random.normal(ks[3], (D_C, D_MODEL), jnp.float32) * s(D_C), 'W_q': jax.random.normal(ks[4], (D_MODEL, D_MODEL), jnp.float32) * s(D_MODEL), 'W_q_rope': jax.random.normal(ks[5], (D_MODEL, D_R), jnp.float32) * s(D_MODEL), 'W_k_rope': jax.random.normal(ks[6], (D_C, D_R), jnp.float32) * s(D_C), 'W_o': jax.random.normal(ks[7], (D_MODEL, D_MODEL), jnp.float32) * s(D_MODEL)}
    _L0_attn_all = _L0_attn_setup()
    _L0_attn_in = {k: v for k, v in _L0_attn_all.items() if k in ('W_kv_down', 'W_k_up', 'W_v_up', 'W_q', 'W_q_rope', 'W_k_rope', 'W_o')}
    del _L0_attn_all

    def _L0_xattn_setup():
        import jax, jax.numpy as jnp
        import numpy as np
        B, T, TC, C, CC, H = (2, 256, 64, 128, 64, 16)
        D = C // H

        def _heads(t):
            b, l, _ = t.shape
            return t.reshape(b, l, H, D).transpose(0, 2, 1, 3)
        key = jax.random.key(seed)
        ks = jax.random.split(key, 18)
        w = lambda k, i, o: jax.random.normal(k, (i, o), jnp.float32) / np.sqrt(i).astype(np.float32)
        return {'x': jax.random.normal(ks[0], (B, T, C), jnp.float32), 'cross_input': jax.random.normal(ks[1], (B, TC, CC), jnp.float32), 'Wk': w(ks[2], C, C), 'bk': jnp.zeros((C,), jnp.float32), 'Wq': w(ks[3], C, C), 'bq': jnp.zeros((C,), jnp.float32), 'Wv': w(ks[4], C, C), 'bv': jnp.zeros((C,), jnp.float32), 'Wck': w(ks[5], CC, C), 'bck': jnp.zeros((C,), jnp.float32), 'Wcq': w(ks[6], C, C), 'bcq': jnp.zeros((C,), jnp.float32), 'Wcv': w(ks[7], CC, C), 'bcv': jnp.zeros((C,), jnp.float32), 'Wp': w(ks[8], C, C), 'bp': jnp.zeros((C,), jnp.float32)}
    _L0_xattn_all = _L0_xattn_setup()
    _L0_xattn_in = {k: v for k, v in _L0_xattn_all.items() if k in ('Wk', 'bk', 'Wq', 'bq', 'Wv', 'bv', 'Wck', 'bck', 'Wcq', 'bcq', 'Wcv', 'bcv', 'Wp', 'bp')}
    del _L0_xattn_all

    def _L0_ffn_setup():
        import jax, jax.numpy as jnp
        import numpy as np
        import math
        B, T, D, H, E, TOPK, CAPF = (4, 256, 128, 16, 8, 2, 2.0)
        HD = D // H

        def layernorm(x, g, b, eps=1e-05):
            m = jnp.mean(x, -1, keepdims=True)
            v = jnp.mean(jnp.square(x - m), -1, keepdims=True)
            return (x - m) * jax.lax.rsqrt(v + eps) * g + b

        def block_forward(x, ln1_g, ln1_b, Wqkv, Wproj, ln2_g, ln2_b, Wgate, W1, b1, W2, b2):
            Bb, Tt, d = x.shape
            hd = HD
            half = hd // 2
            h = layernorm(x, ln1_g, ln1_b)
            qkv = (h @ Wqkv).reshape(Bb, Tt, H, 3 * hd)
            q, k, v = (qkv[..., :hd], qkv[..., hd:2 * hd], qkv[..., 2 * hd:])
            inv_freq = 1.0 / 10000.0 ** (jnp.arange(0, hd, 2, dtype=jnp.float32) / hd)
            ang = jnp.arange(Tt, dtype=jnp.float32)[:, None] * inv_freq
            sin = jnp.sin(ang)[None, :, None, :].astype(x.dtype)
            cos = jnp.cos(ang)[None, :, None, :].astype(x.dtype)

            def rope(t):
                t1, t2 = (t[..., :half], t[..., half:])
                return jnp.concatenate([t1 * cos - t2 * sin, t1 * sin + t2 * cos], -1)
            q, k = (rope(q), rope(k))
            scores = jnp.einsum('bqhd,bkhd->bhqk', q, k) / math.sqrt(hd)
            causal = jnp.tril(jnp.ones((Tt, Tt), dtype=bool))
            scores = jnp.where(causal, scores, jnp.asarray(-1000000000.0, scores.dtype))
            probs = jax.nn.softmax(scores, axis=-1)
            attn = jnp.einsum('bhqk,bkhd->bqhd', probs, v).reshape(Bb, Tt, d) @ Wproj
            x = x + attn
            h2 = layernorm(x, ln2_g, ln2_b)
            flat = h2.reshape(-1, d)
            N = flat.shape[0]
            capacity = int(math.ceil(CAPF * N / E))
            gates = jax.nn.softmax((flat @ Wgate).astype(jnp.float32), -1).astype(flat.dtype)
            _, top_inds = jax.lax.top_k(gates, TOPK)
            mask = jnp.zeros((N, E), dtype=bool).at[jnp.arange(N)[:, None], top_inds].set(True)
            pos = jnp.cumsum(mask.astype(jnp.int32), axis=0) * mask - 1
            keep = (pos < capacity) & mask
            t_flat = jnp.repeat(jnp.arange(N), TOPK)
            e_flat = top_inds.reshape(-1)
            p = pos[t_flat, e_flat]
            kp = keep[t_flat, e_flat]
            p_eff = jnp.where(kp, p, capacity)
            exp_in = jnp.zeros((E, capacity, d), flat.dtype).at[e_flat, p_eff].set(flat[t_flat], mode='drop')
            hmid = jax.nn.gelu(jnp.einsum('ecd,edf->ecf', exp_in, W1) + b1[:, None, :], approximate=False)
            exp_out = jnp.einsum('ecf,efd->ecd', hmid, W2) + b2[:, None, :]
            gate = gates[t_flat, e_flat] * kp.astype(flat.dtype)
            p_g = jnp.minimum(p_eff, capacity - 1)
            moe = jnp.zeros((N, d), flat.dtype).at[t_flat].add(exp_out[e_flat, p_g] * gate[:, None])
            return x + moe.reshape(Bb, Tt, d)
        key = jax.random.key(seed)
        ks = jax.random.split(key, 8)
        s = 0.02
        return {'x': jax.random.normal(ks[0], (B, T, D), jnp.float32), 'ln1_g': jnp.ones((D,), jnp.float32), 'ln1_b': jnp.zeros((D,), jnp.float32), 'Wqkv': jax.random.normal(ks[1], (D, 3 * D), jnp.float32) * s, 'Wproj': jax.random.normal(ks[2], (D, D), jnp.float32) * s, 'ln2_g': jnp.ones((D,), jnp.float32), 'ln2_b': jnp.zeros((D,), jnp.float32), 'Wgate': jax.random.normal(ks[3], (D, E), jnp.float32) * s, 'W1': jax.random.normal(ks[4], (E, D, 4 * D), jnp.float32) * s, 'b1': jnp.zeros((E, 4 * D), jnp.float32), 'W2': jax.random.normal(ks[5], (E, 4 * D, D), jnp.float32) * s, 'b2': jnp.zeros((E, D), jnp.float32)}
    _L0_ffn_all = _L0_ffn_setup()
    _L0_ffn_in = {k: v for k, v in _L0_ffn_all.items() if k in ('ln1_g', 'ln1_b', 'Wqkv', 'Wproj', 'ln2_g', 'ln2_b', 'Wgate', 'W1', 'b1', 'W2', 'b2')}
    del _L0_ffn_all

    def _L1_attn_setup():
        import jax, jax.numpy as jnp
        import numpy as np
        key = jax.random.key(seed)
        k0, k1, k2, k3 = jax.random.split(key, 4)
        B, T, D = (4, 256, 128)
        s = 1.0 / np.sqrt(D)
        return {'inputs': jax.random.normal(k0, (B, T, D), dtype=jnp.float32), 'Wq': jax.random.normal(k1, (D, D), dtype=jnp.float32) * s, 'Wk': jax.random.normal(k2, (D, D), dtype=jnp.float32) * s, 'Wv': jax.random.normal(k3, (D, D), dtype=jnp.float32) * s}
    _L1_attn_all = _L1_attn_setup()
    _L1_attn_in = {k: v for k, v in _L1_attn_all.items() if k in ('Wq', 'Wk', 'Wv')}
    del _L1_attn_all

    def _L1_xattn_setup():
        import jax, jax.numpy as jnp
        import numpy as np
        H, D, C1, C2, S, M, B, W = (16, 32, 128, 64, 256, 64, 2, 4)

        def _ln(x, g, b):
            m = jnp.mean(x, -1, keepdims=True)
            v = jnp.var(x, -1, keepdims=True)
            return (x - m) * jax.lax.rsqrt(v + 1e-05) * g + b

        def _mha(x, y, wq, wk, wv, li1_w, li1_b, lnx_g, lnx_b, lny_g, lny_b, ln3_g, ln3_b, li2_w, li2_b, li3_w, li3_b, causal):
            xn = _ln(x, lnx_g, lnx_b)
            yn = _ln(y, lny_g, lny_b)
            q = jnp.einsum('bsc,hcd->bhsd', xn, wq)
            k = jnp.einsum('btc,hcd->bhtd', yn, wk)
            v = jnp.einsum('btc,hcd->bhtd', yn, wv)
            a = jax.nn.softmax(jnp.einsum('bhsd,bhtd->bhst', q, k) * D ** (-0.5), axis=-1)
            if causal:
                s, t = (a.shape[-2], a.shape[-1])
                mask = (jnp.arange(t)[None, :] > jnp.arange(s)[:, None]).astype(a.dtype)
                a = a * mask
            o = jnp.einsum('bhst,bhtd->bhsd', a, v)
            o = o.transpose(0, 2, 1, 3).reshape(x.shape[0], x.shape[1], H * D)
            x_out = x + o @ li1_w + li1_b
            h = jax.nn.gelu(_ln(x_out, ln3_g, ln3_b) @ li2_w + li2_b, approximate=False)
            return x_out + h @ li3_w + li3_b
        key = jax.random.key(seed)
        ks = iter(jax.random.split(key, 64))

        def w(shape, scale=0.02):
            return jax.random.normal(next(ks), shape, jnp.float32) * scale
        inp = {'xx': jax.random.normal(next(ks), (B, S, C1), jnp.float32), 'ee': jax.random.normal(next(ks), (B, M, C2), jnp.float32), 'ln1_g': jnp.ones(C1, jnp.float32), 'ln1_b': jnp.zeros(C1, jnp.float32), 'ln2_g': jnp.ones(C1, jnp.float32), 'ln2_b': jnp.zeros(C1, jnp.float32)}
        for pfx, cy in (('a1', C1), ('a2', C2)):
            inp[pfx + '_wq'] = w((H, C1, D))
            inp[pfx + '_wk'] = w((H, cy, D))
            inp[pfx + '_wv'] = w((H, cy, D))
            inp[pfx + '_li1_w'] = w((H * D, C1))
            inp[pfx + '_li1_b'] = jnp.zeros(C1, jnp.float32)
            inp[pfx + '_lnx_g'] = jnp.ones(C1, jnp.float32)
            inp[pfx + '_lnx_b'] = jnp.zeros(C1, jnp.float32)
            inp[pfx + '_lny_g'] = jnp.ones(cy, jnp.float32)
            inp[pfx + '_lny_b'] = jnp.zeros(cy, jnp.float32)
            inp[pfx + '_ln3_g'] = jnp.ones(C1, jnp.float32)
            inp[pfx + '_ln3_b'] = jnp.zeros(C1, jnp.float32)
            inp[pfx + '_li2_w'] = w((C1, C1 * W))
            inp[pfx + '_li2_b'] = jnp.zeros(C1 * W, jnp.float32)
            inp[pfx + '_li3_w'] = w((C1 * W, C1))
            inp[pfx + '_li3_b'] = jnp.zeros(C1, jnp.float32)
        inp['training'] = 0
        return inp
    _L1_xattn_all = _L1_xattn_setup()
    _L1_xattn_in = {k: v for k, v in _L1_xattn_all.items() if k in ('ln1_g', 'ln1_b', 'ln2_g', 'ln2_b', 'a1_wq', 'a1_wk', 'a1_wv', 'a1_li1_w', 'a1_li1_b', 'a1_lnx_g', 'a1_lnx_b', 'a1_lny_g', 'a1_lny_b', 'a1_ln3_g', 'a1_ln3_b', 'a1_li2_w', 'a1_li2_b', 'a1_li3_w', 'a1_li3_b', 'a2_wq', 'a2_wk', 'a2_wv', 'a2_li1_w', 'a2_li1_b', 'a2_lnx_g', 'a2_lnx_b', 'a2_lny_g', 'a2_lny_b', 'a2_ln3_g', 'a2_ln3_b', 'a2_li2_w', 'a2_li2_b', 'a2_li3_w', 'a2_li3_b')}
    del _L1_xattn_all

    def _L1_ffn_setup():
        import jax, jax.numpy as jnp
        import numpy as np
        E, G, TOPK = (32, 16, 2)
        HID, INTER, A_INTER = (128, 256, 128)
        CAP_FACTOR = 1.25
        SCALE = 0.05

        def _stats(x):
            mean = x.mean(-1, keepdims=True)
            std = jnp.std(x, axis=-1, keepdims=True, ddof=1)
            mn = x.min(-1, keepdims=True)
            mx = x.max(-1, keepdims=True)
            l2 = jnp.linalg.norm(x, axis=-1, keepdims=True)
            sp = (jnp.abs(x) < 1e-06).astype(x.dtype).mean(-1, keepdims=True)
            return jnp.concatenate([mean, std, mn, mx, l2, sp], -1)
        key = jax.random.key(seed)
        ks = jax.random.split(key, 8)
        B, N = (4, 128)
        s = lambda k, shape, sc: jax.random.normal(k, shape, jnp.float32) * sc
        return {'x': jax.random.normal(ks[0], (B, N, HID), jnp.float32), 'r1_w': s(ks[1], (HID // 2, HID + 6), 0.02), 'r1_b': jnp.zeros((HID // 2,), jnp.float32), 'r2_w': s(ks[2], (E, HID // 2), 0.02), 'w_up': s(ks[3], (E, 2 * INTER, HID), 0.02), 'w_down': s(ks[4], (E, HID, INTER), 0.02), 'a_up': s(ks[5], (G, 2 * A_INTER, HID), 0.02), 'a_down': s(ks[6], (G, HID, A_INTER), 0.02)}
    _L1_ffn_all = _L1_ffn_setup()
    _L1_ffn_in = {k: v for k, v in _L1_ffn_all.items() if k in ('r1_w', 'r1_b', 'r2_w', 'w_up', 'w_down', 'a_up', 'a_down')}
    del _L1_ffn_all
    return {'x': x, 'ctx_512': ctx_512, 'L0_attn_W_kv_down': _L0_attn_in['W_kv_down'], 'L0_attn_W_k_up': _L0_attn_in['W_k_up'], 'L0_attn_W_v_up': _L0_attn_in['W_v_up'], 'L0_attn_W_q': _L0_attn_in['W_q'], 'L0_attn_W_q_rope': _L0_attn_in['W_q_rope'], 'L0_attn_W_k_rope': _L0_attn_in['W_k_rope'], 'L0_attn_W_o': _L0_attn_in['W_o'], 'L0_xattn_Wk': _L0_xattn_in['Wk'], 'L0_xattn_bk': _L0_xattn_in['bk'], 'L0_xattn_Wq': _L0_xattn_in['Wq'], 'L0_xattn_bq': _L0_xattn_in['bq'], 'L0_xattn_Wv': _L0_xattn_in['Wv'], 'L0_xattn_bv': _L0_xattn_in['bv'], 'L0_xattn_Wck': _L0_xattn_in['Wck'], 'L0_xattn_bck': _L0_xattn_in['bck'], 'L0_xattn_Wcq': _L0_xattn_in['Wcq'], 'L0_xattn_bcq': _L0_xattn_in['bcq'], 'L0_xattn_Wcv': _L0_xattn_in['Wcv'], 'L0_xattn_bcv': _L0_xattn_in['bcv'], 'L0_xattn_Wp': _L0_xattn_in['Wp'], 'L0_xattn_bp': _L0_xattn_in['bp'], 'L0_ffn_ln1_g': _L0_ffn_in['ln1_g'], 'L0_ffn_ln1_b': _L0_ffn_in['ln1_b'], 'L0_ffn_Wqkv': _L0_ffn_in['Wqkv'], 'L0_ffn_Wproj': _L0_ffn_in['Wproj'], 'L0_ffn_ln2_g': _L0_ffn_in['ln2_g'], 'L0_ffn_ln2_b': _L0_ffn_in['ln2_b'], 'L0_ffn_Wgate': _L0_ffn_in['Wgate'], 'L0_ffn_W1': _L0_ffn_in['W1'], 'L0_ffn_b1': _L0_ffn_in['b1'], 'L0_ffn_W2': _L0_ffn_in['W2'], 'L0_ffn_b2': _L0_ffn_in['b2'], 'L1_attn_Wq': _L1_attn_in['Wq'], 'L1_attn_Wk': _L1_attn_in['Wk'], 'L1_attn_Wv': _L1_attn_in['Wv'], 'L1_xattn_ln1_g': _L1_xattn_in['ln1_g'], 'L1_xattn_ln1_b': _L1_xattn_in['ln1_b'], 'L1_xattn_ln2_g': _L1_xattn_in['ln2_g'], 'L1_xattn_ln2_b': _L1_xattn_in['ln2_b'], 'L1_xattn_a1_wq': _L1_xattn_in['a1_wq'], 'L1_xattn_a1_wk': _L1_xattn_in['a1_wk'], 'L1_xattn_a1_wv': _L1_xattn_in['a1_wv'], 'L1_xattn_a1_li1_w': _L1_xattn_in['a1_li1_w'], 'L1_xattn_a1_li1_b': _L1_xattn_in['a1_li1_b'], 'L1_xattn_a1_lnx_g': _L1_xattn_in['a1_lnx_g'], 'L1_xattn_a1_lnx_b': _L1_xattn_in['a1_lnx_b'], 'L1_xattn_a1_lny_g': _L1_xattn_in['a1_lny_g'], 'L1_xattn_a1_lny_b': _L1_xattn_in['a1_lny_b'], 'L1_xattn_a1_ln3_g': _L1_xattn_in['a1_ln3_g'], 'L1_xattn_a1_ln3_b': _L1_xattn_in['a1_ln3_b'], 'L1_xattn_a1_li2_w': _L1_xattn_in['a1_li2_w'], 'L1_xattn_a1_li2_b': _L1_xattn_in['a1_li2_b'], 'L1_xattn_a1_li3_w': _L1_xattn_in['a1_li3_w'], 'L1_xattn_a1_li3_b': _L1_xattn_in['a1_li3_b'], 'L1_xattn_a2_wq': _L1_xattn_in['a2_wq'], 'L1_xattn_a2_wk': _L1_xattn_in['a2_wk'], 'L1_xattn_a2_wv': _L1_xattn_in['a2_wv'], 'L1_xattn_a2_li1_w': _L1_xattn_in['a2_li1_w'], 'L1_xattn_a2_li1_b': _L1_xattn_in['a2_li1_b'], 'L1_xattn_a2_lnx_g': _L1_xattn_in['a2_lnx_g'], 'L1_xattn_a2_lnx_b': _L1_xattn_in['a2_lnx_b'], 'L1_xattn_a2_lny_g': _L1_xattn_in['a2_lny_g'], 'L1_xattn_a2_lny_b': _L1_xattn_in['a2_lny_b'], 'L1_xattn_a2_ln3_g': _L1_xattn_in['a2_ln3_g'], 'L1_xattn_a2_ln3_b': _L1_xattn_in['a2_ln3_b'], 'L1_xattn_a2_li2_w': _L1_xattn_in['a2_li2_w'], 'L1_xattn_a2_li2_b': _L1_xattn_in['a2_li2_b'], 'L1_xattn_a2_li3_w': _L1_xattn_in['a2_li3_w'], 'L1_xattn_a2_li3_b': _L1_xattn_in['a2_li3_b'], 'L1_ffn_r1_w': _L1_ffn_in['r1_w'], 'L1_ffn_r1_b': _L1_ffn_in['r1_b'], 'L1_ffn_r2_w': _L1_ffn_in['r2_w'], 'L1_ffn_w_up': _L1_ffn_in['w_up'], 'L1_ffn_w_down': _L1_ffn_in['w_down'], 'L1_ffn_a_up': _L1_ffn_in['a_up'], 'L1_ffn_a_down': _L1_ffn_in['a_down']}

def reference(x, ctx_512, L0_attn_W_kv_down, L0_attn_W_k_up, L0_attn_W_v_up, L0_attn_W_q, L0_attn_W_q_rope, L0_attn_W_k_rope, L0_attn_W_o, L0_xattn_Wk, L0_xattn_bk, L0_xattn_Wq, L0_xattn_bq, L0_xattn_Wv, L0_xattn_bv, L0_xattn_Wck, L0_xattn_bck, L0_xattn_Wcq, L0_xattn_bcq, L0_xattn_Wcv, L0_xattn_bcv, L0_xattn_Wp, L0_xattn_bp, L0_ffn_ln1_g, L0_ffn_ln1_b, L0_ffn_Wqkv, L0_ffn_Wproj, L0_ffn_ln2_g, L0_ffn_ln2_b, L0_ffn_Wgate, L0_ffn_W1, L0_ffn_b1, L0_ffn_W2, L0_ffn_b2, L1_attn_Wq, L1_attn_Wk, L1_attn_Wv, L1_xattn_ln1_g, L1_xattn_ln1_b, L1_xattn_ln2_g, L1_xattn_ln2_b, L1_xattn_a1_wq, L1_xattn_a1_wk, L1_xattn_a1_wv, L1_xattn_a1_li1_w, L1_xattn_a1_li1_b, L1_xattn_a1_lnx_g, L1_xattn_a1_lnx_b, L1_xattn_a1_lny_g, L1_xattn_a1_lny_b, L1_xattn_a1_ln3_g, L1_xattn_a1_ln3_b, L1_xattn_a1_li2_w, L1_xattn_a1_li2_b, L1_xattn_a1_li3_w, L1_xattn_a1_li3_b, L1_xattn_a2_wq, L1_xattn_a2_wk, L1_xattn_a2_wv, L1_xattn_a2_li1_w, L1_xattn_a2_li1_b, L1_xattn_a2_lnx_g, L1_xattn_a2_lnx_b, L1_xattn_a2_lny_g, L1_xattn_a2_lny_b, L1_xattn_a2_ln3_g, L1_xattn_a2_ln3_b, L1_xattn_a2_li2_w, L1_xattn_a2_li2_b, L1_xattn_a2_li3_w, L1_xattn_a2_li3_b, L1_ffn_r1_w, L1_ffn_r1_b, L1_ffn_r2_w, L1_ffn_w_up, L1_ffn_w_down, L1_ffn_a_up, L1_ffn_a_down):
    import jax
    import jax.numpy as jnp

    def _L0_attn_ref(x, W_kv_down, W_k_up, W_v_up, W_q, W_q_rope, W_k_rope, W_o):
        import jax, jax.numpy as jnp
        import numpy as np
        import math
        D_MODEL, D_C, D_R, NH = (128, 128, 32, 16)
        HD = D_MODEL // NH
        B, T = (2, 256)

        def _rope_tables(T, d_R):
            inv_freq = 1.0 / 10000.0 ** (jnp.arange(0, d_R, 2, dtype=jnp.float32) / d_R)
            t = jnp.arange(T, dtype=jnp.float32)
            freqs = jnp.outer(t, inv_freq)
            return (jnp.cos(freqs), jnp.sin(freqs))

        def _rotary_apply(x, cos, sin):
            d = x.shape[-1]
            x1, x2 = (x[..., :d // 2], x[..., d // 2:])
            return jnp.concatenate([x1 * cos - x2 * sin, x2 * cos + x1 * sin], axis=-1)
        Bb, Tt, _ = x.shape
        cos, sin = _rope_tables(Tt, D_R)
        cos = cos[None]
        sin = sin[None]
        c_kv = x @ W_kv_down
        k_rope = _rotary_apply(c_kv @ W_k_rope, cos, sin)
        k = (c_kv @ W_k_up).reshape(Bb, Tt, NH, HD)
        v = (c_kv @ W_v_up).reshape(Bb, Tt, NH, HD)
        q = (x @ W_q).reshape(Bb, Tt, NH, HD)
        q_rope = _rotary_apply(x @ W_q_rope, cos, sin)
        scale = math.sqrt(HD + D_R)
        scores = jnp.einsum('bqhd,bkhd->bhqk', q, k)
        scores = scores + jnp.einsum('bqr,bkr->bqk', q_rope, k_rope)[:, None]
        scores = scores / scale
        causal = jnp.triu(jnp.ones((Tt, Tt), dtype=bool), k=1)
        scores = jnp.where(causal[None, None], -jnp.inf, scores)
        w = jax.nn.softmax(scores, axis=-1)
        attn = jnp.einsum('bhqk,bkhd->bqhd', w, v).reshape(Bb, Tt, D_MODEL)
        return attn @ W_o

    def _L0_xattn_ref(x, cross_input, Wk, bk, Wq, bq, Wv, bv, Wck, bck, Wcq, bcq, Wcv, bcv, Wp, bp):
        import jax, jax.numpy as jnp
        import numpy as np
        B, T, TC, C, CC, H = (2, 256, 64, 128, 64, 16)
        D = C // H

        def _heads(t):
            b, l, _ = t.shape
            return t.reshape(b, l, H, D).transpose(0, 2, 1, 3)
        scale = np.float32(1.0 / np.sqrt(D))
        q = _heads(x @ Wq + bq)
        k = _heads(x @ Wk + bk)
        v = _heads(x @ Wv + bv)
        att = jnp.einsum('bhqd,bhkd->bhqk', q, k) * scale
        causal = jnp.tril(jnp.ones((T, T), bool))
        att = jnp.where(causal[None, None], att, -jnp.inf)
        y = jnp.einsum('bhqk,bhkd->bhqd', jax.nn.softmax(att, axis=-1), v)
        qc = _heads(x @ Wcq + bcq)
        kc = _heads(cross_input @ Wck + bck)
        vc = _heads(cross_input @ Wcv + bcv)
        attc = jnp.einsum('bhqd,bhkd->bhqk', qc, kc) * scale
        y = y + jnp.einsum('bhqk,bhkd->bhqd', jax.nn.softmax(attc, axis=-1), vc)
        y = y.transpose(0, 2, 1, 3).reshape(x.shape[0], T, C)
        return y @ Wp + bp

    def _L0_ffn_ref(x, ln1_g, ln1_b, Wqkv, Wproj, ln2_g, ln2_b, Wgate, W1, b1, W2, b2):
        import jax, jax.numpy as jnp
        import numpy as np
        import math
        B, T, D, H, E, TOPK, CAPF = (4, 256, 128, 16, 8, 2, 2.0)
        HD = D // H

        def layernorm(x, g, b, eps=1e-05):
            m = jnp.mean(x, -1, keepdims=True)
            v = jnp.mean(jnp.square(x - m), -1, keepdims=True)
            return (x - m) * jax.lax.rsqrt(v + eps) * g + b

        def block_forward(x, ln1_g, ln1_b, Wqkv, Wproj, ln2_g, ln2_b, Wgate, W1, b1, W2, b2):
            Bb, Tt, d = x.shape
            hd = HD
            half = hd // 2
            h = layernorm(x, ln1_g, ln1_b)
            qkv = (h @ Wqkv).reshape(Bb, Tt, H, 3 * hd)
            q, k, v = (qkv[..., :hd], qkv[..., hd:2 * hd], qkv[..., 2 * hd:])
            inv_freq = 1.0 / 10000.0 ** (jnp.arange(0, hd, 2, dtype=jnp.float32) / hd)
            ang = jnp.arange(Tt, dtype=jnp.float32)[:, None] * inv_freq
            sin = jnp.sin(ang)[None, :, None, :].astype(x.dtype)
            cos = jnp.cos(ang)[None, :, None, :].astype(x.dtype)

            def rope(t):
                t1, t2 = (t[..., :half], t[..., half:])
                return jnp.concatenate([t1 * cos - t2 * sin, t1 * sin + t2 * cos], -1)
            q, k = (rope(q), rope(k))
            scores = jnp.einsum('bqhd,bkhd->bhqk', q, k) / math.sqrt(hd)
            causal = jnp.tril(jnp.ones((Tt, Tt), dtype=bool))
            scores = jnp.where(causal, scores, jnp.asarray(-1000000000.0, scores.dtype))
            probs = jax.nn.softmax(scores, axis=-1)
            attn = jnp.einsum('bhqk,bkhd->bqhd', probs, v).reshape(Bb, Tt, d) @ Wproj
            x = x + attn
            h2 = layernorm(x, ln2_g, ln2_b)
            flat = h2.reshape(-1, d)
            N = flat.shape[0]
            capacity = int(math.ceil(CAPF * N / E))
            gates = jax.nn.softmax((flat @ Wgate).astype(jnp.float32), -1).astype(flat.dtype)
            _, top_inds = jax.lax.top_k(gates, TOPK)
            mask = jnp.zeros((N, E), dtype=bool).at[jnp.arange(N)[:, None], top_inds].set(True)
            pos = jnp.cumsum(mask.astype(jnp.int32), axis=0) * mask - 1
            keep = (pos < capacity) & mask
            t_flat = jnp.repeat(jnp.arange(N), TOPK)
            e_flat = top_inds.reshape(-1)
            p = pos[t_flat, e_flat]
            kp = keep[t_flat, e_flat]
            p_eff = jnp.where(kp, p, capacity)
            exp_in = jnp.zeros((E, capacity, d), flat.dtype).at[e_flat, p_eff].set(flat[t_flat], mode='drop')
            hmid = jax.nn.gelu(jnp.einsum('ecd,edf->ecf', exp_in, W1) + b1[:, None, :], approximate=False)
            exp_out = jnp.einsum('ecf,efd->ecd', hmid, W2) + b2[:, None, :]
            gate = gates[t_flat, e_flat] * kp.astype(flat.dtype)
            p_g = jnp.minimum(p_eff, capacity - 1)
            moe = jnp.zeros((N, d), flat.dtype).at[t_flat].add(exp_out[e_flat, p_g] * gate[:, None])
            return x + moe.reshape(Bb, Tt, d)
        return block_forward(x, ln1_g, ln1_b, Wqkv, Wproj, ln2_g, ln2_b, Wgate, W1, b1, W2, b2)

    def _L1_attn_ref(inputs, Wq, Wk, Wv):
        import jax, jax.numpy as jnp
        import numpy as np
        B, T, D = inputs.shape
        q = jnp.einsum('btd,ed->bte', inputs, Wq)
        k = jnp.einsum('btd,ed->bte', inputs, Wk)
        v = jnp.einsum('btd,ed->bte', inputs, Wv)
        scores = jnp.einsum('bqe,bke->bqk', q, k)
        causal = jnp.tril(jnp.ones((T, T), dtype=bool))
        scores = jnp.where(causal, scores, -jnp.inf)
        scale = jnp.asarray(1.0 / np.sqrt(D), dtype=scores.dtype)
        weights = jax.nn.softmax(scores * scale, axis=-1)
        return jnp.einsum('bqk,bke->bqe', weights, v)

    def _L1_xattn_ref(xx, ee, ln1_g, ln1_b, ln2_g, ln2_b, a1_wq, a1_wk, a1_wv, a1_li1_w, a1_li1_b, a1_lnx_g, a1_lnx_b, a1_lny_g, a1_lny_b, a1_ln3_g, a1_ln3_b, a1_li2_w, a1_li2_b, a1_li3_w, a1_li3_b, a2_wq, a2_wk, a2_wv, a2_li1_w, a2_li1_b, a2_lnx_g, a2_lnx_b, a2_lny_g, a2_lny_b, a2_ln3_g, a2_ln3_b, a2_li2_w, a2_li2_b, a2_li3_w, a2_li3_b, training):
        import jax, jax.numpy as jnp
        import numpy as np
        H, D, C1, C2, S, M, B, W = (16, 32, 128, 64, 256, 64, 2, 4)

        def _ln(x, g, b):
            m = jnp.mean(x, -1, keepdims=True)
            v = jnp.var(x, -1, keepdims=True)
            return (x - m) * jax.lax.rsqrt(v + 1e-05) * g + b

        def _mha(x, y, wq, wk, wv, li1_w, li1_b, lnx_g, lnx_b, lny_g, lny_b, ln3_g, ln3_b, li2_w, li2_b, li3_w, li3_b, causal):
            xn = _ln(x, lnx_g, lnx_b)
            yn = _ln(y, lny_g, lny_b)
            q = jnp.einsum('bsc,hcd->bhsd', xn, wq)
            k = jnp.einsum('btc,hcd->bhtd', yn, wk)
            v = jnp.einsum('btc,hcd->bhtd', yn, wv)
            a = jax.nn.softmax(jnp.einsum('bhsd,bhtd->bhst', q, k) * D ** (-0.5), axis=-1)
            if causal:
                s, t = (a.shape[-2], a.shape[-1])
                mask = (jnp.arange(t)[None, :] > jnp.arange(s)[:, None]).astype(a.dtype)
                a = a * mask
            o = jnp.einsum('bhst,bhtd->bhsd', a, v)
            o = o.transpose(0, 2, 1, 3).reshape(x.shape[0], x.shape[1], H * D)
            x_out = x + o @ li1_w + li1_b
            h = jax.nn.gelu(_ln(x_out, ln3_g, ln3_b) @ li2_w + li2_b, approximate=False)
            return x_out + h @ li3_w + li3_b
        x = _ln(xx, ln1_g, ln1_b)
        x = x + _mha(x, x, a1_wq, a1_wk, a1_wv, a1_li1_w, a1_li1_b, a1_lnx_g, a1_lnx_b, a1_lny_g, a1_lny_b, a1_ln3_g, a1_ln3_b, a1_li2_w, a1_li2_b, a1_li3_w, a1_li3_b, causal=True)
        x = _ln(x, ln2_g, ln2_b)
        return x + _mha(x, ee, a2_wq, a2_wk, a2_wv, a2_li1_w, a2_li1_b, a2_lnx_g, a2_lnx_b, a2_lny_g, a2_lny_b, a2_ln3_g, a2_ln3_b, a2_li2_w, a2_li2_b, a2_li3_w, a2_li3_b, causal=False)

    def _L1_ffn_ref(x, r1_w, r1_b, r2_w, w_up, w_down, a_up, a_down):
        import jax, jax.numpy as jnp
        import numpy as np
        E, G, TOPK = (32, 16, 2)
        HID, INTER, A_INTER = (128, 256, 128)
        CAP_FACTOR = 1.25
        SCALE = 0.05

        def _stats(x):
            mean = x.mean(-1, keepdims=True)
            std = jnp.std(x, axis=-1, keepdims=True, ddof=1)
            mn = x.min(-1, keepdims=True)
            mx = x.max(-1, keepdims=True)
            l2 = jnp.linalg.norm(x, axis=-1, keepdims=True)
            sp = (jnp.abs(x) < 1e-06).astype(x.dtype).mean(-1, keepdims=True)
            return jnp.concatenate([mean, std, mn, mx, l2, sp], -1)
        B, N, C = x.shape
        xf = x.reshape(-1, C)
        T = xf.shape[0]
        cap = int(CAP_FACTOR * T / E)
        ri = jnp.concatenate([xf, _stats(xf)], -1)
        h = jax.nn.gelu(ri @ r1_w.T + r1_b, approximate=False)
        probs = jax.nn.softmax(h @ r2_w.T, -1)
        topp, topi = jax.lax.top_k(probs, TOPK)
        wnorm = topp / topp.sum(-1, keepdims=True)
        eids = jnp.arange(E)
        hit = topi[..., None] == eids
        routed = hit.any(1)
        Wc = jnp.where(hit, wnorm[..., None], 0.0).sum(1)
        score = jnp.where(routed, probs, -jnp.inf)
        idx = jnp.argsort(-score, axis=0)[:cap].T
        valid = jnp.take_along_axis(routed.T, idx, 1)
        w = jnp.take_along_axis(Wc.T, idx, 1) * valid
        xe = xf[idx]
        up = jnp.einsum('eci,eji->ecj', xe, w_up)
        gate, upv = jnp.split(up, 2, axis=-1)
        hact = jax.nn.silu(gate) * upv
        ye = jnp.einsum('ecj,eoj->eco', hact, w_down)
        out = jnp.zeros((T, C), xf.dtype).at[idx.reshape(-1)].add((w[..., None] * ye).reshape(-1, C))
        Wmask = jnp.zeros((T, E), xf.dtype).at[idx, eids[:, None]].add(w)
        gw = SCALE * Wmask.reshape(T, G, E // G).sum(-1)
        aup = jnp.einsum('tc,gjc->tgj', xf, a_up)
        ag, av = jnp.split(aup, 2, axis=-1)
        ah = jax.nn.silu(ag) * av
        ay = jnp.einsum('tgj,goj->tgo', ah, a_down)
        out = out + jnp.einsum('tg,tgo->to', gw, ay)
        return out.reshape(B, N, C)
    x = _layernorm(x + _L0_attn_ref(x, L0_attn_W_kv_down, L0_attn_W_k_up, L0_attn_W_v_up, L0_attn_W_q, L0_attn_W_q_rope, L0_attn_W_k_rope, L0_attn_W_o), axis=-1)
    x = _layernorm(x + _L0_xattn_ref(x, ctx_512, L0_xattn_Wk, L0_xattn_bk, L0_xattn_Wq, L0_xattn_bq, L0_xattn_Wv, L0_xattn_bv, L0_xattn_Wck, L0_xattn_bck, L0_xattn_Wcq, L0_xattn_bcq, L0_xattn_Wcv, L0_xattn_bcv, L0_xattn_Wp, L0_xattn_bp), axis=-1)
    x = _layernorm(x + _L0_ffn_ref(x, L0_ffn_ln1_g, L0_ffn_ln1_b, L0_ffn_Wqkv, L0_ffn_Wproj, L0_ffn_ln2_g, L0_ffn_ln2_b, L0_ffn_Wgate, L0_ffn_W1, L0_ffn_b1, L0_ffn_W2, L0_ffn_b2), axis=-1)
    x = _layernorm(x + _L1_attn_ref(x, L1_attn_Wq, L1_attn_Wk, L1_attn_Wv), axis=-1)
    x = _layernorm(x + _L1_xattn_ref(x, ctx_512, L1_xattn_ln1_g, L1_xattn_ln1_b, L1_xattn_ln2_g, L1_xattn_ln2_b, L1_xattn_a1_wq, L1_xattn_a1_wk, L1_xattn_a1_wv, L1_xattn_a1_li1_w, L1_xattn_a1_li1_b, L1_xattn_a1_lnx_g, L1_xattn_a1_lnx_b, L1_xattn_a1_lny_g, L1_xattn_a1_lny_b, L1_xattn_a1_ln3_g, L1_xattn_a1_ln3_b, L1_xattn_a1_li2_w, L1_xattn_a1_li2_b, L1_xattn_a1_li3_w, L1_xattn_a1_li3_b, L1_xattn_a2_wq, L1_xattn_a2_wk, L1_xattn_a2_wv, L1_xattn_a2_li1_w, L1_xattn_a2_li1_b, L1_xattn_a2_lnx_g, L1_xattn_a2_lnx_b, L1_xattn_a2_lny_g, L1_xattn_a2_lny_b, L1_xattn_a2_ln3_g, L1_xattn_a2_ln3_b, L1_xattn_a2_li2_w, L1_xattn_a2_li2_b, L1_xattn_a2_li3_w, L1_xattn_a2_li3_b, 0), axis=-1)
    x = _layernorm(x + _L1_ffn_ref(x, L1_ffn_r1_w, L1_ffn_r1_b, L1_ffn_r2_w, L1_ffn_w_up, L1_ffn_w_down, L1_ffn_a_up, L1_ffn_a_down), axis=-1)
    return x

_drawn_inputs = setup_inputs


def setup_inputs(seed=0):
    import zlib

    import numpy as np

    out = dict(_drawn_inputs(seed))
    spreads = {'L0_xattn_bk': (0.0, 2.0),
     'L0_xattn_bq': (0.0, 0.434),
     'L0_xattn_bv': (0.0, 0.1),
     'L0_xattn_bck': (0.0, 2.0),
     'L0_xattn_bcq': (0.0, 0.336),
     'L0_xattn_bcv': (0.0, 0.1),
     'L0_xattn_bp': (0.0, 0.1),
     'L0_ffn_ln1_g': (1.0, 0.6),
     'L0_ffn_ln1_b': (0.0, 0.8),
     'L0_ffn_ln2_g': (1.0, 0.6),
     'L0_ffn_ln2_b': (0.0, 0.8),
     'L0_ffn_b1': (0.0, 0.8),
     'L0_ffn_b2': (0.0, 0.741),
     'L1_xattn_ln1_g': (1.0, 0.2),
     'L1_xattn_ln1_b': (0.0, 0.1),
     'L1_xattn_ln2_g': (1.0, 0.2),
     'L1_xattn_ln2_b': (0.0, 0.1),
     'L1_xattn_a1_li1_b': (0.0, 0.1),
     'L1_xattn_a1_lnx_g': (1.0, 0.6),
     'L1_xattn_a1_lnx_b': (0.0, 0.8),
     'L1_xattn_a1_lny_g': (1.0, 0.6),
     'L1_xattn_a1_lny_b': (0.0, 0.8),
     'L1_xattn_a1_ln3_g': (1.0, 0.6),
     'L1_xattn_a1_ln3_b': (0.0, 0.8),
     'L1_xattn_a1_li2_b': (0.0, 0.8),
     'L1_xattn_a1_li3_b': (0.0, 0.1),
     'L1_xattn_a2_li1_b': (0.0, 0.1),
     'L1_xattn_a2_lnx_g': (1.0, 0.6),
     'L1_xattn_a2_lnx_b': (0.0, 0.8),
     'L1_xattn_a2_lny_g': (1.0, 0.6),
     'L1_xattn_a2_lny_b': (0.0, 0.8),
     'L1_xattn_a2_ln3_g': (1.0, 0.6),
     'L1_xattn_a2_ln3_b': (0.0, 0.8),
     'L1_xattn_a2_li2_b': (0.0, 0.8),
     'L1_xattn_a2_li3_b': (0.0, 0.1),
     'L1_ffn_r1_b': (0.0, 0.8)}
    factors = {'L0_ffn_Wqkv': 3.046,
     'L0_ffn_Wproj': 3.003,
     'L0_ffn_Wgate': 5.271,
     'L0_ffn_W1': 8.0,
     'L0_ffn_W2': 8.0,
     'L1_xattn_a1_wq': 8.0,
     'L1_xattn_a1_wk': 8.0,
     'L1_xattn_a1_wv': 4.839,
     'L1_xattn_a1_li1_w': 4.799,
     'L1_xattn_a1_li2_w': 3.249,
     'L1_xattn_a1_li3_w': 3.008,
     'L1_xattn_a2_wq': 8.0,
     'L1_xattn_a2_wk': 8.0,
     'L1_xattn_a2_wv': 4.11,
     'L1_xattn_a2_li1_w': 4.152,
     'L1_xattn_a2_li2_w': 3.118,
     'L1_xattn_a2_li3_w': 2.793,
     'L1_ffn_r1_w': 8.0,
     'L1_ffn_r2_w': 8.0,
     'L1_ffn_w_up': 8.0,
     'L1_ffn_w_down': 8.0,
     'L1_ffn_a_up': 28.112,
     'L1_ffn_a_down': 27.519}
    for name, (base, spread) in spreads.items():
        noise = np.random.default_rng([zlib.crc32(name.encode()), seed]).standard_normal(out[name].shape)
        drawn = base * np.exp(spread * noise) if base else spread * noise
        out[name] = jnp.asarray(drawn.astype(out[name].dtype))
    for name, factor in factors.items():
        out[name] = (out[name] * factor).astype(out[name].dtype)
    return out
```

```python
from contextlib import ExitStack

import concourse.bass as bass
from concourse import mybir

ALU = mybir.AluOpType
ACT = mybir.ActivationFunctionType
F32 = mybir.dt.float32
BF16 = mybir.dt.bfloat16
I32 = mybir.dt.int32
U32 = mybir.dt.uint32
AX_X = mybir.AxisListType.X

P = 128
B, T = 8, 256
NT = B * T // P
N = B * T
H = 16
QT_PER_B = T // P
BANK = 512
CH = N // BANK
CTX, CC = 1601, 64
NKT = -(-CTX // P)
CTX_PAD = NKT * P
EPS = 1e-5


class Core:

    def __init__(self, nc, ctx, ins):
        self.nc, self.ctx, self.ins, self.count = nc, ctx, ins, 0
        self.seen = nc.alloc_semaphore("seen")
        self.used = []

    def sem(self, name, by_gpsimd=False):
        self.count += 1
        sem = self.nc.alloc_semaphore(f"{name}_{self.count}")
        if not by_gpsimd:
            self.used.append(sem)
        return sem

    def end_stage(self):
        used, self.used = self.used, []
        with self.nc.Block() as block:
            @block.gpsimd
            def _(pool):
                for sem in used:
                    pool.sem_clear(sem)
        for sem in used:
            self.nc.release_semaphore(sem)

    def sbuf(self, ctx, name, shape, dt=F32):
        self.count += 1
        return ctx.enter_context(self.nc.sbuf_tensor(f"{name}_{self.count}", shape, dt))

    def psum(self, ctx, name, shape, dt=F32):
        self.count += 1
        return ctx.enter_context(self.nc.psum_tensor(f"{name}_{self.count}", shape, dt))


def load_stage(c, ctx, names):
    nc, held = c.nc, {}
    loaded = c.sem("weights_loaded")
    for name in names:
        src = c.ins[name.strip("*")]
        shape = list(src.shape)
        if name.startswith("*"):
            shape[0] = P
        held[name.strip("*")] = c.sbuf(ctx, name.strip("*"), shape, src.dtype)
    with nc.Block() as block:
        @block.sync
        def _(sp):
            for name in names:
                src = c.ins[name.strip("*")]
                if name.startswith("*"):
                    src = src.partition_broadcast(P) if len(src.shape) == 1 else src.to_broadcast([P, src.shape[1]])
                sp.dma_start(held[name.strip("*")][:], src).then_inc(loaded, 16)
            sp.wait_ge(loaded, 16 * len(names))
    return held


def transpose_tiles(c, groups, ident):
    nc = c.nc
    with ExitStack() as ctx:
        turned = c.psum(ctx, "turned", [P, 8, BANK])
        tiles_turned = c.sem("tiles_turned")
        copied = [c.sem("copied_by_scalar"), c.sem("copied_by_vector")]
        block = ctx.enter_context(nc.Block())

        @block.tensor
        def _(pe):
            for g, (srcs, dst, post) in enumerate(groups):
                if g >= 8:
                    pe.wait_ge(copied[g % 2], (g - 8) // 2 + 1)
                for k, src in enumerate(srcs):
                    rows, cols = src.shape
                    last = pe.transpose(turned[0:cols, g % 8, k * P:k * P + rows], src, ident[0:rows, 0:rows])
                last.then_inc(tiles_turned, 1)

        @block.scalar
        def _(act):
            for g, (srcs, dst, post) in enumerate(groups):
                if g % 2 == 0:
                    act.wait_ge(tiles_turned, g + 1)
                    src = turned[0:dst.shape[0], g % 8, 0:dst.shape[1]]
                    if post is None:
                        act.activation(dst, src, ACT.Copy).then_inc(copied[0], 1)
                    else:
                        act.activation(dst, src, ACT.Identity, scale=post[0], bias=post[1]).then_inc(copied[0], 1)

        @block.vector
        def _(dve):
            for g, (srcs, dst, post) in enumerate(groups):
                if g % 2 == 1:
                    dve.wait_ge(tiles_turned, g + 1)
                    src = turned[0:dst.shape[0], g % 8, 0:dst.shape[1]]
                    if post is None:
                        dve.tensor_copy(dst, src).then_inc(copied[1], 1)
                    else:
                        dve.tensor_scalar(dst, src, post[0], post[1], ALU.mult, ALU.add).then_inc(copied[1], 1)


def products(c, jobs):
    nc = c.nc

    def by_scalar(n):
        kind = jobs[n][2][0]
        return kind == "gelu" or (kind != "mul" and n % 2 == 0)

    def place(n):
        mine = by_scalar(n)
        return (0 if mine else 1), sum(by_scalar(m) == mine for m in range(n + 1))

    with ExitStack() as ctx:
        acc = c.psum(ctx, "acc", [P, 8, BANK])
        summed = c.sem("summed")
        taken = [c.sem("taken_by_scalar"), c.sem("taken_by_vector")]
        block = ctx.enter_context(nc.Block())

        @block.tensor
        def _(pe):
            for n, (dst, terms, post) in enumerate(jobs):
                if n >= 8:
                    engine, done = place(n - 8)
                    pe.wait_ge(taken[engine], done)
                rows, cols = terms[0][0].shape[-1], dst.free_size()
                for k, (lhsT, rhs) in enumerate(terms):
                    last = pe.matmul(acc[0:rows, n % 8, 0:cols], lhsT, rhs, start=k == 0, stop=k == len(terms) - 1)
                last.then_inc(summed, 1)

        @block.scalar
        def _(act):
            for n, (dst, terms, post) in enumerate(jobs):
                if by_scalar(n):
                    act.wait_ge(summed, n + 1)
                    src = acc[0:dst.shape[0], n % 8, 0:dst.free_size()]
                    if post[0] == "copy":
                        act.activation(dst, src, ACT.Copy).then_inc(taken[0], 1)
                    else:
                        act.activation(dst, src, ACT.Gelu if post[0] == "gelu" else ACT.Identity,
                                       bias=post[1]).then_inc(taken[0], 1)

        @block.vector
        def _(dve):
            for n, (dst, terms, post) in enumerate(jobs):
                if not by_scalar(n):
                    dve.wait_ge(summed, n + 1)
                    src = acc[0:dst.shape[0], n % 8, 0:dst.free_size()]
                    if post[0] == "copy":
                        dve.tensor_copy(dst, src).then_inc(taken[1], 1)
                    elif post[0] == "bias":
                        dve.tensor_scalar(dst, src, post[1], None, ALU.add).then_inc(taken[1], 1)
                    else:
                        dve.tensor_tensor(dst, src, post[1], ALU.mult).then_inc(taken[1], 1)


def add_pairs(c, pairs):
    with c.nc.Block() as block:
        @block.vector
        def _(dve):
            for dst, other in pairs:
                dve.tensor_tensor(dst, dst, other, ALU.add)


def sum_and_norm(c, tok_terms, summed, norm, residuals, gain=None, shift=None):
    nc = c.nc
    with ExitStack() as ctx:
        acc = c.psum(ctx, "acc", [P, 8, BANK])
        stats = c.sbuf(ctx, "stats", [P, NT, 6])
        moments = c.sbuf(ctx, "moments", [P, NT, 2])
        deviation = c.sbuf(ctx, "deviation", [P, NT])
        rstd = c.sbuf(ctx, "rstd", [P, NT])
        eps = c.sbuf(ctx, "eps", [P, 1])
        tile_product, tile_taken = c.sem("tile_product"), c.sem("tile_taken")
        variances, deviations = c.sem("variances"), c.sem("deviations")
        block = ctx.enter_context(nc.Block())

        @block.tensor
        def _(pe):
            if tok_terms is not None:
                for t in range(NT):
                    if t >= 8:
                        pe.wait_ge(tile_taken, t - 7)
                    terms = tok_terms(t)
                    for k, (lhsT, rhs) in enumerate(terms):
                        last = pe.matmul(acc[:, t % 8, 0:P], lhsT, rhs, start=k == 0, stop=k == len(terms) - 1)
                    last.then_inc(tile_product, 1)

        @block.vector
        def _(dve):
            dve.memset(eps[:], EPS)
            source = residuals[0] if tok_terms is None else summed
            if tok_terms is not None:
                for t in range(NT):
                    dve.wait_ge(tile_product, t + 1)
                    dve.tensor_tensor(summed[:, t, :], acc[:, t % 8, 0:P], residuals[0][:, t, :], ALU.add)\
                       .then_inc(tile_taken, 1)
                for other in residuals[1:]:
                    dve.drain()
                    dve.tensor_tensor(summed[:], summed[:], other[:], ALU.add)
                dve.drain()
            if norm is None:
                return
            for t in range(NT):
                dve.bn_stats(stats[:, t, :], source[:, t, :])
            dve.drain()
            for t in range(NT):
                last = dve.bn_aggr(moments[:, t, :], stats[:, t, :])
            last.then_inc(variances, 1)
            dve.wait_ge(deviations, 1)
            dve.reciprocal(rstd[:], deviation[:])
            dve.drain()
            for t in range(NT):
                dve.tensor_scalar(norm[:, t, :], source[:, t, :], moments[:, t, 0:1], rstd[:, t:t + 1],
                                  ALU.subtract, ALU.mult)
            if gain is not None:
                dve.drain()
                dve.tensor_tensor(norm[:], norm[:], gain[:].unsqueeze(1).to_broadcast([P, NT, P]), ALU.mult)
                dve.drain()
                dve.tensor_tensor(norm[:], norm[:], shift[:].unsqueeze(1).to_broadcast([P, NT, P]), ALU.add)

        @block.scalar
        def _(act):
            if norm is None:
                return
            act.wait_ge(variances, 1)
            act.activation(deviation[:], moments[:, :, 1], ACT.Sqrt, bias=eps[:, 0:1]).then_inc(deviations, 1)


def self_attention(c, QT, KT, V, O, consts, d, heads, kind, scale, masks=None, QR=None, KR=None):
    nc = c.nc
    HQ = min(4, heads)
    quads_per_batch = max(1, heads // 4)
    per_body = max(2, quads_per_batch)
    batches_per_body = per_body // quads_per_batch
    loops = B // batches_per_body
    causal = kind == "causal"
    per_group = P // d if heads > 1 else 1
    n_qm = HQ + (QR is not None)
    w0 = P if causal else T
    width = w0 + T
    blocks = width // P
    layout = [(0, 0, 0), (1, 0, 1), (2, 1, 1)] if causal else [(0, 0, 0), (1, 1, 0), (2, 0, 1), (3, 1, 1)]
    with ExitStack() as ctx:
        S = c.psum(ctx, "scores", [P, HQ if HQ > 1 else 1, BANK])
        PTp = c.psum(ctx, "probs_turned", [P, 2, BANK])
        Op = c.psum(ctx, "weighted", [P, 2, BANK])
        Qm = c.sbuf(ctx, "one_heads_queries", [P, 2, n_qm, T])
        Pr = c.sbuf(ctx, "probs", [P, 2, HQ, width])
        PT = c.sbuf(ctx, "probsT", [P, 2, width])
        PTm = c.sbuf(ctx, "masked_probsT", [P, 2, 2, P]) if not causal else None
        mx = c.sbuf(ctx, "row_max", [P, HQ, 2])
        rec = c.sbuf(ctx, "sum_reciprocal", [P, 2, HQ])
        queries_ready = c.sem("queries_ready")
        scores_ready = c.sem("scores_ready")
        shifted_ready = c.sem("shifted_ready")
        probs_ready = c.sem("probs_ready")
        turned_ready = c.sem("turned_ready")
        copied = c.sem("probsT_copied")
        masked = c.sem("probsT_masked")
        weighted_ready = c.sem("weighted_ready")
        normed = c.sem("normed")
        block = ctx.enter_context(nc.Block())

        def quad_place(it, i):
            return (it * batches_per_body + i // quads_per_batch, (i % quads_per_batch) * 4)

        def over_bodies(eng, body):
            with eng.Fori(0, loops - 1, 1) as it:
                body(it, False)
            body(loops - 1, True)

        @block.gpsimd
        def _(pool):
            def queries(it, i):
                q = it * per_body + i
                b, h0 = quad_place(it, i)
                pool.wait_ge(scores_ready, q + 1)
                pool.sem_inc(c.seen, 1)
                for j in range(HQ):
                    g, m = (h0 + j) // per_group, (h0 + j) % per_group
                    src = QT[:, g, bass.ds(b * T, T)]
                    if masks is None:
                        op = pool.tensor_copy(Qm[:, i % 2, j, :], src)
                    else:
                        op = pool.tensor_tensor(Qm[:, i % 2, j, :], src, masks[:, m:m + 1].to_broadcast([P, T]),
                                                ALU.mult)
                if QR is not None:
                    op = pool.tensor_copy(Qm[:, i % 2, HQ, :], QR[:, bass.ds(b * T, T)])
                op.then_inc(queries_ready, 1)

            def body(it, last):
                for i in range(per_body):
                    if not (last and i == per_body - 1):
                        queries(*((it, i + 1) if i + 1 < per_body else (it + 1, 0)))
                    if not causal:
                        mask_probs(it, i)

            def mask_probs(it, i):
                for h in range(HQ):
                    n = (it * per_body + i) * HQ + h
                    pool.wait_ge(copied, n + 3)
                    pool.wait_ge(weighted_ready, n - 1 + 2 * HQ)
                    pool.tensor_tensor(PTm[:, h % 2, 0, :], PT[:, h % 2, 0:P], consts["future_mask"][:], ALU.mult)
                    pool.tensor_tensor(PTm[:, h % 2, 1, :], PT[:, h % 2, 3 * P:4 * P], consts["future_mask"][:],
                                       ALU.mult).then_inc(masked, 1)

            queries(0, 0)
            over_bodies(pool, body)

        @block.tensor
        def _(pe):
            def scores(it, i):
                q = it * per_body + i
                b, h0 = quad_place(it, i)
                pe.wait_ge(queries_ready, q + 1)
                pe.wait_ge(shifted_ready, q + 1)
                for j in range(HQ):
                    g = (h0 + j) // per_group
                    for qt in range(2):
                        cols = slice(0, w0) if qt == 0 else slice(w0, width)
                        keys = w0 if qt == 0 else T
                        out = S[:, j, cols]
                        rest = causal or QR is not None
                        op = pe.matmul(out, Qm[:, i % 2, j, qt * P:qt * P + P], KT[:, g, bass.ds(b * T, keys)],
                                       start=True, stop=not rest)
                        if QR is not None:
                            op = pe.matmul(out, Qm[:, i % 2, HQ, qt * P:qt * P + P], KR[:, bass.ds(b * T, keys)],
                                           start=False, stop=not causal)
                        if causal:
                            op = pe.matmul(out, consts["identb"][:], consts["causal_bias"][:, T - keys:T],
                                           start=False, stop=True)
                op.then_inc(scores_ready, 1)

            def turn(it, i, h):
                q = it * per_body + i
                n = q * HQ + h
                if h == 0:
                    pe.wait_ge(probs_ready, q + 1)
                pe.wait_ge(copied, n + 1)
                slot = n_slot(i, h)
                for k in range(blocks):
                    op = pe.transpose(PTp[:, slot, k * P:k * P + P], Pr[:, i % 2, h, k * P:k * P + P],
                                      consts["ident"][:])
                op.then_inc(turned_ready, 1)

            def weigh(it, i, h):
                q = it * per_body + i
                n = q * HQ + h
                b, h0 = quad_place(it, i)
                pe.wait_ge(copied, n + 3)
                if h == 0:
                    pe.wait_ge(normed, q + 1)
                if not causal:
                    pe.wait_ge(masked, n + 1)
                slot = n_slot(i, h)
                for qt in range(2):
                    at = (qt * HQ + h) * (d + 1)
                    mine = [(k, kt) for k, kt, q_of in layout if q_of == qt]
                    if causal:
                        for n_, (k, kt) in enumerate(mine):
                            op = pe.matmul(Op[:, i % 2, at:at + d + 1], PT[:, slot, k * P:k * P + P],
                                           value(b, kt, h0 + h, 0, d + 1), start=n_ == 0, stop=n_ == len(mine) - 1)
                        continue
                    later = [(PTm[:, slot, 0, :], 0), (PT[:, slot, P:2 * P], 1)] if qt == 0 else \
                        [(PTm[:, slot, 1, :], 1)]
                    for n_, (lhsT, kt) in enumerate(later):
                        pe.matmul(Op[:, i % 2, at:at + d], lhsT, value(b, kt, h0 + h, 0, d),
                                  start=n_ == 0, stop=n_ == len(later) - 1)
                    for n_, (k, kt) in enumerate(mine):
                        op = pe.matmul(Op[:, i % 2, at + d:at + d + 1], PT[:, slot, k * P:k * P + P],
                                       value(b, kt, h0 + h, d, d + 1), start=n_ == 0, stop=n_ == len(mine) - 1)
                op.then_inc(weighted_ready, 1)

            def value(b, kt, h, lo, hi):
                return V[:, bass.ds(b * QT_PER_B + kt, 1), h * (d + 1) + lo:h * (d + 1) + hi]

            def n_slot(i, h):
                return (i * HQ + h) % 2

            def body(it, last):
                for i in range(per_body):
                    if not (last and i == per_body - 1):
                        nxt = (it, i + 1) if i + 1 < per_body else (it + 1, 0)
                        scores(*nxt)
                    turn(it, i, 0)
                    for h in range(1, HQ):
                        turn(it, i, h)
                        weigh(it, i, h - 1)
                    weigh(it, i, HQ - 1)

            pe.sem_inc(scores_ready, 2)
            pe.sem_inc(weighted_ready, 2 * HQ)
            scores(0, 0)
            over_bodies(pe, body)

        @block.vector
        def _(dve):
            def shift(it, i):
                q = it * per_body + i
                dve.drain()
                dve.wait_ge(weighted_ready, HQ * (q + 1))
                dve.wait_ge(scores_ready, q + 3)
                if causal:
                    dve.tensor_reduce(mx[:, :, 0], S[:, 0:HQ, 0:P], AX_X, ALU.max)
                    dve.tensor_reduce(mx[:, :, 1], S[:, 0:HQ, P:3 * P], AX_X, ALU.max)
                    dve.drain()
                    dve.tensor_tensor(Pr[:, i % 2, :, 0:P], S[:, 0:HQ, 0:P],
                                      mx[:, :, 0:1].to_broadcast([P, HQ, P]), ALU.subtract)
                    op = dve.tensor_tensor(Pr[:, i % 2, :, P:3 * P], S[:, 0:HQ, P:3 * P],
                                           mx[:, :, 1:2].to_broadcast([P, HQ, T]), ALU.subtract)
                else:
                    src = S[:, 0:HQ, :].rearrange("p h (q k) -> p h q k", q=2)
                    dve.tensor_reduce(mx[:, :, :], src, AX_X, ALU.max)
                    dve.drain()
                    op = dve.tensor_tensor(Pr[:, i % 2, :, :].rearrange("p h (q k) -> p h q k", q=2), src,
                                           mx[:, :, :].unsqueeze(3).to_broadcast([P, HQ, 2, T]), ALU.subtract)
                op.then_inc(shifted_ready, 1)

            def norm(it, i):
                q = it * per_body + i
                b, h0 = quad_place(it, i)
                out = Op[:, i % 2, 0:2 * HQ * (d + 1)].rearrange("p (q h e) -> p q h e", q=2, h=HQ)
                dve.drain()
                dve.wait_ge(weighted_ready, HQ * (q + 1) + 2 * HQ)
                dve.reciprocal(rec[:], out[:, :, :, d])
                dve.drain()
                for qt in range(2):
                    dst = O[:, bass.ds(b * QT_PER_B + qt, 1), h0 * d:(h0 + HQ) * d]
                    op = dve.tensor_tensor(dst.rearrange("p o (h e) -> p (o h) e", h=HQ), out[:, qt, :, 0:d],
                                           rec[:, qt, :].unsqueeze(2).to_broadcast([P, HQ, d]), ALU.mult)
                op.then_inc(normed, 1)

            def body(it, last):
                for i in range(per_body):
                    if not (last and i == per_body - 1):
                        shift(*((it, i + 1) if i + 1 < per_body else (it + 1, 0)))
                    norm(it, i)

            dve.sem_inc(shifted_ready, 1)
            dve.sem_inc(normed, 2)
            shift(0, 0)
            over_bodies(dve, body)

        @block.scalar
        def _(act):
            def body(it, last):
                for i in range(per_body):
                    q = it * per_body + i
                    act.wait_ge(shifted_ready, q + 2)
                    act.activation(Pr[:, i % 2, :, :], Pr[:, i % 2, :, :], ACT.Exp, scale=scale)\
                       .then_inc(probs_ready, 1)
                    for h in range(HQ):
                        n = q * HQ + h
                        slot = (i * HQ + h) % 2
                        act.wait_ge(turned_ready, n + 1)
                        act.wait_ge(weighted_ready, n - 1 + 2 * HQ)
                        act.activation(PT[:, slot, :], PTp[:, slot, 0:width], ACT.Copy).then_inc(copied, 1)

            act.sem_inc(copied, 2)
            over_bodies(act, body)


LEVELS = 3


def product_terms(d):
    parts = [(0, 0), (0, 1), (1, 0), (1, 1), (0, 2), (2, 0)]
    per_pack = 96 // d
    return [(t // per_pack, t % per_pack * d, *parts[t]) for t in range(len(parts))]


def split_queries(c, QT, groups, parts):
    nc = c.nc
    with ExitStack() as ctx:
        level = c.sbuf(ctx, "levels", [P, 2, LEVELS, N], BF16)
        rest = c.sbuf(ctx, "rests", [P, 2, N])
        high, middle, low = c.sem("high_ready"), c.sem("middle_ready"), c.sem("low_ready")
        rest_ready = c.sem("rest_ready")
        stored = [c.sem("parts_stored0"), c.sem("parts_stored1")]
        block = ctx.enter_context(nc.Block())

        @block.scalar
        def _(act):
            for g in range(groups):
                if g >= 2:
                    act.wait_ge(stored[g % 2], g // 2 * 16 * LEVELS)
                act.activation(level[:, g % 2, 0, :], QT[:, g, :], ACT.Copy).then_inc(high, 1)
                act.wait_ge(rest_ready, g + 1)
                act.activation(level[:, g % 2, 1, :], rest[:, g % 2, :], ACT.Copy).then_inc(middle, 1)

        @block.vector
        def _(dve):
            for g in range(groups):
                dve.drain()
                dve.wait_ge(high, g + 1)
                dve.tensor_tensor(rest[:, g % 2, :], QT[:, g, :], level[:, g % 2, 0, :], ALU.subtract)\
                   .then_inc(rest_ready, 1)
                dve.drain()
                dve.wait_ge(middle, g + 1)
                dve.tensor_tensor(level[:, g % 2, 2, :], rest[:, g % 2, :], level[:, g % 2, 1, :], ALU.subtract)\
                   .then_inc(low, 1)

        @block.sync
        def _(sp):
            for g in range(groups):
                for l, ready in enumerate((high, middle, low)):
                    sp.wait_ge(ready, g + 1)
                    sp.dma_start(parts[l, g * P:g * P + P, :], level[:, g % 2, l, :]).then_inc(stored[g % 2], 16)
            for s in range(2):
                uses = len(range(s, groups, 2))
                if uses:
                    sp.wait_ge(stored[s], uses * 16 * LEVELS)


def cross_attention(c, query_parts, O, wk, wv, ctx_src, consts, d, add_to, scale):
    nc = c.nc
    PG = P // d
    GB = H // PG
    BPB = 2 if GB == 1 else 1
    HB, GBODY, LOOPS = H * BPB, GB * BPB, B // BPB
    HEADS, GROUPS = B * H, B * GB
    VW = PG * (d + 1)
    SLOTS = 4
    terms = product_terms(d)
    NP = terms[-1][0] + 1
    ROWS, SHIFT = 96, 96
    AHEAD_K = 1 if GB == 1 else 2
    units = [(k, min(2, NKT - k)) for k in range(0, NKT, 2)]
    NU = len(units)
    kcw = CTX_PAD // 4
    mcw = -(-CTX // 4)
    chunks = [(k, min(mcw, CTX - k)) for k in range(0, CTX, mcw)]
    NC = len(chunks)
    max_of_unit = [range(u, u + 1) for u in range(NU - 1)] + [range(NU - 1, 2 * NC)]
    weigh_of_unit = [range(-(-NKT * u // (NU - 1)), -(-NKT * (u + 1) // (NU - 1))) for u in range(NU - 1)] + [range(0)]

    side = {}
    for s in range(HB):
        side[s, 1] = ("shift", None, None)
    for j in range(GBODY):
        if GB == 1:
            places = [(j * H + 2, u) for u in (2, 3, 4, 5)]
            places += [(j * H + 6 + k // 4, 2 + k % 4) for k in range(NKT)]
        else:
            places = [(j * PG + s, u) for s in range(3) for u in (0, 2, 3, 4, 5, 6)]
        jobs = [("key", j + AHEAD_K, k) for k in range(4)] + [("value", j + 1, k) for k in range(NKT)]
        for at, job in zip(places, jobs):
            side[at] = job
    context_steps = (0, 6) if GB == 1 else (6, 11)

    def body_jobs(last):
        left = {}
        for (s, u), (kind, g, k) in sorted(side.items()):
            if last and (kind == "shift" and s + 2 >= HB or kind != "shift" and g >= GBODY):
                continue
            left[s, u] = (len(left), kind, g, k)
        return left

    JB = len(body_jobs(False))
    first_jobs = [("key", g, k) for g in range(AHEAD_K) for k in range(4)] + [("value", 0, k) for k in range(NKT)] \
        + [("shift", None, None)] * 2
    J0 = len(first_jobs)

    def over_bodies(eng, body):
        with eng.Fori(0, LOOPS - 1, 1) as it:
            body(it, False)
        body(LOOPS - 1, True)

    with ExitStack() as ctx:
        ST = c.psum(ctx, "scoresT", [P, 3, BANK])
        SM = c.psum(ctx, "scores_for_max", [P, 2, BANK])
        Side = c.psum(ctx, "side", [P, BANK])
        Op = c.psum(ctx, "weighted", [P, 2, BANK])
        ctxK = c.sbuf(ctx, "context_for_keys", [P, CTX_PAD])
        ctxV = c.sbuf(ctx, "context_for_values", [P, CTX_PAD])
        level = c.sbuf(ctx, "key_parts", [P, 2, LEVELS, CTX_PAD], BF16)
        rest = c.sbuf(ctx, "key_rests", [P, CTX_PAD])
        KP = c.sbuf(ctx, "key_packs", [P, SLOTS, NP, CTX_PAD], BF16)
        QP = c.sbuf(ctx, "query_packs", [P, 8, NP, T], BF16)
        V = c.sbuf(ctx, "values", [P, 2, NKT, VW])
        PT = c.sbuf(ctx, "probsT", [P, 2, NKT, T])
        chunk_max = c.sbuf(ctx, "chunk_max", [P, 2, NC])
        neg_max = c.sbuf(ctx, "neg_max", [P, 2])
        high_max = c.sbuf(ctx, "neg_max_high", [P, 2], BF16)
        low_max = c.sbuf(ctx, "neg_max_rest", [P, 2])
        diag = c.sbuf(ctx, "neg_max_diagonals", [P, 2, 2, P], BF16)
        OT = c.sbuf(ctx, "weightedT", [P, T])
        rec = c.sbuf(ctx, "sum_reciprocal", [P, 2])
        pad_ready = c.sem("pad_ready")
        context_for_keys = c.sem("context_for_keys_loaded")
        context_for_values = c.sem("context_for_values_loaded")
        key_packs = [c.sem(f"key_pack_loaded{s}") for s in range(SLOTS)]
        query_packs = [c.sem("query_packs_loaded0"), c.sem("query_packs_loaded1")]
        side_product = c.sem("side_product")
        side_taken = c.sem("side_taken")
        high_ready = c.sem("keys_high_ready")
        chunk_split = c.sem("keys_chunk_split")
        max_scores = c.sem("max_scores")
        chunk_reduced = c.sem("chunk_reduced")
        diagonal_ready = c.sem("diagonal_ready")
        unit_scored = c.sem("unit_scored")
        unit_exp = c.sem("unit_exp")
        weighted = c.sem("weighted")
        weighted_copied, turned = c.sem("weighted_copied"), c.sem("turned")
        normed = c.sem("normed")
        block = ctx.enter_context(nc.Block())

        @block.gpsimd
        def _(pool):
            for buffer in (QP[:], ctxK[CC:P, :], ctxV[CC:P, :], ctxK[0:CC, CTX:CTX_PAD], ctxV[0:CC, CTX:CTX_PAD]):
                pool.memset(buffer, 0.0)
                pool.drain()
            pool.memset(ctxK[CC:CC + 1, 0:CTX], 1.0)
            pool.drain()
            pool.memset(ctxV[CC:CC + 1, 0:CTX], 1.0).then_inc(pad_ready, 1)

            def split(number, slot, k):
                cols = slice(k * kcw, (k + 1) * kcw)
                pool.wait_ge(side_taken, number + 2)
                pool.sem_inc(c.seen, 1)
                pool.tensor_copy(level[:, slot, 1, cols], rest[:, cols])
                pool.drain()
                pool.tensor_tensor(level[:, slot, 2, cols], rest[:, cols], level[:, slot, 1, cols], ALU.subtract)\
                    .then_inc(chunk_split, 1)
                pool.drain()

            for number, (kind, g, k) in enumerate(first_jobs):
                if kind == "key":
                    split(number, g % 2, k)

            def body(it, last):
                for number, kind, g, k in body_jobs(last).values():
                    if kind == "key":
                        split(J0 + it * JB + number, g % 2, k)

            over_bodies(pool, body)

        @block.sync
        def _(sp):
            def load_context(buffer, loaded, b):
                sp.dma_start(buffer[0:CC, 0:CTX], ctx_src(b)).then_inc(loaded, 16)

            def load_head(it, i):
                b, h = it * BPB + i // H, i % H
                if i % 4 == 0:
                    for pack, row, _, l in terms:
                        rows = query_parts[l, h * d:(h + 4) * d, bass.ds(b * T, T)].rearrange("(h f) n -> f h n", h=4)
                        sp.dma_start(QP[row:row + d, i % 8:i % 8 + 4, pack, :], rows)\
                          .then_inc(query_packs[i // 4 % 2], 16)
                sp.wait_ge(chunk_split, (it * GBODY + i // PG + 1) * 4)
                at = h % PG * d
                for pack, row, l, _ in terms:
                    sp.dma_start(KP[row:row + d, i % SLOTS, pack, :], level[at:at + d, i // PG % 2, l, :])\
                      .then_inc(key_packs[i % SLOTS], 16)

            sp.wait_ge(pad_ready, 2)
            load_context(ctxK, context_for_keys, 0)
            load_context(ctxV, context_for_values, 0)
            for i in range(SLOTS):
                load_head(0, i)

            def body(it, last):
                for i in range(HB):
                    sp.wait_ge(unit_scored, (it * HB + i + 1) * NU)
                    sp.sem_inc(c.seen, 1)
                    b, s = it * BPB + i // H, i % H
                    next_batch = not (last and i // H == BPB - 1)
                    jobs_before = sum(step < i for step, _ in body_jobs(last))
                    if s == context_steps[0] and next_batch:
                        sp.wait_ge(side_product, J0 + it * JB + jobs_before)
                        load_context(ctxK, context_for_keys, b + 1)
                    if s == context_steps[1] and next_batch:
                        sp.wait_ge(side_product, J0 + it * JB + jobs_before)
                        load_context(ctxV, context_for_values, b + 1)
                    m = i + SLOTS
                    if m < HB:
                        load_head(it, m)
                    elif not last:
                        load_head(it + 1, m - HB)

            over_bodies(sp, body)

        @block.tensor
        def _(pe):
            def side_job(number, head, kind, g, k, b):
                if kind == "shift":
                    pe.wait_ge(diagonal_ready, head + 1)
                pe.wait_ge(side_taken, number + 1)
                if kind == "shift":
                    for part in range(2):
                        op = pe.matmul(Side[:, 0:T], consts["row_pickers"][:, part * P:part * P + P],
                                       diag[:, part, :, :].rearrange("p q k -> p (q k)"), start=part == 0, stop=part == 1)
                    op.then_inc(side_product, 1)
                    return
                gi = g % GB
                if kind == "key":
                    if gi == 0 and k == 0:
                        pe.wait_ge(context_for_keys, (b + 1) * 16)
                    pe.matmul(Side[:, 0:kcw], wk[0:CC + 1, gi * P:gi * P + P], ctxK[0:CC + 1, k * kcw:(k + 1) * kcw],
                              start=True, stop=True).then_inc(side_product, 1)
                else:
                    if gi == 0 and k == 0:
                        pe.wait_ge(context_for_values, (b + 1) * 16)
                    pe.matmul(Side[:, 0:VW], ctxV[0:CC + 1, k * P:k * P + P], wv[0:CC + 1, gi * VW:gi * VW + VW],
                              start=True, stop=True).then_inc(side_product, 1)

            def max_part(n, i, n_body, j):
                qt, k = j // NC, j % NC
                if j == 0:
                    pe.wait_ge(key_packs[i % SLOTS], (n_body * (HB // SLOTS) + i // SLOTS + 1) * (16 * len(terms)))
                    if i % 4 == 0:
                        pe.wait_ge(query_packs[i // 4 % 2], (n_body * (HB // 8) + i // 8 + 1) * (16 * len(terms)))
                pe.wait_ge(chunk_reduced, n * 2 * NC + j + 1)
                at, size = chunks[k]
                pe.matmul(SM[:, j % 2, 0:size], QP[0:ROWS, i % 8, 0, qt * P:qt * P + P], KP[0:ROWS, i % SLOTS, 0, at:at + size],
                          start=True, stop=True).then_inc(max_scores, 1)

            def unit(n, i, u, shift_number):
                if u == 0:
                    pe.wait_ge(side_taken, shift_number + 2)
                before = n * NU + u - 3 if u >= 3 else n * NU - NU + (5, 6, 4)[u] if i % 2 == 0 else n * NU - NU + 4 + u
                pe.wait_ge(unit_exp, before + NU + 1)
                kt0, size = units[u]
                bank = (u + i % 2) % 3
                for k in range(size):
                    for pack in range(NP):
                        rows = P if pack == 0 else ROWS
                        op = pe.matmul(ST[:, bank, k * T:k * T + T], KP[0:rows, i % SLOTS, pack, (kt0 + k) * P:(kt0 + k + 1) * P],
                                       QP[0:rows, i % 8, pack, :], start=pack == 0, stop=pack == NP - 1)
                op.then_inc(unit_scored, 1)

            def weigh(n, i, tiles):
                for kt in tiles:
                    if kt == 0:
                        pe.wait_ge(normed, n + 1)
                    if kt % 2 == 0:
                        pe.wait_ge(unit_exp, n * NU + kt // 2 + 1 + NU)
                    op = pe.matmul(Op[0:d + 1, i % 2, 0:T], V[:, i // PG % 2, kt, i % PG * (d + 1):(i % PG + 1) * (d + 1)],
                                   PT[:, i % 2, kt, :], start=kt == 0, stop=kt == NKT - 1)
                    if kt == NKT - 1:
                        op.then_inc(weighted, 1)

            def turn(n, i):
                pe.wait_ge(weighted_copied, n + 1)
                pe.sem_inc(c.seen, 1)
                for qt in range(2):
                    at = T + qt * (d + 1)
                    op = pe.transpose(Op[:, i % 2, at:at + d + 1], OT[0:d + 1, qt * P:qt * P + P],
                                      consts["ident"][0:d + 1, 0:d + 1])
                op.then_inc(turned, 1)

            pe.sem_inc(weighted, 2)
            pe.wait_ge(pad_ready, 2)
            for number, (kind, g, k) in enumerate(first_jobs[:-2]):
                side_job(number, None, kind, g, k, 0)
            for head in range(2):
                for j in range(2 * NC):
                    max_part(head, head, 0, j)
                side_job(J0 - 2 + head, head, "shift", None, None, None)
            for u in range(NU):
                unit(0, 0, u, J0 - 2)
            for j in range(2 * NC):
                max_part(2, 2, 0, j)

            def body(it, last):
                jobs = body_jobs(last)
                base = J0 + it * JB
                for i in range(HB):
                    n = it * HB + i
                    for u in range(NU):
                        if not (last and i + 1 >= HB):
                            number = base + jobs[i - 1, 1][0] if i else base - 1
                            unit(n + 1, (i + 1) % HB, u, number)
                        for j in max_of_unit[u]:
                            if i + 3 < HB:
                                max_part(n + 3, i + 3, it, j)
                            elif not last:
                                max_part(n + 3, i + 3 - HB, it + 1, j)
                        if (i, u) in jobs:
                            number, kind, g, k = jobs[i, u]
                            b = None if kind == "shift" else it * BPB + g // GB
                            side_job(base + number, n + 2, kind, g, k, b)
                        weigh(n, i, weigh_of_unit[u])
                    turn(n, i)

            over_bodies(pe, body)

        @block.scalar
        def _(act):
            def exp(n, i, u):
                kt0, size = units[u]
                if u == 0:
                    act.wait_ge(weighted, n + 1)
                act.wait_ge(unit_scored, n * NU + u + 1)
                act.activation(PT[:, i % 2, kt0:kt0 + size, :].rearrange("p k q -> p (k q)"),
                               ST[:, (u + i % 2) % 3, 0:size * T], ACT.Exp, scale=scale).then_inc(unit_exp, 1)

            def side_job(number, i, kind, g, k):
                act.wait_ge(side_product, number + 1)
                if kind == "shift":
                    act.activation(QP[SHIFT:SHIFT + 2, i % 8, 0, :], Side[SHIFT:SHIFT + 2, 0:T], ACT.Copy)\
                       .then_inc(side_taken, 1)
                elif kind == "key":
                    act.activation(level[:, g % 2, 0, k * kcw:(k + 1) * kcw], Side[:, 0:kcw], ACT.Copy)\
                       .then_inc(high_ready, 1)
                else:
                    act.activation(V[:, g % 2, k, :], Side[:, 0:VW], ACT.Copy).then_inc(side_taken, 1)

            act.sem_inc(side_taken, 1)
            act.sem_inc(unit_exp, NU)
            for number, (kind, g, k) in enumerate(first_jobs[:-2]):
                side_job(number, None, kind, g, k)
            for head in range(2):
                side_job(J0 - 2 + head, head, "shift", None, None)
            for u in range(NU):
                exp(0, 0, u)

            def body(it, last):
                jobs = body_jobs(last)
                for i in range(HB):
                    for u in range(NU):
                        if u == NU - 1:
                            act.wait_ge(weighted, it * HB + i + 3)
                            act.activation(OT[0:d + 1, :], Op[0:d + 1, i % 2, 0:T], ACT.Copy).then_inc(weighted_copied, 1)
                        if not (last and i + 1 >= HB):
                            exp(it * HB + i + 1, (i + 1) % HB, u)
                        if (i, u) in jobs:
                            number, kind, g, k = jobs[i, u]
                            side_job(J0 + it * JB + number, i + 2, kind, g, k)

            over_bodies(act, body)

        @block.vector
        def _(dve):
            def reduce_part(n, j):
                dve.wait_ge(max_scores, n * 2 * NC + j + 1)
                dve.tensor_reduce(chunk_max[:, j // NC, j % NC:j % NC + 1], SM[:, j % 2, 0:chunks[j % NC][1]],
                                  AX_X, ALU.max).then_inc(chunk_reduced, 1)

            def diagonals(n, job):
                dve.drain()
                dve.tensor_reduce(neg_max[:], chunk_max[:], AX_X, ALU.max, negate=True)
                dve.drain()
                dve.tensor_copy(high_max[:], neg_max[:])
                dve.drain()
                dve.tensor_tensor(low_max[:], neg_max[:], high_max[:], ALU.subtract)
                dve.drain()
                if not (isinstance(n, int) and n == 0):
                    dve.wait_ge(side_product, job + 1)
                for part, value in enumerate((neg_max, low_max)):
                    op = dve.tensor_tensor(diag[:, part, :, :], consts["ident"][:].unsqueeze(1).to_broadcast([P, 2, P]),
                                           value[:].unsqueeze(2).to_broadcast([P, 2, P]), ALU.mult)
                op.then_inc(diagonal_ready, 1)
                dve.drain()

            def key_rest(count, g, k):
                cols = slice(k * kcw, (k + 1) * kcw)
                if isinstance(count, int) and count < 4:
                    pass
                else:
                    dve.wait_ge(chunk_split, count - 3)
                dve.wait_ge(high_ready, count + 1)
                dve.tensor_tensor(rest[:, cols], Side[:, 0:kcw], level[:, g % 2, 0, cols], ALU.subtract)\
                   .then_inc(side_taken, 1)

            def norm(it, i):
                b, h = it * BPB + i // H, i % H
                dve.drain()
                dve.wait_ge(turned, it * HB + i + 1)
                out = Op[:, i % 2, T:T + 2 * (d + 1)].rearrange("p (q e) -> p q e", q=2)
                dve.reciprocal(rec[:], out[:, :, d])
                dve.drain()
                for qt in range(2):
                    dst = O[:, bass.ds(b * QT_PER_B + qt, 1), h * d:h * d + d]
                    if add_to:
                        op = dve.scalar_tensor_tensor(out=dst, in0=out[:, qt:qt + 1, 0:d], scalar=rec[:, qt:qt + 1],
                                                      in1=dst, op0=ALU.mult, op1=ALU.add)
                    else:
                        op = dve.tensor_scalar(dst, out[:, qt:qt + 1, 0:d], rec[:, qt:qt + 1], None, ALU.mult)
                op.then_inc(normed, 1)

            dve.memset(KP[:], 0.0)
            dve.drain()
            dve.memset(KP[SHIFT:SHIFT + 2, :, 0, 0:CTX], 1.0).then_inc(pad_ready, 1)
            dve.sem_inc(chunk_reduced, 2)
            dve.sem_inc(normed, 2)
            for number, (kind, g, k) in enumerate(first_jobs):
                if kind == "key":
                    key_rest(number, g, k)
            for head in range(3):
                for j in range(2 * NC):
                    reduce_part(head, j)
                diagonals(head, J0 - 3 + head)

            def body(it, last):
                jobs = body_jobs(last)
                chunks_split = 4 * AHEAD_K + it * (4 * GBODY)
                for i in range(HB):
                    more = not (last and i + 3 >= HB)
                    for u in range(NU):
                        if more:
                            for j in max_of_unit[u]:
                                reduce_part(it * HB + i + 3, j)
                        if (i, u) in jobs and jobs[i, u][1] == "key":
                            _, _, g, k = jobs[i, u]
                            key_rest(chunks_split + 4 * (g - AHEAD_K) + k, g, k)
                    if more:
                        diagonals(it * HB + i + 3, J0 + it * JB + jobs[i, 1][0])
                    norm(it, i)

            over_bodies(dve, body)


def tok(a, t):
    return a[:, t * P:(t + 1) * P]


def chunk(a, k):
    return a[:, k * BANK:(k + 1) * BANK]


def turn_tokens(c, dst, src, ident, post=None):
    transpose_tiles(c, [([src[:, 4 * g + k, :] for k in range(4)], chunk(dst, g), post) for g in range(CH)], ident)


def project(dst, w, xT, post=("copy",)):
    return [(chunk(dst, k), [(w, chunk(xT, k))], post) for k in range(CH)]


def value_jobs(V, w, row, ones, xT):
    n = w.shape[1]
    parts = -(-n // BANK)
    s = n // parts
    return [(V[:, t, k * s:k * s + s], [(tok(xT, t), w[:, k * s:k * s + s]), (ones[0:1, 0:P], row[0:1, k * s:k * s + s])],
             ("copy",)) for t in range(NT) for k in range(parts)]


def stage_mla(c, x, K):
    with ExitStack() as ctx:
        W = load_stage(c, ctx, ["A_kvd", "A_ku", "A_q", "A_qr", "A_qrs", "A_kr", "A_krs", "A_vu", "A_vrow", "A_wo",
                                "A_cos", "A_sin", "mask8"])
        O = c.sbuf(ctx, "O", [P, NT, P])
        QT, KT = c.sbuf(ctx, "QT", [P, 1, N]), c.sbuf(ctx, "KT", [P, 1, N])
        with ExitStack() as inner:
            xT, ckvT = c.sbuf(inner, "xT", [P, N]), c.sbuf(inner, "ckvT", [P, N])
            QR, KR = c.sbuf(inner, "QR", [P, N]), c.sbuf(inner, "KR", [P, N])
            QRs, KRs = c.sbuf(inner, "QRs", [P, N]), c.sbuf(inner, "KRs", [P, N])
            V = c.sbuf(inner, "V", [P, NT, H * 9])
            turn_tokens(c, xT, x, K["ident"])
            cos, sin = ("mul", W["A_cos"][:]), ("mul", W["A_sin"][:])
            products(c, project(ckvT, W["A_kvd"][:], xT) + project(QT[:, 0, :], W["A_q"][:], xT)
                     + project(QR, W["A_qr"][:], xT, cos) + project(QRs, W["A_qrs"][:], xT, sin))
            products(c, project(KT[:, 0, :], W["A_ku"][:], ckvT) + project(KR, W["A_kr"][:], ckvT, cos)
                     + project(KRs, W["A_krs"][:], ckvT, sin) + value_jobs(V, W["A_vu"], W["A_vrow"], K["ones"], ckvT))
            add_pairs(c, [(QR[:], QRs[:]), (KR[:], KRs[:])])
            self_attention(c, QT, KT, V, O, K, 8, H, "causal", 40 ** -0.5, W["mask8"], QR, KR)
        OT = QT
        turn_tokens(c, OT[:, 0, :], O, K["ident"])
        summed = c.sbuf(ctx, "summed", [P, NT, P])
        sum_and_norm(c, lambda t: [(tok(OT[:, 0, :], t), W["A_wo"][:])], summed, x, [x])


def context_from_dram(src):
    return lambda b: src[bass.ds(b, 1), :, :].rearrange("o c k -> (o c) k")


def stage_self_and_cross(c, x, K):
    with ExitStack() as ctx:
        W = load_stage(c, ctx, ["B_q", "B_k", "B_cq", "B_bq", "B_bk", "B_bcq", "B_v", "B_vrow", "B_wk", "B_wv",
                                "B_wp", "B_bp", "mask8"])
        O = c.sbuf(ctx, "O", [P, NT, P])
        QcT = c.sbuf(ctx, "QcT", [P, 1, N])
        with ExitStack() as inner:
            xT = c.sbuf(inner, "xT", [P, N])
            QT, KT = c.sbuf(inner, "QT", [P, 1, N]), c.sbuf(inner, "KT", [P, 1, N])
            V = c.sbuf(inner, "V", [P, NT, H * 9])
            turn_tokens(c, xT, x, K["ident"])
            products(c, project(QT[:, 0, :], W["B_q"][:], xT, ("bias", W["B_bq"][:, 0:1]))
                     + project(KT[:, 0, :], W["B_k"][:], xT, ("bias", W["B_bk"][:, 0:1]))
                     + project(QcT[:, 0, :], W["B_cq"][:], xT, ("bias", W["B_bcq"][:, 0:1]))
                     + value_jobs(V, W["B_v"], W["B_vrow"], K["ones"], xT))
            self_attention(c, QT, KT, V, O, K, 8, H, "causal", 8 ** -0.5, W["mask8"])
        query_parts = c.nc.dram_tensor("query_parts_0", (LEVELS, P, N), BF16).ap()
        split_queries(c, QcT, 1, query_parts)
        cross_attention(c, query_parts, O, W["B_wk"], W["B_wv"], context_from_dram(c.ins["ctxT"]), K, 8, True, 8 ** -0.5)
        OT = QcT[:, 0, :]
        turn_tokens(c, OT, O, K["ident"])
        summed = c.sbuf(ctx, "summed", [P, NT, P])
        sum_and_norm(c, lambda t: [(tok(OT, t), W["B_wp"][:]), (K["ones"][0:1, 0:P], W["B_bp"][0:1, :])], summed, x, [x])



E1, CAP1, F1 = 8, 512, 512
E2, CAP2, ADAPTERS = 32, 80, 16
BIG = 65536.0


def zero_rows(c, arrays):
    nc = c.nc
    with ExitStack() as ctx:
        zeros = c.sbuf(ctx, "zeros", [P, 2048])
        cleared, filled = c.sem("cleared"), c.sem("filled")
        block = ctx.enter_context(nc.Block())

        @block.vector
        def _(dve):
            dve.memset(zeros[:], 0.0).then_inc(cleared, 1)

        @block.sync
        def _(sp):
            sp.wait_ge(cleared, 1)
            count = 0
            for a in arrays:
                rows = 2048 // a.shape[1] * P
                for r in range(0, a.shape[0], rows):
                    sp.dma_start(a[r:r + rows, :].rearrange("(p k) d -> p (k d)", p=P), zeros[:]).then_inc(filled, 16)
                    count += 1
            sp.wait_ge(filled, 16 * count)


def choose_two(c, ctx, logit_terms, E, iota):
    nc = c.nc
    gates = c.sbuf(ctx, "gates", [P, NT, E])
    top = c.sbuf(ctx, "top", [P, NT, 8])
    hot = [c.sbuf(ctx, f"hot{k}", [P, NT, E]) for k in range(2)]
    with ExitStack() as inner:
        acc = c.psum(inner, "logits", [P, NT, E])
        row_max, row_sum = c.sbuf(inner, "row_max", [P, NT]), c.sbuf(inner, "row_sum", [P, NT])
        index = c.sbuf(inner, "index", [P, NT, 8], U32)
        indexf = c.sbuf(inner, "indexf", [P, NT, 8])
        logits_ready, shifted, powers = c.sem("logits_ready"), c.sem("logits_shifted"), c.sem("powers")
        block = inner.enter_context(nc.Block())

        @block.tensor
        def _(pe):
            for t in range(NT):
                lhsT, rhs = logit_terms(t)
                op = pe.matmul(acc[:, t, :], lhsT, rhs, start=True, stop=True)
            op.then_inc(logits_ready, 1)

        @block.scalar
        def _(act):
            act.wait_ge(shifted, 1)
            act.activation(gates[:], gates[:], ACT.Exp).then_inc(powers, 1)

        @block.vector
        def _(dve):
            dve.wait_ge(logits_ready, 1)
            dve.tensor_reduce(row_max[:], acc[:], AX_X, ALU.max)
            dve.drain()
            dve.tensor_tensor(gates[:], acc[:], row_max[:].unsqueeze(2).to_broadcast([P, NT, E]), ALU.subtract)\
               .then_inc(shifted, 1)
            dve.wait_ge(powers, 1)
            dve.tensor_reduce(row_sum[:], gates[:], AX_X, ALU.add)
            dve.drain()
            dve.reciprocal(row_max[:], row_sum[:])
            dve.drain()
            dve.tensor_tensor(gates[:], gates[:], row_max[:].unsqueeze(2).to_broadcast([P, NT, E]), ALU.mult)
            dve.drain()
            for t in range(NT):
                dve.max(top[:, t, :], gates[:, t, :])
            dve.drain()
            for t in range(NT):
                dve.max_index(index[:, t, :], top[:, t, :], gates[:, t, :])
            dve.drain()
            dve.tensor_copy(indexf[:], index[:])
            dve.drain()
            for k in range(2):
                dve.tensor_tensor(hot[k][:], iota[:].unsqueeze(1).to_broadcast([P, NT, E]),
                                  indexf[:, :, k:k + 1].to_broadcast([P, NT, E]), ALU.is_equal)
    return gates, top, hot


def stage_moe(c, x, K):
    nc = c.nc
    rows = nc.dram_tensor("expert_rows", (E1 * CAP1, P), F32).ap()
    results = nc.dram_tensor("expert_results", (E1 * CAP1, P), F32).ap()
    with ExitStack() as ctx:
        W = load_stage(c, ctx, ["C_q", "C_qs", "C_k", "C_ks", "C_v", "C_vrow", "C_proj", "C_g1", "C_s1", "C_g2", "C_s2",
                                "C_gate", "C_b1", "C_b2", "C_cos", "C_sin", "mask8", "iota8", "slot_base", "upto", "all_ones"])
        y = c.sbuf(ctx, "y", [P, NT, P])
        yhat = c.sbuf(ctx, "yhat", [P, NT, P])
        with ExitStack() as inner:
            O = c.sbuf(inner, "O", [P, NT, P])
            hT = c.sbuf(inner, "hT", [P, N])
            QT, KT = c.sbuf(inner, "QT", [P, 1, N]), c.sbuf(inner, "KT", [P, 1, N])
            V = c.sbuf(inner, "V", [P, NT, H * 9])
            with ExitStack() as part:
                Qs, Ks = c.sbuf(part, "Qs", [P, N]), c.sbuf(part, "Ks", [P, N])
                sum_and_norm(c, None, None, yhat, [x])
                turn_tokens(c, hT, yhat, K["ident"], (W["C_g1"][:, 0:1], W["C_s1"][:, 0:1]))
                cos, sin = ("mul", W["C_cos"][:]), ("mul", W["C_sin"][:])
                products(c, project(QT[:, 0, :], W["C_q"][:], hT, cos) + project(Qs, W["C_qs"][:], hT, sin)
                         + project(KT[:, 0, :], W["C_k"][:], hT, cos) + project(Ks, W["C_ks"][:], hT, sin)
                         + value_jobs(V, W["C_v"], W["C_vrow"], K["ones"], hT))
                add_pairs(c, [(QT[:, 0, :], Qs[:]), (KT[:, 0, :], Ks[:])])
            self_attention(c, QT, KT, V, O, K, 8, H, "causal", 8 ** -0.5, W["mask8"])
            turn_tokens(c, hT, O, K["ident"])
            sum_and_norm(c, lambda t: [(tok(hT, t), W["C_proj"][:])], y, yhat, [x])
        h2T = c.sbuf(ctx, "h2T", [P, N])
        turn_tokens(c, h2T, yhat, K["ident"], (W["C_g2"][:, 0:1], W["C_s2"][:, 0:1]))
        zero_rows(c, [rows])
        gates, top, hot = choose_two(c, ctx, lambda t: (tok(h2T, t), W["C_gate"][:]), E1, W["iota8"])

        place = [c.sbuf(ctx, f"place{k}", [P, NT], I32) for k in range(2)]
        source = [c.sbuf(ctx, f"source{k}", [P, NT], I32) for k in range(2)]
        weight = [c.sbuf(ctx, f"weight{k}", [P, NT]) for k in range(2)]
        with ExitStack() as inner:
            acc = c.psum(inner, "counts", [P, 2, BANK])
            chosen = c.sbuf(inner, "chosen", [P, NT, E1])
            sums = [c.sbuf(inner, f"sums{k}", [P, NT, E1]) for k in range(2)]
            slot, keep, pick = (c.sbuf(inner, n, [P, NT, E1]) for n in ("slot", "keep", "pick"))
            at, kept, scratch = (c.sbuf(inner, n, [P, NT]) for n in ("at", "kept", "scratch"))
            chosen_ready, counted = c.sem("chosen_ready"), c.sem("counted")
            places_ready, scattered = c.sem("places_ready"), c.sem("scattered", True)
            block = inner.enter_context(nc.Block())

            @block.tensor
            def _(pe):
                pe.wait_ge(chosen_ready, 1)
                flat = chosen[:].rearrange("p t e -> p (t e)")
                pe.matmul(acc[:, 0, 0:NT * E1], W["upto"][:], flat, start=True, stop=True)
                pe.matmul(acc[:, 1, 0:NT * E1], W["all_ones"][:], flat, start=True, stop=True).then_inc(counted, 1)

            @block.vector
            def _(dve):
                dve.tensor_tensor(chosen[:], hot[0][:], hot[1][:], ALU.add).then_inc(chosen_ready, 1)
                dve.wait_ge(counted, 1)
                within = acc[:, 0, 0:NT * E1].rearrange("p (t e) -> p t e", t=NT)
                totals = acc[:, 1, 0:NT * E1].rearrange("p (t e) -> p t e", t=NT)
                dve.tensor_copy(sums[0][:], totals)
                step, now = 1, 0
                while step < NT:
                    dve.drain()
                    a, b_ = sums[now], sums[1 - now]
                    dve.tensor_copy(b_[:, 0:step, :], a[:, 0:step, :])
                    dve.tensor_tensor(b_[:, step:, :], a[:, step:, :], a[:, 0:NT - step, :], ALU.add)
                    step, now = 2 * step, 1 - now
                dve.drain()
                dve.tensor_tensor(slot[:], sums[now][:], totals, ALU.subtract)
                dve.drain()
                dve.tensor_tensor(slot[:], slot[:], within, ALU.add)
                dve.drain()
                dve.tensor_scalar(keep[:], slot[:], CAP1 + 0.5, None, ALU.is_lt)
                dve.tensor_tensor(sums[0][:], slot[:], W["slot_base"][:].unsqueeze(1).to_broadcast([P, NT, E1]), ALU.add)
                for k in range(2):
                    dve.drain()
                    dve.tensor_tensor(pick[:], hot[k][:], sums[0][:], ALU.mult)
                    dve.tensor_tensor(slot[:], hot[k][:], keep[:], ALU.mult)
                    dve.drain()
                    dve.tensor_reduce(at[:], pick[:], AX_X, ALU.add)
                    dve.tensor_reduce(kept[:], slot[:], AX_X, ALU.add)
                    dve.drain()
                    dve.tensor_tensor(weight[k][:], top[:, :, k], kept[:], ALU.mult)
                    dve.tensor_tensor(source[k][:], at[:], kept[:], ALU.mult)
                    dve.tensor_scalar(scratch[:], kept[:], -BIG, BIG, ALU.mult, ALU.add)
                    dve.drain()
                    dve.tensor_tensor(place[k][:], at[:], scratch[:], ALU.add)
                dve.drain().then_inc(places_ready, 1)

            @block.gpsimd
            def _(pool):
                pool.wait_ge(places_ready, 1)
                for t in range(NT):
                    for k in range(2):
                        pool.indirect_dma_start(rows, bass.IndirectOffsetOnAxis(place[k][:, t:t + 1], 0), yhat[:, t, :],
                                                None, bounds_check=E1 * CAP1 - 1, oob_is_err=False)\
                            .then_inc(scattered, 16)
                pool.wait_ge(scattered, 16 * 2 * NT)

        moe_experts(c, W, K, rows, results)

        back = [c.sbuf(ctx, f"back{k}", [P, NT, P]) for k in range(2)]
        gathered = c.sem("gathered", True)
        with nc.Block() as block:
            @block.gpsimd
            def _(pool):
                for t in range(NT):
                    for k in range(2):
                        pool.indirect_dma_start(back[k][:, t, :], None, results,
                                                bass.IndirectOffsetOnAxis(source[k][:, t:t + 1], 0))\
                            .then_inc(gathered, 16)

            @block.vector
            def _(dve):
                dve.tensor_tensor(y[:], y[:], x[:], ALU.add)
                dve.wait_ge(gathered, 16 * 2 * NT)
                for k in range(2):
                    dve.drain()
                    for t in range(NT):
                        dve.scalar_tensor_tensor(out=y[:, t, :], in0=back[k][:, t, :], scalar=weight[k][:, t:t + 1],
                                                 in1=y[:, t, :], op0=ALU.mult, op1=ALU.add)
        sum_and_norm(c, None, None, x, [y])


def moe_experts(c, W, K, rows, results):
    nc = c.nc
    NF, NS = F1 // P, CAP1 // P
    with ExitStack() as ctx:
        turned = c.psum(ctx, "turned", [P, BANK])
        wide = c.psum(ctx, "wide", [P, NF, BANK])
        back = c.psum(ctx, "back", [P, NS, P])
        xe = c.sbuf(ctx, "expert_rows", [P, 2, NS, P])
        w1, w2 = c.sbuf(ctx, "w1", [P, 2, F1]), c.sbuf(ctx, "w2", [P, 2, NF, P])
        xeT = c.sbuf(ctx, "expert_rowsT", [P, CAP1])
        hid = c.sbuf(ctx, "hidden", [P, NF, CAP1])
        res = c.sbuf(ctx, "result_rows", [P, 2, NS, P])
        loaded = [c.sem("expert_loaded0"), c.sem("expert_loaded1")]
        turned_ready, turned_copied = c.sem("turned_ready"), c.sem("turned_copied")
        wide_ready, hidden_ready = c.sem("wide_ready"), c.sem("hidden_ready")
        back_ready, back_copied = c.sem("back_ready"), c.sem("back_copied")
        stored = [c.sem("stored0"), c.sem("stored1")]
        block = ctx.enter_context(nc.Block())

        @block.sync
        def _(sp):
            def load(e, s):
                sp.wait_ge(back_ready, e + 1)
                sp.dma_start(xe[:, s, :, :], rows[bass.ds(e * CAP1, CAP1), :].rearrange("(s p) d -> p s d", p=P))\
                  .then_inc(loaded[s], 16)
                sp.dma_start(w1[:, s, :], c.ins["C_w1"][bass.ds(e, 1), :, :].rearrange("o p f -> (o p) f"))\
                  .then_inc(loaded[s], 16)
                sp.dma_start(w2[:, s, :, :], c.ins["C_w2"][bass.ds(e, 1), :, :, :].rearrange("o p f d -> (o p) f d"))\
                  .then_inc(loaded[s], 16)

            def store(e, s):
                sp.wait_ge(back_copied, e + 2)
                sp.dma_start(results[bass.ds(e * CAP1, CAP1), :].rearrange("(s p) d -> p s d", p=P), res[:, s, :, :])\
                  .then_inc(stored[s], 16)

            for s in range(2):
                sp.sem_inc(stored[s], 16)
                load(s, s)
            with sp.Fori(1, E1 // 2, 1) as i:
                for s in range(2):
                    load(i * 2 + s, s)
                    store(i * 2 + s - 2, s)
            for s in range(2):
                store(E1 - 2 + s, s)
            for s in range(2):
                sp.wait_ge(stored[s], 16 + 16 * (E1 // 2))

        @block.tensor
        def _(pe):
            pe.sem_inc(back_ready, 2)
            with pe.Fori(0, E1 // 2, 1) as i:
                for s in range(2):
                    e = i * 2 + s
                    pe.wait_ge(loaded[s], i * 48 + 48)
                    pe.wait_ge(turned_copied, e + 1)
                    for k in range(NS):
                        op = pe.transpose(turned[:, k * P:k * P + P], xe[:, s, k, :], K["ident"][:])
                    op.then_inc(turned_ready, 1)
                    pe.wait_ge(turned_copied, e + 2)
                    for f in range(NF):
                        pe.wait_ge(hidden_ready, e * NF + f + 1)
                        pe.matmul(wide[:, f, :], w1[:, s, f * P:f * P + P], xeT[:], start=True, stop=True)\
                          .then_inc(wide_ready, 1)
                    pe.wait_ge(hidden_ready, e * NF + 2 * NF)
                    pe.wait_ge(back_copied, e + 1)
                    for k in range(NS):
                        for f in range(NF):
                            pe.matmul(back[:, k, :], hid[:, f, k * P:k * P + P], w2[:, s, f, :], start=f == 0, stop=False)
                        op = pe.matmul(back[:, k, :], K["ones"][0:1, 0:P], W["C_b2"][0:1, bass.ds(e * P, P)],
                                       start=False, stop=True)
                    op.then_inc(back_ready, 1)

        @block.scalar
        def _(act):
            act.sem_inc(hidden_ready, NF)
            with act.Fori(0, E1 // 2, 1) as i:
                for s in range(2):
                    e = i * 2 + s
                    for f in range(NF):
                        act.wait_ge(wide_ready, e * NF + f + 1)
                        if f == 0:
                            act.wait_ge(back_ready, e + 2)
                        act.activation(hid[:, f, :], wide[:, f, :], ACT.Gelu, bias=W["C_b1"][:, bass.ds(e * NF + f, 1)])\
                           .then_inc(hidden_ready, 1)

        @block.vector
        def _(dve):
            dve.sem_inc(turned_copied, 1)
            dve.sem_inc(back_copied, 1)
            with dve.Fori(0, E1 // 2, 1) as i:
                for s in range(2):
                    e = i * 2 + s
                    dve.wait_ge(turned_ready, e + 1)
                    dve.tensor_scalar(xeT[:], turned[:], W["C_g2"][:, 0:1], W["C_s2"][:, 0:1], ALU.mult, ALU.add)\
                       .then_inc(turned_copied, 1)
                    dve.wait_ge(stored[s], i * 16 + 16)
                    dve.wait_ge(back_ready, e + 3)
                    dve.tensor_copy(res[:, s, :, :], back[:]).then_inc(back_copied, 1)


def stage_single_head(c, x, K):
    with ExitStack() as ctx:
        W = load_stage(c, ctx, ["D_q", "D_k", "D_v", "D_vrow"])
        O = c.sbuf(ctx, "O", [P, NT, P])
        xT = c.sbuf(ctx, "xT", [P, N])
        QT, KT = c.sbuf(ctx, "QT", [P, 1, N]), c.sbuf(ctx, "KT", [P, 1, N])
        V = c.sbuf(ctx, "V", [P, NT, P + 1])
        turn_tokens(c, xT, x, K["ident"])
        products(c, project(QT[:, 0, :], W["D_q"][:], xT) + project(KT[:, 0, :], W["D_k"][:], xT)
                 + value_jobs(V, W["D_v"], W["D_vrow"], K["ones"], xT))
        self_attention(c, QT, KT, V, O, K, P, 1, "causal", P ** -0.5)
        add_pairs(c, [(O[:], x[:])])
        sum_and_norm(c, None, None, x, [O])


def feed_forward(c, W, K, name, xo, others, out):
    nc = c.nc
    NF = 4
    with ExitStack() as ctx:
        hat, hatT = c.sbuf(ctx, "hat", [P, NT, P]), c.sbuf(ctx, "hatT", [P, N])
        wide = c.sbuf(ctx, "wide", [P, NF, N])
        sum_and_norm(c, None, None, hat, [xo])
        turn_tokens(c, hatT, hat, K["ident"], (W[name + "_g3"][:, 0:1], W[name + "_s3"][:, 0:1]))
        products(c, [(chunk(wide[:, f, :], k), [(W[name + "_w2"][:, f * P:f * P + P], chunk(hatT, k))],
                      ("gelu", W[name + "_b2"][:, f:f + 1])) for k in range(CH) for f in range(NF)])
        sum_and_norm(c, lambda t: [(tok(wide[:, f, :], t), W[name + "_w3"][:, f, :]) for f in range(NF)]
                     + [(K["ones"][0:1, 0:P], W[name + "_b3"][0:1, :])], out, None, others + [xo])


def turn_wide(c, dst, src, K):
    transpose_tiles(c, [([src[:, 4 * g + k, w * P:w * P + P] for k in range(4)], chunk(dst[:, w, :], g), None)
                        for w in range(4) for g in range(CH)], K["ident"])


def norm_context(c, W, K, dst):
    nc = c.nc
    full, rest = CTX // P, CTX % P
    with ExitStack() as ctx:
        raw = c.sbuf(ctx, "raw", [P, 2, NKT, CC])
        hat = c.sbuf(ctx, "hat", [P, NKT, CC])
        stats, moments = c.sbuf(ctx, "stats", [P, NKT, 6]), c.sbuf(ctx, "moments", [P, NKT, 2])
        deviation, rstd = c.sbuf(ctx, "deviation", [P, NKT]), c.sbuf(ctx, "rstd", [P, NKT])
        eps = c.sbuf(ctx, "eps", [P, 1])
        out = c.sbuf(ctx, "out", [CC, CTX_PAD])
        turned = c.psum(ctx, "turned", [P, 4, BANK])
        cleared = c.sem("cleared")
        loaded = [c.sem("raw_loaded0"), c.sem("raw_loaded1")]
        variances, deviations = c.sem("variances"), c.sem("deviations")
        normed, turned_ready, copied, stored = c.sem("normed"), c.sem("turned_ready"), c.sem("copied"), c.sem("stored")
        block = ctx.enter_context(nc.Block())

        @block.sync
        def _(sp):
            def load(b, s):
                src = c.ins["ctx"][bass.ds(b, 1), :, :].rearrange("o k d -> (o k) d")
                sp.dma_start(raw[:, s, 0:full, :], src[0:full * P, :].rearrange("(t p) d -> p t d", p=P))\
                  .then_inc(loaded[s], 16)
                sp.dma_start(raw[0:rest, s, full, :], src[full * P:CTX, :]).then_inc(loaded[s], 16)

            def store(b):
                sp.wait_ge(copied, b * 4 + 8)
                sp.dma_start(dst[bass.ds(b, 1), :, :].rearrange("o c k -> (o c) k"), out[:, 0:CTX]).then_inc(stored, 16)

            sp.wait_ge(cleared, 1)
            sp.sem_inc(stored, 16)
            for s in range(2):
                load(s, s)
            with sp.Fori(1, B // 2, 1) as i:
                for s in range(2):
                    b = i * 2 + s
                    sp.wait_ge(normed, b - 1)
                    load(b, s)
                    store(b - 2)
            for b in range(B - 2, B):
                store(b)
            sp.wait_ge(stored, 16 + 16 * B)

        @block.tensor
        def _(pe):
            with pe.Fori(0, B, 1) as b:
                pe.wait_ge(normed, b + 1)
                for g in range(4):
                    pe.wait_ge(copied, b * 4 + g + 1)
                    pe.sem_inc(c.seen, 1)
                    for t in range(4 * g, min(4 * g + 4, NKT)):
                        op = pe.transpose(turned[0:CC, g, (t % 4) * P:(t % 4) * P + P], hat[:, t, :], K["ident"][:])
                    op.then_inc(turned_ready, 1)

        @block.scalar
        def _(act):
            act.sem_inc(copied, 4)
            with act.Fori(0, B, 1) as b:
                act.wait_ge(variances, b + 1)
                act.activation(deviation[:], moments[:, :, 1], ACT.Sqrt, bias=eps[:, 0:1]).then_inc(deviations, 1)
                act.wait_ge(stored, b * 16 + 16)
                for g in range(4):
                    act.wait_ge(turned_ready, b * 4 + g + 1)
                    cols = min(BANK, CTX_PAD - g * BANK)
                    act.activation(out[:, g * BANK:g * BANK + cols], turned[0:CC, g, 0:cols], ACT.Identity,
                                   scale=W["a2_yg"][:, 0:1], bias=W["a2_ys"][:, 0:1]).then_inc(copied, 1)

        @block.vector
        def _(dve):
            dve.memset(eps[:], EPS)
            dve.memset(raw[:], 0.0).then_inc(cleared, 1)
            with dve.Fori(0, B // 2, 1) as i:
                for s in range(2):
                    b = i * 2 + s
                    dve.wait_ge(loaded[s], i * 32 + 32)
                    for t in range(NKT):
                        dve.bn_stats(stats[:, t, :], raw[:, s, t, :])
                    dve.drain()
                    for t in range(NKT):
                        op = dve.bn_aggr(moments[:, t, :], stats[:, t, :])
                    op.then_inc(variances, 1)
                    dve.wait_ge(deviations, b + 1)
                    dve.reciprocal(rstd[:], deviation[:])
                    dve.drain()
                    dve.wait_ge(copied, b * 4 + 4)
                    for t in range(NKT):
                        op = dve.tensor_scalar(hat[:, t, :], raw[:, s, t, :], moments[:, t, 0:1], rstd[:, t:t + 1],
                                               ALU.subtract, ALU.mult)
                    op.then_inc(normed, 1)
                    dve.drain()


def stage_two_blocks(c, x, K):
    nc = c.nc
    normed_ctx = nc.dram_tensor("normed_context", (B, CC, CTX), F32).ap()
    with ExitStack() as ctx:
        x1 = c.sbuf(ctx, "x1", [P, NT, P])
        with ExitStack() as first:
            W = load_stage(c, first, ["*E_g1", "*E_s1", "*E_g2", "*E_s2", "a1_q", "a1_k", "a1_v", "a1_vrow", "a1_li1",
                                      "a1_b1", "a1_xg", "a1_xs", "a1_yg", "a1_ys", "a1_g3", "a1_s3", "a1_w2", "a1_b2",
                                      "a1_w3", "a1_b3", "mask32"])
            sum_and_norm(c, None, None, x1, [x], W["E_g1"], W["E_s1"])
            xo = c.sbuf(first, "xo", [P, NT, P])
            QT = c.sbuf(first, "QT", [P, 4, N])
            with ExitStack() as inner:
                O = c.sbuf(inner, "O", [P, NT, 4 * P])
                with ExitStack() as part:
                    KT = c.sbuf(part, "KT", [P, 4, N])
                    V = c.sbuf(part, "V", [P, NT, H * 33])
                    with ExitStack() as proj:
                        hat, hatT = c.sbuf(proj, "hat", [P, NT, P]), c.sbuf(proj, "hatT", [P, N])
                        sum_and_norm(c, None, None, hat, [x1])
                        turn_tokens(c, hatT, hat, K["ident"], (W["a1_xg"][:, 0:1], W["a1_xs"][:, 0:1]))
                        products(c, [j for g in range(4) for j in project(QT[:, g, :], W["a1_q"][:, g * P:g * P + P], hatT)])
                        turn_tokens(c, hatT, hat, K["ident"], (W["a1_yg"][:, 0:1], W["a1_ys"][:, 0:1]))
                        products(c, [j for g in range(4) for j in project(KT[:, g, :], W["a1_k"][:, g * P:g * P + P], hatT)]
                                 + value_jobs(V, W["a1_v"], W["a1_vrow"], K["ones"], hatT))
                    self_attention(c, QT, KT, V, O, K, 32, H, "future", 32 ** -0.5, W["mask32"])
                turn_wide(c, QT, O, K)
            sum_and_norm(c, lambda t: [(tok(QT[:, g, :], t), W["a1_li1"][:, g, :]) for g in range(4)]
                         + [(K["ones"][0:1, 0:P], W["a1_b1"][0:1, :])], xo, None, [x1])
            feed_forward(c, W, K, "a1", xo, [x1], x1)
            sum_and_norm(c, None, None, x1, [x1], W["E_g2"], W["E_s2"])
        with ExitStack() as second:
            W = load_stage(c, second, ["a2_q", "a2_wk", "a2_wv", "a2_li1", "a2_b1", "a2_xg", "a2_xs", "a2_yg", "a2_ys",
                                       "a2_g3", "a2_s3", "a2_w2", "a2_b2", "a2_w3", "a2_b3"])
            norm_context(c, W, K, normed_ctx)
            query_parts = nc.dram_tensor("query_parts_1", (LEVELS, 4 * P, N), BF16).ap()
            with ExitStack() as inner:
                QT = c.sbuf(inner, "QT", [P, 4, N])
                hat, hatT = c.sbuf(inner, "hat", [P, NT, P]), c.sbuf(inner, "hatT", [P, N])
                sum_and_norm(c, None, None, hat, [x1])
                turn_tokens(c, hatT, hat, K["ident"], (W["a2_xg"][:, 0:1], W["a2_xs"][:, 0:1]))
                products(c, [j for g in range(4) for j in project(QT[:, g, :], W["a2_q"][:, g * P:g * P + P], hatT)])
                split_queries(c, QT, 4, query_parts)
            O = c.sbuf(second, "O", [P, NT, 4 * P])
            cross_attention(c, query_parts, O, W["a2_wk"], W["a2_wv"], context_from_dram(normed_ctx), K, 32, False,
                            32 ** -0.5)
            OT = c.sbuf(second, "OT", [P, 4, N])
            turn_wide(c, OT, O, K)
            xo = c.sbuf(second, "xo", [P, NT, P])
            sum_and_norm(c, lambda t: [(tok(OT[:, g, :], t), W["a2_li1"][:, g, :]) for g in range(4)]
                         + [(K["ones"][0:1, 0:P], W["a2_b1"][0:1, :])], xo, None, [x1])
            feed_forward(c, W, K, "a2", xo, [x1, x], x1)
        sum_and_norm(c, None, None, x, [x1])


def stage_routed(c, x, K):
    nc = c.nc
    ROW = P + 2 * E2
    table = nc.dram_tensor("token_table", (N, ROW), F32).ap()
    results = nc.dram_tensor("slot_results", (2 * N, P), F32).ap()
    with ExitStack() as ctx:
        W = load_stage(c, ctx, ["F_r1", "F_r1s", "F_b1", "F_r2", "iota32", "double_token"])
        zero_rows(c, [results])
        rows = c.sbuf(ctx, "rows", [P, NT, ROW])
        indexT = c.sbuf(ctx, "indexT", [CAP2, E2], I32)
        with ExitStack() as inner:
            xT = c.sbuf(inner, "xT", [P, N])
            st = c.sbuf(inner, "st", [P, NT, 6])
            stT = c.sbuf(inner, "stT", [6, N])
            hT = c.sbuf(inner, "hT", [64, N])
            token_statistics(c, x, st)
            turn_tokens(c, xT, x, K["ident"])
            turn_tokens(c, stT, st, K["ident"])
            products(c, [(hT[:, k * BANK:k * BANK + BANK], [(W["F_r1"][:], chunk(xT, k)), (W["F_r1s"][:], stT[:, k * BANK:k * BANK + BANK])],
                          ("gelu", W["F_b1"][:, 0:1])) for k in range(CH)])
            probs, top, hot = choose_two(c, inner, lambda t: (hT[:, t * P:t * P + P], W["F_r2"][:]), E2, W["iota32"])
            score = c.sbuf(inner, "score", [P, NT, E2])
            wsum, wnorm = c.sbuf(inner, "wsum", [P, NT]), c.sbuf(inner, "wnorm", [P, 2, NT])
            routed, tmp = c.sbuf(inner, "routed", [P, NT, E2]), c.sbuf(inner, "tmp", [P, NT, E2])
            with nc.Block() as block:
                @block.vector
                def _(dve):
                    dve.tensor_copy(rows[:, :, 0:P], x[:])
                    dve.tensor_tensor(wsum[:], top[:, :, 0], top[:, :, 1], ALU.add)
                    dve.tensor_tensor(routed[:], hot[0][:], hot[1][:], ALU.add)
                    dve.drain()
                    dve.reciprocal(wsum[:], wsum[:])
                    dve.tensor_tensor(score[:], probs[:], routed[:], ALU.mult)
                    dve.drain()
                    for k in range(2):
                        dve.tensor_tensor(wnorm[:, k, :], top[:, :, k], wsum[:], ALU.mult)
                    dve.scalar_tensor_tensor(out=score[:], in0=routed[:], scalar=-1.0, in1=score[:], op0=ALU.add, op1=ALU.add)
                    dve.scalar_tensor_tensor(out=tmp[:], in0=routed[:], scalar=-BIG, in1=hot[1][:], op0=ALU.mult, op1=ALU.add)
                    dve.drain()
                    dve.tensor_tensor(rows[:, :, P + E2:ROW], tmp[:], W["double_token"][:].unsqueeze(2).to_broadcast([P, NT, E2]),
                                      ALU.add)
                    dve.tensor_tensor(rows[:, :, P:P + E2], hot[0][:], wnorm[:, 0, :].unsqueeze(2).to_broadcast([P, NT, E2]),
                                      ALU.mult)
                    dve.tensor_tensor(routed[:], hot[1][:], wnorm[:, 1, :].unsqueeze(2).to_broadcast([P, NT, E2]), ALU.mult)
                    dve.drain()
                    dve.tensor_tensor(rows[:, :, P:P + E2], rows[:, :, P:P + E2], routed[:], ALU.add)
            scoreT = [c.sbuf(inner, f"scoreT{k}", [E2, N]) for k in range(2)]
            turn_tokens(c, scoreT[0], score, K["ident"])
            choose_tokens(c, scoreT, indexT, table, rows, K)
        routed_experts(c, K, table, results, indexT)
        back = c.sbuf(ctx, "back", [P, NT, 2, P])
        came = c.sem("results_loaded")
        total = c.sbuf(ctx, "total", [P, NT, P])
        with nc.Block() as block:
            @block.sync
            def _(sp):
                sp.dma_start(back[:].rearrange("p t k d -> p t (k d)"), results.rearrange("(t p k) d -> p t (k d)", p=P, k=2))\
                  .then_inc(came, 16)

            @block.vector
            def _(dve):
                dve.wait_ge(came, 16)
                dve.tensor_tensor(total[:], back[:, :, 0, :], back[:, :, 1, :], ALU.add)
                dve.drain()
                dve.tensor_tensor(total[:], total[:], x[:], ALU.add)
        sum_and_norm(c, None, None, x, [total])


def token_statistics(c, x, st):
    nc = c.nc
    with ExitStack() as ctx:
        stats, moments = c.sbuf(ctx, "stats", [P, NT, 6]), c.sbuf(ctx, "moments", [P, NT, 2])
        roots, near = c.sbuf(ctx, "roots", [P, 2, NT]), c.sbuf(ctx, "near", [P, NT, P])
        zeros = c.sem("near_zeros")
        squares, rooted = c.sem("squares"), c.sem("rooted")
        block = ctx.enter_context(nc.Block())

        @block.vector
        def _(dve):
            for t in range(NT):
                dve.bn_stats(stats[:, t, :], x[:, t, :])
            dve.drain()
            for t in range(NT):
                dve.bn_aggr(moments[:, t, :], stats[:, t, :])
            dve.drain()
            dve.tensor_scalar(roots[:, 0, :], moments[:, :, 1], P / (P - 1.0), None, ALU.mult)
            dve.tensor_tensor(roots[:, 1, :], moments[:, :, 0], moments[:, :, 0], ALU.mult)
            dve.drain()
            dve.tensor_tensor(roots[:, 1, :], roots[:, 1, :], moments[:, :, 1], ALU.add)
            dve.drain()
            dve.tensor_scalar(roots[:, 1, :], roots[:, 1, :], float(P), None, ALU.mult).then_inc(squares, 1)
            dve.tensor_copy(st[:, :, 0], moments[:, :, 0])
            dve.tensor_reduce(st[:, :, 2], x[:], AX_X, ALU.min)
            dve.tensor_reduce(st[:, :, 3], x[:], AX_X, ALU.max)
            dve.tensor_scalar(near[:], x[:], 1e-6, None, ALU.is_lt)
            dve.drain()
            dve.scalar_tensor_tensor(out=near[:], in0=x[:], scalar=-1e-6, in1=near[:], op0=ALU.is_gt, op1=ALU.mult)
            dve.drain()
            dve.tensor_reduce(st[:, :, 5], near[:], AX_X, ALU.add)
            dve.drain()
            dve.tensor_scalar(st[:, :, 5], st[:, :, 5], 1.0 / P, None, ALU.mult)
            dve.wait_ge(rooted, 1)
            dve.tensor_copy(st[:, :, 1], roots[:, 0, :])
            dve.tensor_copy(st[:, :, 4], roots[:, 1, :])

        @block.scalar
        def _(act):
            act.wait_ge(squares, 1)
            act.activation(roots[:], roots[:], ACT.Sqrt).then_inc(rooted, 1)


def choose_tokens(c, scoreT, indexT, table, rows, K):
    nc = c.nc
    with ExitStack() as ctx:
        best = c.sbuf(ctx, "best", [E2, CAP2])
        index, indexf = c.sbuf(ctx, "index", [E2, CAP2], U32), c.sbuf(ctx, "indexf", [E2, CAP2])
        turned = c.psum(ctx, "turned", [CAP2, E2])
        stored, ready, turned_ready = c.sem("table_stored"), c.sem("index_ready"), c.sem("turned_ready")
        block = ctx.enter_context(nc.Block())

        @block.sync
        def _(sp):
            sp.dma_start(table.rearrange("(t p) w -> p t w", p=P), rows[:]).then_inc(stored, 16)
            sp.wait_ge(stored, 16)

        @block.vector
        def _(dve):
            for r in range(CAP2 // 8):
                now, then, eight = scoreT[r % 2], scoreT[1 - r % 2], slice(8 * r, 8 * r + 8)
                dve.max(best[:, eight], now[:])
                dve.drain()
                dve.max_index(index[:, eight], best[:, eight], now[:])
                dve.match_replace(then[:], best[:, eight], now[:], -2.0)
                dve.drain()
            dve.tensor_copy(indexf[:], index[:]).then_inc(ready, 1)
            dve.wait_ge(turned_ready, 1)
            dve.tensor_copy(indexT[:], turned[:])

        @block.tensor
        def _(pe):
            pe.wait_ge(ready, 1)
            pe.transpose(turned[:], indexf[:], K["ident"][0:E2, 0:E2]).then_inc(turned_ready, 1)


def routed_experts(c, K, table, results, indexT):
    nc = c.nc
    ROW = table.shape[1]
    with ExitStack() as ctx:
        xg = c.sbuf(ctx, "token_rows", [CAP2, 2, ROW])
        which = c.sbuf(ctx, "which", [CAP2, 2], I32)
        target = c.sbuf(ctx, "target", [CAP2, 2], I32)
        xgT = c.sbuf(ctx, "tokenT", [P, 2, CAP2])
        wu, wd = c.sbuf(ctx, "w_up", [P, 2, 512]), c.sbuf(ctx, "w_down", [P, 2, 2, P])
        au, ad = c.sbuf(ctx, "a_up", [P, 2 * P]), c.sbuf(ctx, "a_down", [P, P])
        gate = c.sbuf(ctx, "gate", [P, 2, 3 * CAP2])
        hid = c.sbuf(ctx, "hidden", [P, 2, 3 * CAP2])
        res = c.sbuf(ctx, "result", [CAP2, 2, P])
        turned = c.psum(ctx, "turned", [P, 2, BANK])
        up = c.psum(ctx, "up", [P, 2, BANK])
        down = c.psum(ctx, "down", [P, 2, BANK])
        weights = [c.sem("weights0"), c.sem("weights1")]
        adapters = c.sem("adapters")
        which_ready, gathered = c.sem("which_ready"), [c.sem("gathered0", True), c.sem("gathered1", True)]
        turned_ready, token_ready = c.sem("turned_ready"), c.sem("token_ready")
        up_ready, gate_ready, hidden_ready = c.sem("up_ready"), c.sem("gate_ready"), c.sem("hidden_ready")
        down_ready, result_ready = c.sem("down_ready"), c.sem("result_ready")
        scattered = [c.sem("scattered0", True), c.sem("scattered1", True)]
        block = ctx.enter_context(nc.Block())

        @block.sync
        def _(sp):
            with sp.Fori(0, E2 // 2, 1) as i:
                for s in range(2):
                    e = i * 2 + s
                    sp.wait_ge(down_ready, e + 1)
                    sp.dma_start(wu[:, s, :], c.ins["F_up"][bass.ds(e, 1), :, :].rearrange("o p j -> (o p) j"))\
                      .then_inc(weights[s], 16)
                    sp.dma_start(wd[:, s, :, :], c.ins["F_down"][bass.ds(e, 1), :, :, :].rearrange("o p j d -> (o p) j d"))\
                      .then_inc(weights[s], 16)
                    if s == 0:
                        sp.wait_ge(down_ready, e + 2)
                        sp.dma_start(au[:], c.ins["F_aup"][bass.ds(i, 1), :, :].rearrange("o p j -> (o p) j"))\
                          .then_inc(adapters, 16)
                        sp.dma_start(ad[:], c.ins["F_adown"][bass.ds(i, 1), :, :].rearrange("o p j -> (o p) j"))\
                          .then_inc(adapters, 16)

        @block.gpsimd
        def _(pool):
            def gather(s, wait):
                pool.wait_ge(which_ready, wait)
                pool.indirect_dma_start(xg[:, s, :], None, table, bass.IndirectOffsetOnAxis(which[:, s:s + 1], 0))\
                    .then_inc(gathered[s], 16)

            with pool.Fori(0, E2 // 2, 1) as i:
                for s in range(2):
                    pool.wait_ge(which_ready, i * 2 + s + 1)
                    pool.sem_inc(c.seen, 1)
                    pool.indirect_dma_start(xg[:, s, :], None, table, bass.IndirectOffsetOnAxis(which[:, s:s + 1], 0))\
                        .then_inc(gathered[s], 16)
                for s in range(2):
                    pool.wait_ge(result_ready, i * 2 + s + 1)
                    pool.sem_inc(c.seen, 1)
                    pool.indirect_dma_start(results, bass.IndirectOffsetOnAxis(target[:, s:s + 1], 0), res[:, s, :], None,
                                            bounds_check=2 * N - 1, oob_is_err=False).then_inc(scattered[s], 16)
            for s in range(2):
                pool.wait_ge(scattered[s], 16 * (E2 // 2))

        @block.tensor
        def _(pe):
            pe.sem_inc(down_ready, 2)
            with pe.Fori(0, E2 // 2, 1) as i:
                for s in range(2):
                    e = i * 2 + s
                    pe.wait_ge(gathered[s], i * 16 + 16)
                    pe.wait_ge(token_ready, e + 1)
                    pe.transpose(turned[:, s, 0:CAP2], xg[:, s, 0:P], K["ident"][0:CAP2, 0:CAP2]).then_inc(turned_ready, 1)
                for s in range(2):
                    e = i * 2 + s
                    pe.wait_ge(weights[s], i * 32 + 32)
                    pe.wait_ge(adapters, i * 32 + 32)
                    pe.wait_ge(token_ready, e + 3)
                    pe.wait_ge(hidden_ready, e + 1)
                    for n, w in enumerate([wu[:, s, 0:P], wu[:, s, P:2 * P], au[:, 0:P], wu[:, s, 2 * P:3 * P],
                                           wu[:, s, 3 * P:4 * P], au[:, P:2 * P]]):
                        op = pe.matmul(up[:, s, n * CAP2:n * CAP2 + CAP2], w, xgT[:, s, :], start=True, stop=True)
                    op.then_inc(up_ready, 1)
                for s in range(2):
                    e = i * 2 + s
                    pe.wait_ge(hidden_ready, e + 3)
                    for n, w in enumerate([wd[:, s, 0, :], wd[:, s, 1, :], ad[:]]):
                        op = pe.matmul(down[0:CAP2, s, 0:P], hid[:, s, n * CAP2:n * CAP2 + CAP2], w, start=n == 0, stop=n == 2)
                    op.then_inc(down_ready, 1)

        @block.scalar
        def _(act):
            with act.Fori(0, E2 // 2, 1) as i:
                for s in range(2):
                    e = i * 2 + s
                    act.wait_ge(up_ready, e + 1)
                    act.activation(gate[:, s, :], up[:, s, 0:3 * CAP2], ACT.Silu).then_inc(gate_ready, 1)

        @block.vector
        def _(dve):
            dve.sem_inc(token_ready, 2)
            dve.sem_inc(hidden_ready, 2)

            def pair(i, first):
                for s in range(2):
                    dve.tensor_copy(which[:, s:s + 1], indexT[:, bass.ds(i * 2 + s, 1)]).then_inc(which_ready, 1)
                for s in range(2):
                    e = i * 2 + s
                    dve.wait_ge(turned_ready, e + 1)
                    dve.tensor_copy(xgT[:, s, :], turned[:, s, 0:CAP2]).then_inc(token_ready, 1)
                for s in range(2):
                    e = i * 2 + s
                    dve.wait_ge(gate_ready, e + 1)
                    dve.tensor_tensor(hid[:, s, 0:2 * CAP2], gate[:, s, 0:2 * CAP2], up[:, s, 3 * CAP2:5 * CAP2], ALU.mult)
                    dve.scalar_tensor_tensor(out=hid[:, s, 2 * CAP2:], in0=gate[:, s, 2 * CAP2:], scalar=0.05,
                                             in1=up[:, s, 5 * CAP2:6 * CAP2], op0=ALU.mult, op1=ALU.mult)\
                       .then_inc(hidden_ready, 1)
                for s in range(2):
                    e = i * 2 + s
                    if not first:
                        dve.wait_ge(scattered[s], i * 16)
                    dve.tensor_copy(target[:, s:s + 1], xg[:, s, bass.ds(e + P + E2, 1)])
                    dve.wait_ge(down_ready, e + 3)
                    dve.tensor_scalar(res[:, s, :], down[0:CAP2, s, 0:P], xg[:, s, bass.ds(e + P, 1)], None, ALU.mult)\
                       .then_inc(result_ready, 1)
                dve.drain()

            pair(0, True)
            with dve.Fori(1, E2 // 2, 1) as i:
                pair(i, False)


STAGES = [stage_mla, stage_self_and_cross, stage_moe, stage_single_head, stage_two_blocks, stage_routed]


def build_program(nc, ins, out, stages=STAGES):
    with ExitStack() as ctx:
        c = Core(nc, ctx, ins)
        x = c.sbuf(ctx, "x", [P, NT, P])
        K = load_stage(c, ctx, ["ident", "identb", "causal_bias", "future_mask", "row_pickers", "ones"])
        came = c.sem("x_loaded")
        with nc.Block() as block:
            @block.sync
            def _(sp):
                sp.dma_start(x[:], ins["x"].rearrange("(t p) d -> p t d", p=P)).then_inc(came, 16)
                sp.wait_ge(came, 16)
        c.end_stage()
        for stage in stages:
            stage(c, x, K)
            c.end_stage()
        gone = c.sem("out_stored")
        with nc.Block() as block:
            @block.sync
            def _(sp):
                sp.dma_start(out.rearrange("(t p) d -> p t d", p=P), x[:]).then_inc(gone, 16)
                sp.wait_ge(gone, 16)


def constants():
    import numpy as np
    f = np.float32
    K = {}
    K["ident"] = np.eye(P, dtype=f)
    K["identb"] = np.eye(P).astype(mybir.dt.np(BF16))
    q, k = np.arange(P)[:, None], np.arange(P)[None, :]
    bias = np.zeros((P, T), f)
    bias[:, P:] = np.where(k <= q, 0.0, -1e30)
    K["causal_bias"] = bias.astype(mybir.dt.np(BF16))
    K["future_mask"] = (q > k).astype(f)
    pick = np.zeros((P, 2 * P), f)
    pick[:, 96] = pick[:, P + 97] = 1
    K["row_pickers"] = pick.astype(mybir.dt.np(BF16))
    K["ones"] = np.ones((1, P), f)
    K["all_ones"] = np.ones((P, P), f)
    K["upto"] = (q <= k).astype(f)
    K["iota8"] = np.tile(np.arange(E1, dtype=f), (P, 1))
    K["iota32"] = np.tile(np.arange(E2, dtype=f), (P, 1))
    K["slot_base"] = np.tile(np.arange(E1, dtype=f) * CAP1 - 1, (P, 1))
    K["double_token"] = (2 * (np.arange(NT)[None, :] * P + np.arange(P)[:, None]) + BIG).astype(f)
    K["mask8"] = (np.arange(P)[:, None] // 8 == np.arange(16)[None, :]).astype(f)
    K["mask32"] = (np.arange(P)[:, None] // 32 == np.arange(4)[None, :]).astype(f)

    def rope(width, rows):
        inv = (f(1.0) / f(10000.0) ** (np.arange(0, width, 2, dtype=f) / f(width))).astype(f)
        ang = np.outer(np.arange(T, dtype=f), inv).astype(f)
        i = np.arange(P)
        cos, sin = np.cos(ang)[:, i % (width // 2)].T, np.sin(ang)[:, i % (width // 2)].T
        sin = sin * np.where(i % width < width // 2, -1, 1)[:, None]
        cos, sin = cos.astype(f), sin.astype(f)
        return np.tile(cos, (1, 2)), np.tile(sin, (1, 2))

    K["A_cos"], K["A_sin"] = rope(32, 32)
    K["C_cos"], K["C_sin"] = rope(8, P)
    return K


def layouts(I):
    import numpy as np
    f = np.float32
    I = {k: np.asarray(v) for k, v in I.items()}
    L = {"x": np.ascontiguousarray(I["x"].reshape(N, P))}

    def pad_cols(w, n):
        z = np.zeros((w.shape[0], n), f)
        z[:, :w.shape[1]] = w
        return z

    def values(w, bias, d):
        wz = np.zeros((w.shape[0], H, d + 1), f)
        wz[:, :, :d] = w.reshape(w.shape[0], H, d)
        row = np.zeros((1, H, d + 1), f)
        row[0, :, :d] = 0 if bias is None else bias.reshape(H, d)
        row[0, :, d] = 1
        return wz.reshape(w.shape[0], -1), row.reshape(1, -1)

    def halves_swapped(w, width):
        n = w.shape[1] // width
        return w.reshape(w.shape[0], n, 2, width // 2)[:, :, ::-1].reshape(w.shape[0], -1)

    p = "L0_attn_"
    L["A_kvd"], L["A_ku"], L["A_q"], L["A_wo"] = (I[p + k] for k in ("W_kv_down", "W_k_up", "W_q", "W_o"))
    L["A_vu"], L["A_vrow"] = values(I[p + "W_v_up"], None, 8)
    for k, w in (("A_qr", "W_q_rope"), ("A_kr", "W_k_rope")):
        L[k] = pad_cols(I[p + w], P)
        L[k + "s"] = pad_cols(halves_swapped(I[p + w], 32), P)

    def context_keys(w, bias):
        return np.concatenate([w, np.zeros((1, w.shape[1]), f) if bias is None else bias.reshape(1, -1)])

    def context_values(w, bias, d):
        wz, row = values(w, bias, d)
        z = np.zeros((P, wz.shape[1]), f)
        z[:CC], z[CC] = wz, row[0]
        return z

    p = "L0_xattn_"
    L["B_q"], L["B_k"], L["B_cq"], L["B_wp"] = (I[p + k] for k in ("Wq", "Wk", "Wcq", "Wp"))
    L["B_bq"], L["B_bk"], L["B_bcq"] = (I[p + k].reshape(P, 1) for k in ("bq", "bk", "bcq"))
    L["B_bp"] = I[p + "bp"].reshape(1, P)
    L["B_v"], L["B_vrow"] = values(I[p + "Wv"], I[p + "bv"], 8)
    L["B_wk"] = context_keys(I[p + "Wck"], I[p + "bck"])
    L["B_wv"] = context_values(I[p + "Wcv"], I[p + "bcv"], 8)
    L["ctxT"] = I["ctx_512"].transpose(0, 2, 1)
    L["ctx"] = I["ctx_512"]

    p = "L0_ffn_"
    qkv = I[p + "Wqkv"].reshape(P, H, 3, 8)
    L["C_q"], L["C_k"] = (qkv[:, :, k].reshape(P, P) for k in range(2))
    L["C_qs"], L["C_ks"] = halves_swapped(L["C_q"], 8), halves_swapped(L["C_k"], 8)
    L["C_v"], L["C_vrow"] = values(qkv[:, :, 2].reshape(P, P), None, 8)
    L["C_proj"], L["C_gate"] = I[p + "Wproj"], I[p + "Wgate"]
    for n, k in (("C_g1", "ln1_g"), ("C_s1", "ln1_b"), ("C_g2", "ln2_g"), ("C_s2", "ln2_b")):
        L[n] = I[p + k].reshape(P, 1)
    L["C_w1"] = I[p + "W1"]
    L["C_w2"] = I[p + "W2"].reshape(E1, F1 // P, P, P).transpose(0, 2, 1, 3)
    L["C_b1"] = I[p + "b1"].reshape(E1 * F1 // P, P).T
    L["C_b2"] = I[p + "b2"].reshape(1, E1 * P)

    L["D_q"], L["D_k"] = I["L1_attn_Wq"].T, I["L1_attn_Wk"].T
    L["D_v"] = pad_cols(I["L1_attn_Wv"].T, P + 1)
    L["D_vrow"] = np.zeros((1, P + 1), f)
    L["D_vrow"][0, P] = 1

    p = "L1_xattn_"
    for n, k in (("E_g1", "ln1_g"), ("E_s1", "ln1_b"), ("E_g2", "ln2_g"), ("E_s2", "ln2_b")):
        L[n] = I[p + k].reshape(1, P)
    for a in ("a1_", "a2_"):
        by_head = lambda w: w.transpose(1, 0, 2).reshape(w.shape[1], -1)
        L[a + "q"] = by_head(I[p + a + "wq"])
        wk, wv = by_head(I[p + a + "wk"]), by_head(I[p + a + "wv"])
        if a == "a1_":
            L["a1_k"] = wk
            L["a1_v"], L["a1_vrow"] = values(wv, None, 32)
        else:
            L["a2_wk"], L["a2_wv"] = context_keys(wk, None), context_values(wv, None, 32)
        L[a + "li1"] = I[p + a + "li1_w"].reshape(4, P, P).transpose(1, 0, 2)
        L[a + "b1"] = I[p + a + "li1_b"].reshape(1, P)
        for n, k in (("xg", "lnx_g"), ("xs", "lnx_b"), ("yg", "lny_g"), ("ys", "lny_b"), ("g3", "ln3_g"), ("s3", "ln3_b")):
            L[a + n] = I[p + a + k].reshape(-1, 1)
        L[a + "w2"] = I[p + a + "li2_w"]
        L[a + "b2"] = I[p + a + "li2_b"].reshape(4, P).T
        L[a + "w3"] = I[p + a + "li3_w"].reshape(4, P, P).transpose(1, 0, 2)
        L[a + "b3"] = I[p + a + "li3_b"].reshape(1, P)

    p = "L1_ffn_"
    L["F_r1"], L["F_r1s"] = I[p + "r1_w"][:, :P].T, I[p + "r1_w"][:, P:].T
    L["F_b1"], L["F_r2"] = I[p + "r1_b"].reshape(64, 1), I[p + "r2_w"].T
    L["F_up"] = I[p + "w_up"].transpose(0, 2, 1)
    L["F_down"] = I[p + "w_down"].transpose(0, 2, 1).reshape(E2, 2, P, P).transpose(0, 2, 1, 3)
    L["F_aup"], L["F_adown"] = I[p + "a_up"].transpose(0, 2, 1), I[p + "a_down"].transpose(0, 2, 1)
    return {k: np.ascontiguousarray(v) for k, v in L.items()}


def launch_arrays(inputs):
    arrays = layouts(inputs)
    arrays.update(constants())
    return {f"in_{k}": v for k, v in arrays.items()}


def make(nc, arrays, stages=STAGES):
    from concourse import mybir as _mybir
    ins = {k[3:]: nc.dram_tensor(k, v.shape, _mybir.dt.from_np(v.dtype), kind="ExternalInput").ap()
           for k, v in arrays.items()}
    out = nc.dram_tensor("out", (N, P), F32, kind="ExternalOutput").ap()
    build_program(nc, ins, out, stages)


def kernel(**inputs):
    import concourse.bacc as _bacc
    from concourse.bass_utils import run_bass_kernel_spmd as _run
    arrays = launch_arrays(inputs)
    nc = _bacc.Bacc("TRN2", target_bir_lowering=False, num_devices=1)
    make(nc, arrays)
    r = _run(nc, [arrays], core_ids=[0])
    return r.results[0]["out"].reshape(B, T, P)
```

```python
from contextlib import ExitStack

import concourse.bass as bass
from concourse import mybir

ALU = mybir.AluOpType
ACT = mybir.ActivationFunctionType
F32 = mybir.dt.float32
BF16 = mybir.dt.bfloat16
I32 = mybir.dt.int32
U32 = mybir.dt.uint32
AX_X = mybir.AxisListType.X

P = 128
B, T = 8, 256
NT = B * T // P
N = B * T
H = 16
QT_PER_B = T // P
BANK = 512
CH = N // BANK
CTX, CC = 1601, 64
NKT = -(-CTX // P)
CTX_PAD = NKT * P
EPS = 1e-5


class Core:

    def __init__(self, nc, ctx, ins):
        self.nc, self.ctx, self.ins, self.count = nc, ctx, ins, 0
        self.seen = nc.alloc_semaphore("seen")
        self.used = []

    def sem(self, name, by_gpsimd=False):
        self.count += 1
        sem = self.nc.alloc_semaphore(f"{name}_{self.count}")
        if not by_gpsimd:
            self.used.append(sem)
        return sem

    def end_stage(self):
        used, self.used = self.used, []
        with self.nc.Block() as block:
            @block.gpsimd
            def _(pool):
                for sem in used:
                    pool.sem_clear(sem)
        for sem in used:
            self.nc.release_semaphore(sem)

    def sbuf(self, ctx, name, shape, dt=F32):
        self.count += 1
        return ctx.enter_context(self.nc.sbuf_tensor(f"{name}_{self.count}", shape, dt))

    def psum(self, ctx, name, shape, dt=F32):
        self.count += 1
        return ctx.enter_context(self.nc.psum_tensor(f"{name}_{self.count}", shape, dt))


def load_stage(c, ctx, names):
    nc, held = c.nc, {}
    loaded = c.sem("weights_loaded")
    for name in names:
        src = c.ins[name.strip("*")]
        shape = list(src.shape)
        if name.startswith("*"):
            shape[0] = P
        held[name.strip("*")] = c.sbuf(ctx, name.strip("*"), shape, src.dtype)
    with nc.Block() as block:
        def load(eng, some):
            for name in some:
                src = c.ins[name.strip("*")]
                if name.startswith("*"):
                    src = src.partition_broadcast(P) if len(src.shape) == 1 else src.to_broadcast([P, src.shape[1]])
                eng.dma_start(held[name.strip("*")][:], src).then_inc(loaded, 16)

        @block.sync
        def _(sp):
            load(sp, names[0::2])
            sp.wait_ge(loaded, 16 * len(names))

        @block.scalar
        def _(act):
            load(act, names[1::2])
    return held


def transpose_tiles(c, groups, ident):
    nc = c.nc
    with ExitStack() as ctx:
        turned = c.psum(ctx, "turned", [P, 8, BANK])
        tiles_turned = c.sem("tiles_turned")
        copied = [c.sem("copied_by_scalar"), c.sem("copied_by_vector")]
        block = ctx.enter_context(nc.Block())

        @block.tensor
        def _(pe):
            for g, (srcs, dst, post) in enumerate(groups):
                if g >= 8:
                    pe.wait_ge(copied[g % 2], (g - 8) // 2 + 1)
                for k, src in enumerate(srcs):
                    rows, cols = src.shape
                    last = pe.transpose(turned[0:cols, g % 8, k * P:k * P + rows], src, ident[0:rows, 0:rows])
                last.then_inc(tiles_turned, 1)

        @block.scalar
        def _(act):
            for g, (srcs, dst, post) in enumerate(groups):
                if g % 2 == 0:
                    act.wait_ge(tiles_turned, g + 1)
                    src = turned[0:dst.shape[0], g % 8, 0:dst.shape[1]]
                    if post is None:
                        act.activation(dst, src, ACT.Copy).then_inc(copied[0], 1)
                    else:
                        act.activation(dst, src, ACT.Identity, scale=post[0], bias=post[1]).then_inc(copied[0], 1)

        @block.vector
        def _(dve):
            for g, (srcs, dst, post) in enumerate(groups):
                if g % 2 == 1:
                    dve.wait_ge(tiles_turned, g + 1)
                    src = turned[0:dst.shape[0], g % 8, 0:dst.shape[1]]
                    if post is None:
                        dve.tensor_copy(dst, src).then_inc(copied[1], 1)
                    else:
                        dve.tensor_scalar(dst, src, post[0], post[1], ALU.mult, ALU.add).then_inc(copied[1], 1)


def products(c, jobs):
    nc = c.nc

    def by_scalar(n):
        kind = jobs[n][2][0]
        return kind == "gelu" or (kind != "mul" and n % 2 == 0)

    def place(n):
        mine = by_scalar(n)
        return (0 if mine else 1), sum(by_scalar(m) == mine for m in range(n + 1))

    with ExitStack() as ctx:
        acc = c.psum(ctx, "acc", [P, 8, BANK])
        summed = c.sem("summed")
        taken = [c.sem("taken_by_scalar"), c.sem("taken_by_vector")]
        block = ctx.enter_context(nc.Block())

        @block.tensor
        def _(pe):
            for n, (dst, terms, post) in enumerate(jobs):
                if n >= 8:
                    engine, done = place(n - 8)
                    pe.wait_ge(taken[engine], done)
                rows, cols = terms[0][0].shape[-1], dst.free_size()
                for k, (lhsT, rhs) in enumerate(terms):
                    last = pe.matmul(acc[0:rows, n % 8, 0:cols], lhsT, rhs, start=k == 0, stop=k == len(terms) - 1)
                last.then_inc(summed, 1)

        @block.scalar
        def _(act):
            for n, (dst, terms, post) in enumerate(jobs):
                if by_scalar(n):
                    act.wait_ge(summed, n + 1)
                    src = acc[0:dst.shape[0], n % 8, 0:dst.free_size()]
                    if post[0] == "copy":
                        act.activation(dst, src, ACT.Copy).then_inc(taken[0], 1)
                    else:
                        act.activation(dst, src, ACT.Gelu if post[0] == "gelu" else ACT.Identity,
                                       bias=post[1]).then_inc(taken[0], 1)

        @block.vector
        def _(dve):
            for n, (dst, terms, post) in enumerate(jobs):
                if not by_scalar(n):
                    dve.wait_ge(summed, n + 1)
                    src = acc[0:dst.shape[0], n % 8, 0:dst.free_size()]
                    if post[0] == "copy":
                        dve.tensor_copy(dst, src).then_inc(taken[1], 1)
                    elif post[0] == "bias":
                        dve.tensor_scalar(dst, src, post[1], None, ALU.add).then_inc(taken[1], 1)
                    else:
                        dve.tensor_tensor(dst, src, post[1], ALU.mult).then_inc(taken[1], 1)


def add_pairs(c, pairs):
    with c.nc.Block() as block:
        @block.vector
        def _(dve):
            for dst, other in pairs:
                dve.tensor_tensor(dst, dst, other, ALU.add)


def sum_and_norm(c, tok_terms, summed, norm, residuals, gain=None, shift=None):
    nc = c.nc
    with ExitStack() as ctx:
        acc = c.psum(ctx, "acc", [P, 8, BANK])
        stats = c.sbuf(ctx, "stats", [P, NT, 6])
        moments = c.sbuf(ctx, "moments", [P, NT, 2])
        deviation = c.sbuf(ctx, "deviation", [P, NT])
        rstd = c.sbuf(ctx, "rstd", [P, NT])
        eps = c.sbuf(ctx, "eps", [P, 1])
        tile_product, tile_taken = c.sem("tile_product"), c.sem("tile_taken")
        variances, deviations = c.sem("variances"), c.sem("deviations")
        block = ctx.enter_context(nc.Block())

        @block.tensor
        def _(pe):
            if tok_terms is not None:
                for t in range(NT):
                    if t >= 8:
                        pe.wait_ge(tile_taken, t - 7)
                    terms = tok_terms(t)
                    for k, (lhsT, rhs) in enumerate(terms):
                        last = pe.matmul(acc[:, t % 8, 0:P], lhsT, rhs, start=k == 0, stop=k == len(terms) - 1)
                    last.then_inc(tile_product, 1)

        @block.vector
        def _(dve):
            dve.memset(eps[:], EPS)
            source = residuals[0] if tok_terms is None else summed
            if tok_terms is not None:
                for t in range(NT):
                    dve.wait_ge(tile_product, t + 1)
                    dve.tensor_tensor(summed[:, t, :], acc[:, t % 8, 0:P], residuals[0][:, t, :], ALU.add)\
                       .then_inc(tile_taken, 1)
                for other in residuals[1:]:
                    dve.drain()
                    dve.tensor_tensor(summed[:], summed[:], other[:], ALU.add)
                dve.drain()
            if norm is None:
                return
            for t in range(NT):
                dve.bn_stats(stats[:, t, :], source[:, t, :])
            dve.drain()
            for t in range(NT):
                last = dve.bn_aggr(moments[:, t, :], stats[:, t, :])
            last.then_inc(variances, 1)
            dve.wait_ge(deviations, 1)
            dve.reciprocal(rstd[:], deviation[:])
            dve.drain()
            for t in range(NT):
                dve.tensor_scalar(norm[:, t, :], source[:, t, :], moments[:, t, 0:1], rstd[:, t:t + 1],
                                  ALU.subtract, ALU.mult)
            if gain is not None:
                dve.drain()
                dve.tensor_tensor(norm[:], norm[:], gain[:].unsqueeze(1).to_broadcast([P, NT, P]), ALU.mult)
                dve.drain()
                dve.tensor_tensor(norm[:], norm[:], shift[:].unsqueeze(1).to_broadcast([P, NT, P]), ALU.add)

        @block.scalar
        def _(act):
            if norm is None:
                return
            act.wait_ge(variances, 1)
            act.activation(deviation[:], moments[:, :, 1], ACT.Sqrt, bias=eps[:, 0:1]).then_inc(deviations, 1)


def single_head_attention(c, QT, KT, V, O, consts, scale):
    nc = c.nc
    LOOPS = B // 2
    width = P + T
    blocks_of = [[(0, 0)], [(1, 0), (2, 1)]]
    with ExitStack() as ctx:
        S = c.psum(ctx, "scores", [P, width])
        PTp = c.psum(ctx, "probs_turned", [P, 2, BANK])
        Op = c.psum(ctx, "weighted", [P, 2, BANK])
        Qb = c.sbuf(ctx, "batch_queries", [P, 2, T])
        Pr = c.sbuf(ctx, "probs", [P, 2, width])
        PT = c.sbuf(ctx, "probsT", [P, 2, width])
        mx = c.sbuf(ctx, "row_max", [P, 2])
        rec = c.sbuf(ctx, "sum_reciprocal", [P, 2])
        queries_ready = c.sem("queries_ready")
        scores_ready = c.sem("scores_ready")
        shifted_ready = c.sem("shifted_ready")
        probs_ready = c.sem("probs_ready")
        turned_ready = c.sem("turned_ready")
        copied = c.sem("probsT_copied")
        weighted_ready = c.sem("weighted_ready")
        normed = c.sem("normed")
        block = ctx.enter_context(nc.Block())

        def over_bodies(eng, body):
            with eng.Fori(0, LOOPS - 1, 1) as it:
                body(it, False)
            body(LOOPS - 1, True)

        @block.gpsimd
        def _(pool):
            def queries(b, s):
                pool.wait_ge(scores_ready, b + 1)
                pool.sem_inc(c.seen, 1)
                pool.tensor_copy(Qb[:, s, :], QT[:, bass.ds(b * T, T)]).then_inc(queries_ready, 1)

            def body(it, last):
                for s in range(2):
                    if not (last and s == 1):
                        queries(it * 2 + s + 1, 1 - s)

            queries(0, 0)
            over_bodies(pool, body)

        @block.tensor
        def _(pe):
            def scores(b, s):
                pe.wait_ge(queries_ready, b + 1)
                pe.wait_ge(shifted_ready, b + 1)
                for qt in range(2):
                    out, keys = (S[:, 0:P], P) if qt == 0 else (S[:, P:width], T)
                    pe.matmul(out, Qb[:, s, qt * P:qt * P + P], KT[:, bass.ds(b * T, keys)], start=True, stop=False)
                    op = pe.matmul(out, consts["identb"][:], consts["causal_bias"][:, T - keys:T], start=False, stop=True)
                op.then_inc(scores_ready, 1)

            def body(it, last):
                for s in range(2):
                    b = it * 2 + s
                    if not (last and s == 1):
                        scores(b + 1, 1 - s)
                    pe.wait_ge(probs_ready, b + 1)
                    pe.wait_ge(copied, b + 1)
                    for k in range(3):
                        op = pe.transpose(PTp[:, s, k * P:k * P + P], Pr[:, s, k * P:k * P + P], consts["ident"][:])
                    op.then_inc(turned_ready, 1)
                    pe.wait_ge(copied, b + 3)
                    pe.wait_ge(normed, b + 1)
                    for qt, blocks in enumerate(blocks_of):
                        at = qt * (P + 1)
                        for k, kt in blocks:
                            op = pe.matmul(Op[:, s, at:at + P + 1], PT[:, s, k * P:k * P + P],
                                           V[:, bass.ds(b * QT_PER_B + kt, 1), :], start=(k, kt) == blocks[0],
                                           stop=(k, kt) == blocks[-1])
                    op.then_inc(weighted_ready, 1)

            pe.sem_inc(scores_ready, 2)
            pe.sem_inc(weighted_ready, 2)
            scores(0, 0)
            over_bodies(pe, body)

        @block.vector
        def _(dve):
            def shift(b, s):
                dve.drain()
                dve.wait_ge(weighted_ready, b + 1)
                dve.wait_ge(scores_ready, b + 3)
                for qt, cols in enumerate((slice(0, P), slice(P, width))):
                    dve.tensor_reduce(mx[:, qt:qt + 1], S[:, cols], AX_X, ALU.max)
                dve.drain()
                for qt, cols in enumerate((slice(0, P), slice(P, width))):
                    op = dve.tensor_scalar(Pr[:, s, cols], S[:, cols], mx[:, qt:qt + 1], None, ALU.subtract)
                op.then_inc(shifted_ready, 1)

            def norm(b, s):
                out = Op[:, s, 0:2 * (P + 1)].rearrange("p (q e) -> p q e", q=2)
                dve.drain()
                dve.wait_ge(weighted_ready, b + 3)
                dve.reciprocal(rec[:], out[:, :, P])
                dve.drain()
                for qt in range(2):
                    op = dve.tensor_scalar(O[:, bass.ds(b * QT_PER_B + qt, 1), :], out[:, qt:qt + 1, 0:P], rec[:, qt:qt + 1],
                                           None, ALU.mult)
                op.then_inc(normed, 1)

            def body(it, last):
                for s in range(2):
                    if not (last and s == 1):
                        shift(it * 2 + s + 1, 1 - s)
                    norm(it * 2 + s, s)

            dve.sem_inc(shifted_ready, 1)
            dve.sem_inc(normed, 2)
            shift(0, 0)
            over_bodies(dve, body)

        @block.scalar
        def _(act):
            def body(it, last):
                for s in range(2):
                    b = it * 2 + s
                    act.wait_ge(shifted_ready, b + 2)
                    act.activation(Pr[:, s, :], Pr[:, s, :], ACT.Exp, scale=scale).then_inc(probs_ready, 1)
                    act.wait_ge(turned_ready, b + 1)
                    act.wait_ge(weighted_ready, b + 1)
                    act.activation(PT[:, s, :], PTp[:, s, 0:width], ACT.Copy).then_inc(copied, 1)

            act.sem_inc(copied, 2)
            over_bodies(act, body)


LEVELS = 3


def product_terms(d):
    parts = [(0, 0), (0, 1), (1, 0), (1, 1), (0, 2), (2, 0)]
    per_pack = 96 // d
    return [(t // per_pack, t % per_pack * d, *parts[t]) for t in range(len(parts))]


def split_features(c, jobs):
    nc = c.nc
    SLOTS, W = 4, N // 2
    pieces = [(src[:, k:k + W], parts[:, :, k:k + W]) for src, parts in jobs for k in range(0, N, W)]
    with ExitStack() as ctx:
        level = c.sbuf(ctx, "levels", [P, SLOTS, LEVELS, W], BF16)
        rest = c.sbuf(ctx, "rests", [P, SLOTS, W])
        high, middle, low = c.sem("high_ready"), c.sem("middle_ready"), c.sem("low_ready")
        rest_ready = c.sem("rest_ready")
        stored = [c.sem(f"parts_stored{s}") for s in range(SLOTS)]
        block = ctx.enter_context(nc.Block())

        @block.scalar
        def _(act):
            def high_part(n):
                if n >= SLOTS:
                    act.wait_ge(stored[n % SLOTS], n // SLOTS * 16 * LEVELS)
                act.activation(level[:, n % SLOTS, 0, :], pieces[n][0], ACT.Copy).then_inc(high, 1)

            high_part(0)
            for n in range(len(pieces)):
                if n + 1 < len(pieces):
                    high_part(n + 1)
                act.wait_ge(rest_ready, n + 1)
                act.activation(level[:, n % SLOTS, 1, :], rest[:, n % SLOTS, :], ACT.Copy).then_inc(middle, 1)

        @block.vector
        def _(dve):
            def rest_part(n):
                dve.wait_ge(high, n + 1)
                dve.tensor_tensor(rest[:, n % SLOTS, :], pieces[n][0], level[:, n % SLOTS, 0, :], ALU.subtract)\
                   .then_inc(rest_ready, 1)

            rest_part(0)
            for n in range(len(pieces)):
                if n + 1 < len(pieces):
                    rest_part(n + 1)
                dve.drain()
                dve.wait_ge(middle, n + 1)
                dve.tensor_tensor(level[:, n % SLOTS, 2, :], rest[:, n % SLOTS, :], level[:, n % SLOTS, 1, :], ALU.subtract)\
                   .then_inc(low, 1)

        @block.sync
        def _(sp):
            for n, (src, parts) in enumerate(pieces):
                for l, ready in enumerate((high, middle, low)):
                    sp.wait_ge(ready, n + 1)
                    sp.dma_start(parts[l], level[:, n % SLOTS, l, :]).then_inc(stored[n % SLOTS], 16)
            for s in range(min(SLOTS, len(pieces))):
                sp.wait_ge(stored[s], len(range(s, len(pieces), SLOTS)) * 16 * LEVELS)


def feature_groups(features, parts):
    return [(features[:, g, :], parts[:, g * P:(g + 1) * P, :]) for g in range(features.shape[1])]


def self_attention(c, query_parts, key_parts, V, O, consts, d, kind, scale, shared=None):
    nc = c.nc
    causal = kind == "causal"
    HQ, HN = 4, H * (d + 1)
    QPB = H // HQ
    PER_BODY = 2 * QPB
    LOOPS = B // 2
    terms = product_terms(d)
    NP = terms[-1][0] + 1
    shared_terms = product_terms(shared[2]) if shared else []
    shared_packs = shared_terms[-1][0] + 1 if shared else 0
    ROWS = 96
    w0 = P if causal else T
    width = w0 + T
    made = d + 1 if causal else d
    blocks_of = [[(0, 0)], [(1, 0), (2, 1)]] if causal else [[(0, 0), (1, 1)], [(2, 1)]]
    with ExitStack() as ctx:
        S = c.psum(ctx, "scores", [P, HQ, BANK])
        PTp = c.psum(ctx, "probs_turned", [P, 2, BANK])
        Op = c.psum(ctx, "weighted", [P, 2, BANK])
        QP = c.sbuf(ctx, "query_packs", [P, 2, NP, H, T], BF16)
        KP = c.sbuf(ctx, "key_packs", [P, 2, NP, H, T], BF16)
        if shared:
            QS = c.sbuf(ctx, "shared_query_packs", [P, 2, shared_packs, T], BF16)
            KS = c.sbuf(ctx, "shared_key_packs", [P, 2, shared_packs, T], BF16)
        VB = c.sbuf(ctx, "batch_values", [P, 2, QT_PER_B, HN])
        Pr = c.sbuf(ctx, "probs", [P, 2, HQ, width])
        Pm = c.sbuf(ctx, "masked_probs", [P, 2, HQ, 2, P]) if not causal else None
        PT = c.sbuf(ctx, "probsT", [P, 2, 3 * P])
        OT = c.sbuf(ctx, "weightedT", [P, 2, T])
        mx = c.sbuf(ctx, "row_max", [P, HQ, 2])
        sums = c.sbuf(ctx, "prob_sums", [P, HQ, 2])
        rec = c.sbuf(ctx, "sum_reciprocal", [P, 2, 2, 2])
        packs_cleared = c.sem("packs_cleared")
        packs_loaded = [c.sem("packs_loaded0"), c.sem("packs_loaded1")]
        values_ready = c.sem("batch_values_ready")
        scores_ready = c.sem("scores_ready")
        shifted_ready = c.sem("shifted_ready")
        probs_ready = c.sem("probs_ready")
        masked = c.sem("probs_masked")
        turned_ready = c.sem("turned_ready")
        copied = c.sem("probsT_copied")
        weighed = c.sem("weighed")
        lifted = c.sem("weightedT_copied")
        back_ready = c.sem("turned_back")
        normed = c.sem("normed")
        block = ctx.enter_context(nc.Block())

        def over_bodies(eng, body):
            with eng.Fori(0, LOOPS - 1, 1) as it:
                body(it, False)
            body(LOOPS - 1, True)

        @block.sync
        def _(sp):
            def load(b, slot):
                for packs, parts, which in ((QP, query_parts, 3), (KP, key_parts, 2)):
                    for term in terms:
                        rows = parts[term[which], :, bass.ds(b * T, T)].rearrange("(h f) n -> f h n", h=H)
                        sp.dma_start(packs[term[1]:term[1] + d, slot, term[0], :, :], rows)\
                          .then_inc(packs_loaded[slot], 16)
                if shared:
                    for packs, parts, which in ((QS, shared[0], 3), (KS, shared[1], 2)):
                        for term in shared_terms:
                            sp.dma_start(packs[term[1]:term[1] + shared[2], slot, term[0], :],
                                         parts[term[which], 0:shared[2], bass.ds(b * T, T)]).then_inc(packs_loaded[slot], 16)

            sp.wait_ge(packs_cleared, 2)
            for slot in range(2):
                load(slot, slot)

            def body(it, last):
                if not last:
                    for slot in range(2):
                        sp.wait_ge(scores_ready, it * PER_BODY + (slot + 1) * QPB)
                        sp.sem_inc(c.seen, 1)
                        load(it * 2 + slot + 2, slot)

            over_bodies(sp, body)

        @block.gpsimd
        def _(pool):
            def copy_values(b, slot):
                pool.tensor_copy(VB[:, slot, :, :], V[:, bass.ds(b * QT_PER_B, QT_PER_B), :]).then_inc(values_ready, 1)

            def mask(q, slot):
                for half in range(2):
                    pool.wait_ge(probs_ready, q * 2 + half + 1)
                    pool.sem_inc(c.seen, 1)
                    for qt in range(2):
                        at = 0 if qt == 0 else T + P
                        src = Pr[:, slot, 2 * half:2 * half + 2, at:at + P]
                        op = pool.tensor_tensor(Pm[:, slot, 2 * half:2 * half + 2, qt, :], src,
                                                consts["future_mask"][:].unsqueeze(1).to_broadcast([P, 2, P]), ALU.mult)
                    op.then_inc(masked, 1)

            if terms[-1][1] + d < ROWS:
                pool.memset(QP[:], 0.0)
                pool.drain()
            pool.sem_inc(packs_cleared, 1)
            copy_values(0, 0)
            if not causal:
                mask(0, 0)

            def body(it, last):
                for i in range(PER_BODY):
                    if i % QPB == 1 and not (last and i > QPB):
                        pool.wait_ge(weighed, (it * PER_BODY + i) * HQ)
                        pool.sem_inc(c.seen, 1)
                        copy_values(it * 2 + i // QPB + 1, (i // QPB + 1) % 2)
                    if not causal and not (last and i == PER_BODY - 1):
                        mask(it * PER_BODY + i + 1, (i + 1) % 2)

            over_bodies(pool, body)

        @block.tensor
        def _(pe):
            def scores(q, i, body_of_it):
                slot = i // QPB
                if i % QPB == 0:
                    pe.wait_ge(packs_loaded[slot], (body_of_it + 1) * (32 * (len(terms) + len(shared_terms))))
                pe.wait_ge(shifted_ready, q + 1)
                for j in range(HQ):
                    h = i % QPB * HQ + j
                    for qt in range(2):
                        out = S[:, j, 0:w0] if qt == 0 else S[:, j, w0:width]
                        keys = w0 if qt == 0 else T
                        for pack in range(NP):
                            op = pe.matmul(out, QP[0:ROWS, slot, pack, h, qt * P:qt * P + P], KP[0:ROWS, slot, pack, h, 0:keys],
                                           start=pack == 0, stop=not causal and not shared and pack == NP - 1)
                        for pack in range(shared_packs):
                            op = pe.matmul(out, QS[0:ROWS, slot, pack, qt * P:qt * P + P], KS[0:ROWS, slot, pack, 0:keys],
                                           start=False, stop=not causal and pack == shared_packs - 1)
                        if causal:
                            op = pe.matmul(out, consts["identb"][:], consts["causal_bias"][:, T - keys:T],
                                           start=False, stop=True)
                op.then_inc(scores_ready, 1)

            def turn(q, i, h):
                if h % 2 == 0:
                    pe.wait_ge(probs_ready if causal else masked, q * 2 + h // 2 + 1)
                pe.wait_ge(copied, q * HQ + h + 1)
                if causal:
                    sources = [Pr[:, i % 2, h, k * P:k * P + P] for k in range(3)]
                else:
                    sources = [Pm[:, i % 2, h, 0, :], Pr[:, i % 2, h, P:T], Pm[:, i % 2, h, 1, :]]
                for k, src in enumerate(sources):
                    op = pe.transpose(PTp[:, h % 2, k * P:k * P + P], src, consts["ident"][:])
                op.then_inc(turned_ready, 1)

            def weigh(q, i, h, b):
                pe.wait_ge(copied, q * HQ + h + 3)
                if h == 0:
                    pe.wait_ge(normed, q + 1)
                    if i % QPB == 0:
                        pe.wait_ge(values_ready, b + 1)
                at = (i % QPB * HQ + h) * (d + 1)
                for qt, blocks in enumerate(blocks_of):
                    for k, kt in blocks:
                        op = pe.matmul(Op[0:made, h % 2, qt * P:qt * P + P], VB[:, i // QPB, kt, at:at + made],
                                       PT[:, h % 2, k * P:k * P + P], start=(k, kt) == blocks[0], stop=(k, kt) == blocks[-1])
                op.then_inc(weighed, 1)

            def turn_back(q, h):
                pe.wait_ge(lifted, q * HQ + h + 1)
                pe.sem_inc(c.seen, 1)
                for qt in range(2):
                    at = T + (h // 2 * 2 + qt) * made
                    op = pe.transpose(Op[:, h % 2, at:at + made], OT[0:made, h % 2, qt * P:qt * P + P],
                                      consts["ident"][0:made, 0:made])
                op.then_inc(back_ready, 1)

            def body(it, last):
                for i in range(PER_BODY):
                    q = it * PER_BODY + i
                    turn(q, i, 0)
                    for h in range(HQ):
                        if h + 1 < HQ:
                            turn(q, i, h + 1)
                        weigh(q, i, h, it * 2 + i // QPB)
                        if h >= 1:
                            turn_back(q, h - 1)
                    if i + 2 < PER_BODY:
                        scores(q + 2, i + 2, it)
                    elif not last:
                        scores(q + 2, i + 2 - PER_BODY, it + 1)
                    turn_back(q, HQ - 1)

            pe.sem_inc(turned_ready, 2 * HQ)
            pe.sem_inc(weighed, 2)
            scores(0, 0, 0)
            scores(1, 1, 0)
            over_bodies(pe, body)

        @block.vector
        def _(dve):
            def shift(q, slot):
                dve.wait_ge(turned_ready, (q + 1) * HQ)
                dve.wait_ge(scores_ready, q + 1)
                if causal:
                    dve.tensor_reduce(mx[:, :, 0], S[:, :, 0:P], AX_X, ALU.max)
                    dve.tensor_reduce(mx[:, :, 1], S[:, :, P:3 * P], AX_X, ALU.max)
                    dve.drain()
                    dve.tensor_tensor(Pr[:, slot, :, 0:P], S[:, :, 0:P], mx[:, :, 0:1].to_broadcast([P, HQ, P]), ALU.subtract)
                    op = dve.tensor_tensor(Pr[:, slot, :, P:3 * P], S[:, :, P:3 * P],
                                           mx[:, :, 1:2].to_broadcast([P, HQ, T]), ALU.subtract)
                else:
                    src = S[:].rearrange("p h (q k) -> p h q k", q=2)
                    dve.tensor_reduce(mx[:], src, AX_X, ALU.max)
                    dve.drain()
                    op = dve.tensor_tensor(Pr[:, slot, :, :].rearrange("p h (q k) -> p h q k", q=2), src,
                                           mx[:].unsqueeze(3).to_broadcast([P, HQ, 2, T]), ALU.subtract)
                op.then_inc(shifted_ready, 1)

            def norm(it, i):
                q = it * PER_BODY + i
                b, h0 = it * 2 + i // QPB, i % QPB * HQ
                if not causal:
                    dve.wait_ge(probs_ready, (q + 1) * 2)
                    dve.tensor_reduce(sums[:], Pr[:, i % 2, :, :].rearrange("p h (q k) -> p h q k", q=2), AX_X, ALU.add)
                    dve.drain()
                    dve.reciprocal(rec[:], sums[:].rearrange("p (a k) q -> p k a q", k=2))
                dve.drain()
                dve.wait_ge(back_ready, (q + 1) * HQ)
                out = Op[:, :, T:T + 4 * made].rearrange("p k (a q e) -> p k a q e", a=2, q=2)
                if causal:
                    dve.reciprocal(rec[:], out[:, :, :, :, d])
                    dve.drain()
                for qt in range(2):
                    dst = O[:, bass.ds(b * QT_PER_B + qt, 1), h0 * d:(h0 + HQ) * d]
                    op = dve.tensor_tensor(dst.rearrange("p o (a k e) -> p k (o a) e", a=2, k=2), out[:, :, :, qt, 0:d],
                                           rec[:, :, :, qt].unsqueeze(3).to_broadcast([P, 2, 2, d]), ALU.mult)
                op.then_inc(normed, 1)
                dve.drain()

            if terms[-1][1] + d < ROWS:
                dve.memset(KP[:], 0.0)
                dve.drain()
            dve.sem_inc(packs_cleared, 1)
            dve.sem_inc(shifted_ready, 1)
            dve.sem_inc(normed, 1)
            shift(0, 0)

            def body(it, last):
                for i in range(PER_BODY):
                    if not (last and i == PER_BODY - 1):
                        shift(it * PER_BODY + i + 1, (i + 1) % 2)
                    norm(it, i)

            over_bodies(dve, body)

        @block.scalar
        def _(act):
            def exp(q, slot, half):
                act.wait_ge(shifted_ready, q + 2)
                probs = Pr[:, slot, 2 * half:2 * half + 2, :]
                act.activation(probs, probs, ACT.Exp, scale=scale).then_inc(probs_ready, 1)

            def copy(q, h):
                n = q * HQ + h
                act.wait_ge(turned_ready, n + 1 + 2 * HQ)
                act.wait_ge(weighed, n + 1)
                act.activation(PT[:, h % 2, :], PTp[:, h % 2, 0:3 * P], ACT.Copy).then_inc(copied, 1)

            def lift(q, h):
                act.wait_ge(weighed, q * HQ + h + 3)
                act.activation(OT[0:made, h % 2, :], Op[0:made, h % 2, 0:T], ACT.Copy).then_inc(lifted, 1)

            act.sem_inc(copied, 2)
            exp(0, 0, 0)
            exp(0, 0, 1)

            def body(it, last):
                for i in range(PER_BODY):
                    q = it * PER_BODY + i
                    copy(q, 0)
                    for h in range(1, HQ):
                        copy(q, h)
                        lift(q, h - 1)
                    more = not (last and i == PER_BODY - 1)
                    lift(q, HQ - 1)
                    if more:
                        for half in range(2):
                            exp(q + 1, (i + 1) % 2, half)

            over_bodies(act, body)


def cross_attention(c, query_parts, O, wk, wv, turned_ctx, plain_ctx, consts, d, add_to, scale):
    nc = c.nc
    PG = P // d
    GB = H // PG
    BPB = 2
    HB, GBODY, LOOPS = H * BPB, GB * BPB, B // BPB
    HEADS, GROUPS = B * H, B * GB
    FULL = CTX // P
    REST = CTX - FULL * P
    assert NKT == FULL + 1
    SLOTS = 4
    terms = product_terms(d)
    NP = terms[-1][0] + 1
    ROWS, SHIFT = 96, 96
    AHEAD_K = 1 if GB == 1 else 2
    units = [(k, min(2, NKT - k)) for k in range(0, NKT, 2)]
    NU = len(units)
    kcw = CTX_PAD // 4
    mcw = -(-CTX // 4)
    chunks = [(k, min(mcw, CTX - k)) for k in range(0, CTX, mcw)]
    NC = len(chunks)
    max_of_unit = [range(u, u + 1) for u in range(NU - 1)] + [range(NU - 1, 2 * NC)]
    tiles_before = (0, 4, 6, 8, 10, 12, NKT, NKT)
    assert len(tiles_before) == NU + 1
    weigh_of_unit = [range(tiles_before[u], tiles_before[u + 1]) for u in range(NU)]

    side = {}
    for s in range(HB):
        side[s, 1] = ("shift", None, None)
    for j in range(GBODY):
        if GB == 1:
            places = [(j * H + 2, u) for u in (2, 3, 4, 5)]
        else:
            places = [(j * PG, 3), (j * PG + 1, 3), (j * PG + 2, 3), (j * PG + 2, 5)]
        jobs = [("key", j + AHEAD_K, k) for k in range(4)]
        for at, job in zip(places, jobs):
            side[at] = job
    context_step = 0 if GB == 1 else 7

    def body_jobs(last):
        left = {}
        for (s, u), (kind, g, k) in sorted(side.items()):
            if last and (kind == "shift" and s + 2 >= HB or kind != "shift" and g >= GBODY):
                continue
            left[s, u] = (len(left), kind, g, k)
        return left

    JB = len(body_jobs(False))
    first_jobs = [("key", 0, k) for k in range(4)]
    second_jobs = [("key", 1, k) for k in range(4)] if AHEAD_K == 2 else []
    J1 = len(first_jobs)
    J0 = J1 + len(second_jobs) + 2

    def over_bodies(eng, body):
        with eng.Fori(0, LOOPS - 1, 1) as it:
            body(it, False)
        body(LOOPS - 1, True)

    with ExitStack() as ctx:
        ST = c.psum(ctx, "scoresT", [P, 3, BANK])
        SM = c.psum(ctx, "scores_for_max", [P, 2, BANK])
        Side = c.psum(ctx, "side", [P, BANK])
        Op = c.psum(ctx, "weighted", [P, 2, BANK])
        ctxK = c.sbuf(ctx, "context_for_keys", [P, CTX_PAD])
        VC = c.sbuf(ctx, "plain_context", [P, 2, NKT, CC + 1])
        level = c.sbuf(ctx, "key_parts", [P, 2, LEVELS, CTX_PAD], BF16)
        rest = c.sbuf(ctx, "key_rests", [P, CTX_PAD])
        KP = c.sbuf(ctx, "key_packs", [P, SLOTS, NP, CTX_PAD], BF16)
        QP = c.sbuf(ctx, "query_packs", [P, 8, NP, T], BF16)
        PT = c.sbuf(ctx, "probsT", [P, 2, NKT, T])
        chunk_max = c.sbuf(ctx, "chunk_max", [P, 2, NC])
        neg_max = c.sbuf(ctx, "neg_max", [P, 2])
        high_max = c.sbuf(ctx, "neg_max_high", [P, 2], BF16)
        low_max = c.sbuf(ctx, "neg_max_rest", [P, 2])
        diag = c.sbuf(ctx, "neg_max_diagonals", [P, 2, 2, P], BF16)
        OT = c.sbuf(ctx, "weightedT", [P, T])
        rec = c.sbuf(ctx, "sum_reciprocal", [P, 2])
        context_padded, plain_padded = c.sem("context_padded"), c.sem("plain_context_padded")
        packs_cleared, ones_ready = c.sem("packs_cleared"), c.sem("ones_rows_ready")
        context_for_keys = c.sem("context_for_keys_loaded")
        plain_loaded = [c.sem("plain_context_loaded0"), c.sem("plain_context_loaded1")]
        key_packs = [c.sem(f"key_pack_loaded{s}") for s in range(SLOTS)]
        query_packs = [c.sem("query_packs_loaded0"), c.sem("query_packs_loaded1")]
        side_product = c.sem("side_product")
        side_taken = c.sem("side_taken")
        high_ready = c.sem("keys_high_ready")
        chunk_split = c.sem("keys_chunk_split")
        max_scores = c.sem("max_scores")
        chunk_reduced = c.sem("chunk_reduced")
        diagonal_ready = c.sem("diagonal_ready")
        unit_scored = c.sem("unit_scored")
        unit_exp = c.sem("unit_exp")
        weighted = c.sem("weighted")
        weighted_copied, turned = c.sem("weighted_copied"), c.sem("turned")
        normed = c.sem("normed")
        block = ctx.enter_context(nc.Block())

        @block.gpsimd
        def _(pool):
            for buffer in (ctxK[CC:P, :], ctxK[0:CC, CTX:CTX_PAD]):
                pool.memset(buffer, 0.0)
                pool.drain()
            pool.memset(ctxK[CC:CC + 1, 0:CTX], 1.0).then_inc(context_padded, 1)
            pool.drain()
            if terms[-1][1] + d < ROWS:
                pool.memset(QP[:], 0.0)
                pool.drain()
            pool.sem_inc(packs_cleared, 1)
            pool.memset(VC[:, :, FULL, :], 0.0)
            pool.drain()
            pool.memset(VC[:, :, 0:FULL, CC], 1.0)
            pool.drain()
            pool.memset(VC[0:REST, :, FULL, CC], 1.0).then_inc(plain_padded, 1)
            pool.drain()

            def split(number, slot, k):
                cols = slice(k * kcw, (k + 1) * kcw)
                pool.wait_ge(side_taken, number + 2)
                pool.sem_inc(c.seen, 1)
                pool.tensor_copy(level[:, slot, 1, cols], rest[:, cols])
                pool.drain()
                pool.tensor_tensor(level[:, slot, 2, cols], rest[:, cols], level[:, slot, 1, cols], ALU.subtract)\
                    .then_inc(chunk_split, 1)
                pool.drain()

            for number, (kind, g, k) in enumerate(first_jobs + second_jobs):
                if kind == "key":
                    split(number, g % 2, k)

            def body(it, last):
                for number, kind, g, k in body_jobs(last).values():
                    if kind == "key":
                        split(J0 + it * JB + number, g % 2, k)

            over_bodies(pool, body)

        @block.sync
        def _(sp):
            def load_context(b):
                sp.dma_start(ctxK[0:CC, 0:CTX], turned_ctx[bass.ds(b, 1), :, :].rearrange("o c k -> (o c) k"))\
                  .then_inc(context_for_keys, 16)

            def load_plain_context(b, slot):
                sp.dma_start(VC[:, slot, 0:FULL, 0:CC],
                             plain_ctx[bass.ds(b, 1), 0:FULL * P, :].rearrange("o (t p) c -> p (o t) c", p=P))\
                  .then_inc(plain_loaded[slot], 16)
                sp.dma_start(VC[0:REST, slot, FULL, 0:CC],
                             plain_ctx[bass.ds(b, 1), FULL * P:CTX, :].rearrange("o k c -> (o k) c"))\
                  .then_inc(plain_loaded[slot], 16)

            def load_head(it, i):
                b, h = it * BPB + i // H, i % H
                if i % 4 == 0:
                    for pack, row, _, l in terms:
                        rows = query_parts[l, h * d:(h + 4) * d, bass.ds(b * T, T)].rearrange("(h f) n -> f h n", h=4)
                        sp.dma_start(QP[row:row + d, i % 8:i % 8 + 4, pack, :], rows)\
                          .then_inc(query_packs[i // 4 % 2], 16)
                sp.wait_ge(chunk_split, (it * GBODY + i // PG + 1) * 4)
                at = h % PG * d
                for pack, row, l, _ in terms:
                    sp.dma_start(KP[row:row + d, i % SLOTS, pack, :], level[at:at + d, i // PG % 2, l, :])\
                      .then_inc(key_packs[i % SLOTS], 16)

            load_context(0)
            sp.wait_ge(packs_cleared, 2)
            for i in range(SLOTS):
                load_head(0, i)
            sp.wait_ge(plain_padded, 1)
            load_plain_context(0, 0)

            def body(it, last):
                for i in range(HB):
                    sp.wait_ge(unit_scored, (it * HB + i + 1) * NU)
                    sp.sem_inc(c.seen, 1)
                    b, s = it * BPB + i // H, i % H
                    next_batch = not (last and i // H == BPB - 1)
                    if s == context_step and next_batch:
                        sp.wait_ge(side_product, J0 + it * JB + sum(step < i for step, _ in body_jobs(last)))
                        load_context(b + 1)
                    if s == 4 and next_batch:
                        load_plain_context(b + 1, (i // H + 1) % 2)
                    m = i + SLOTS
                    if m < HB:
                        load_head(it, m)
                    elif not last:
                        load_head(it + 1, m - HB)

            over_bodies(sp, body)

        @block.tensor
        def _(pe):
            def side_job(number, head, kind, g, k, b):
                if kind == "shift":
                    pe.wait_ge(diagonal_ready, head + 1)
                pe.wait_ge(side_taken, number + 1)
                if kind == "shift":
                    for part in range(2):
                        op = pe.matmul(Side[:, 0:T], consts["row_pickers"][:, part * P:part * P + P],
                                       diag[:, part, :, :].rearrange("p q k -> p (q k)"), start=part == 0, stop=part == 1)
                    op.then_inc(side_product, 1)
                    return
                gi = g % GB
                if gi == 0 and k == 0:
                    pe.wait_ge(context_for_keys, (b + 1) * 16)
                pe.matmul(Side[:, 0:kcw], wk[0:CC + 1, gi * P:gi * P + P], ctxK[0:CC + 1, k * kcw:(k + 1) * kcw],
                          start=True, stop=True).then_inc(side_product, 1)

            def max_part(n, i, n_body, j):
                qt, k = j // NC, j % NC
                if j == 0:
                    pe.wait_ge(key_packs[i % SLOTS], (n_body * (HB // SLOTS) + i // SLOTS + 1) * (16 * len(terms)))
                    if i % 4 == 0:
                        pe.wait_ge(query_packs[i // 4 % 2], (n_body * (HB // 8) + i // 8 + 1) * (16 * len(terms)))
                pe.wait_ge(chunk_reduced, n * 2 * NC + j + 1)
                at, size = chunks[k]
                pe.matmul(SM[:, j % 2, 0:size], QP[0:ROWS, i % 8, 0, qt * P:qt * P + P], KP[0:ROWS, i % SLOTS, 0, at:at + size],
                          start=True, stop=True).then_inc(max_scores, 1)

            def unit(n, i, u, shift_number):
                if u == 0:
                    pe.wait_ge(side_taken, shift_number + 2)
                before = n * NU + u - 3 if u >= 3 else n * NU - NU + (5, 6, 4)[u] if i % 2 == 0 else n * NU - NU + 4 + u
                pe.wait_ge(unit_exp, before + NU + 1)
                kt0, size = units[u]
                bank = (u + i % 2) % 3
                for k in range(size):
                    for pack in range(NP):
                        rows = SHIFT + 2 if pack == 0 else ROWS
                        op = pe.matmul(ST[:, bank, k * T:k * T + T], KP[0:rows, i % SLOTS, pack, (kt0 + k) * P:(kt0 + k + 1) * P],
                                       QP[0:rows, i % 8, pack, :], start=pack == 0, stop=pack == NP - 1)
                op.then_inc(unit_scored, 1)

            def weigh(n, i, tiles, n_body):
                slot = i // H % 2
                for kt in tiles:
                    if kt == 0 and i % H == 0:
                        pe.wait_ge(plain_loaded[slot], (n_body + 1) * 32)
                    if kt == 0:
                        pe.wait_ge(normed, n + 1)
                    if kt % 2 == 0:
                        pe.wait_ge(unit_exp, n * NU + kt // 2 + 1 + NU)
                    op = pe.matmul(Op[0:CC + 1, i % 2, 0:T], VC[:, slot, kt, :],
                                   PT[:, i % 2, kt, :], start=kt == 0, stop=kt == NKT - 1)
                    if kt == NKT - 1:
                        op.then_inc(weighted, 1)

            def turn(n, i):
                pe.wait_ge(weighted_copied, n + 1)
                pe.sem_inc(c.seen, 1)
                for qt in range(2):
                    at = T + qt * (d + 1)
                    op = pe.matmul(Op[:, i % 2, at:at + d + 1], OT[0:CC + 1, qt * P:qt * P + P],
                                   wv[0:CC + 1, i % H * (d + 1):(i % H + 1) * (d + 1)], start=True, stop=True)
                op.then_inc(turned, 1)

            pe.sem_inc(weighted, 2)
            pe.wait_ge(context_padded, 1)
            for number, (kind, g, k) in enumerate(first_jobs):
                side_job(number, None, kind, g, k, 0)
            for head in range(2):
                for j in range(2 * NC):
                    max_part(head, head, 0, j)
                    if head == 0 and j < len(second_jobs):
                        side_job(J1 + j, None, *second_jobs[j], 0)
                side_job(J0 - 2 + head, head, "shift", None, None, None)
            pe.wait_ge(ones_ready, 1)
            for u in range(NU):
                unit(0, 0, u, J0 - 2)
            for j in range(2 * NC):
                max_part(2, 2, 0, j)

            def body(it, last):
                jobs = body_jobs(last)
                base = J0 + it * JB
                for i in range(HB):
                    n = it * HB + i
                    for u in range(NU):
                        if not (last and i + 1 >= HB):
                            number = base + jobs[i - 1, 1][0] if i else base - 1
                            unit(n + 1, (i + 1) % HB, u, number)
                        for j in max_of_unit[u]:
                            if i + 3 < HB:
                                max_part(n + 3, i + 3, it, j)
                            elif not last:
                                max_part(n + 3, i + 3 - HB, it + 1, j)
                        if (i, u) in jobs:
                            number, kind, g, k = jobs[i, u]
                            b = None if kind == "shift" else it * BPB + g // GB
                            side_job(base + number, n + 2, kind, g, k, b)
                        weigh(n, i, weigh_of_unit[u], it)
                    turn(n, i)

            over_bodies(pe, body)

        @block.scalar
        def _(act):
            def exp(n, i, u):
                kt0, size = units[u]
                if u == 0:
                    act.wait_ge(weighted, n + 1)
                act.wait_ge(unit_scored, n * NU + u + 1)
                act.activation(PT[:, i % 2, kt0:kt0 + size, :].rearrange("p k q -> p (k q)"),
                               ST[:, (u + i % 2) % 3, 0:size * T], ACT.Exp, scale=scale).then_inc(unit_exp, 1)

            def side_job(number, i, kind, g, k):
                act.wait_ge(side_product, number + 1)
                if kind == "shift":
                    act.activation(QP[SHIFT:SHIFT + 2, i % 8, 0, :], Side[SHIFT:SHIFT + 2, 0:T], ACT.Copy)\
                       .then_inc(side_taken, 1)
                else:
                    act.activation(level[:, g % 2, 0, k * kcw:(k + 1) * kcw], Side[:, 0:kcw], ACT.Copy)\
                       .then_inc(high_ready, 1)

            act.sem_inc(side_taken, 1)
            act.sem_inc(unit_exp, NU)
            for number, (kind, g, k) in enumerate(first_jobs + second_jobs):
                side_job(number, None, kind, g, k)
            for head in range(2):
                side_job(J0 - 2 + head, head, "shift", None, None)
            for u in range(NU):
                exp(0, 0, u)

            def body(it, last):
                jobs = body_jobs(last)
                for i in range(HB):
                    for u in range(NU):
                        if u == NU - 1:
                            act.wait_ge(weighted, it * HB + i + 3)
                            act.activation(OT[0:CC + 1, :], Op[0:CC + 1, i % 2, 0:T], ACT.Copy).then_inc(weighted_copied, 1)
                        if not (last and i + 1 >= HB):
                            exp(it * HB + i + 1, (i + 1) % HB, u)
                        if (i, u) in jobs:
                            number, kind, g, k = jobs[i, u]
                            side_job(J0 + it * JB + number, i + 2, kind, g, k)

            over_bodies(act, body)

        @block.vector
        def _(dve):
            def reduce_part(n, j):
                dve.wait_ge(max_scores, n * 2 * NC + j + 1)
                dve.tensor_reduce(chunk_max[:, j // NC, j % NC:j % NC + 1], SM[:, j % 2, 0:chunks[j % NC][1]],
                                  AX_X, ALU.max).then_inc(chunk_reduced, 1)

            def diagonals(n, job):
                dve.drain()
                dve.tensor_reduce(neg_max[:], chunk_max[:], AX_X, ALU.max, negate=True)
                dve.drain()
                dve.tensor_copy(high_max[:], neg_max[:])
                dve.drain()
                dve.tensor_tensor(low_max[:], neg_max[:], high_max[:], ALU.subtract)
                dve.drain()
                if not (isinstance(n, int) and n == 0):
                    dve.wait_ge(side_product, job + 1)
                for part, value in enumerate((neg_max, low_max)):
                    op = dve.tensor_tensor(diag[:, part, :, :], consts["ident"][:].unsqueeze(1).to_broadcast([P, 2, P]),
                                           value[:].unsqueeze(2).to_broadcast([P, 2, P]), ALU.mult)
                op.then_inc(diagonal_ready, 1)
                dve.drain()

            def key_rest(count, g, k):
                cols = slice(k * kcw, (k + 1) * kcw)
                if isinstance(count, int) and count < 4:
                    pass
                else:
                    dve.wait_ge(chunk_split, count - 3)
                dve.wait_ge(high_ready, count + 1)
                dve.tensor_tensor(rest[:, cols], Side[:, 0:kcw], level[:, g % 2, 0, cols], ALU.subtract)\
                   .then_inc(side_taken, 1)

            def norm(it, i):
                b, h = it * BPB + i // H, i % H
                dve.drain()
                dve.wait_ge(turned, it * HB + i + 1)
                out = Op[:, i % 2, T:T + 2 * (d + 1)].rearrange("p (q e) -> p q e", q=2)
                dve.reciprocal(rec[:], out[:, :, d])
                dve.drain()
                for qt in range(2):
                    dst = O[:, bass.ds(b * QT_PER_B + qt, 1), h * d:h * d + d]
                    if add_to:
                        op = dve.scalar_tensor_tensor(out=dst, in0=out[:, qt:qt + 1, 0:d], scalar=rec[:, qt:qt + 1],
                                                      in1=dst, op0=ALU.mult, op1=ALU.add)
                    else:
                        op = dve.tensor_scalar(dst, out[:, qt:qt + 1, 0:d], rec[:, qt:qt + 1], None, ALU.mult)
                op.then_inc(normed, 1)

            if terms[-1][1] + d < ROWS:
                dve.memset(KP[:], 0.0)
                dve.drain()
            dve.sem_inc(packs_cleared, 1)
            dve.sem_inc(chunk_reduced, 2)
            dve.sem_inc(normed, 2)
            for kind, g, k in first_jobs:
                key_rest(k, g, k)
            dve.memset(KP[SHIFT:SHIFT + 2, :, 0, CTX:CTX_PAD], 0.0)
            dve.memset(KP[SHIFT:SHIFT + 2, :, 0, 0:CTX], 1.0).then_inc(ones_ready, 1)
            for head in range(3):
                for j in range(2 * NC):
                    reduce_part(head, j)
                    if head == 0 and j < len(second_jobs):
                        key_rest(4 + j, 1, j)
                diagonals(head, J0 - 3 + head)

            def body(it, last):
                jobs = body_jobs(last)
                chunks_split = 4 * AHEAD_K + it * (4 * GBODY)
                for i in range(HB):
                    more = not (last and i + 3 >= HB)
                    for u in range(NU):
                        if more:
                            for j in max_of_unit[u]:
                                reduce_part(it * HB + i + 3, j)
                        if (i, u) in jobs and jobs[i, u][1] == "key":
                            _, _, g, k = jobs[i, u]
                            key_rest(chunks_split + 4 * (g - AHEAD_K) + k, g, k)
                    if more:
                        diagonals(it * HB + i + 3, J0 + it * JB + jobs[i, 1][0])
                    norm(it, i)

            over_bodies(dve, body)


def tok(a, t):
    return a[:, t * P:(t + 1) * P]


def chunk(a, k):
    return a[:, k * BANK:(k + 1) * BANK]


def turn_tokens(c, dst, src, ident, post=None):
    transpose_tiles(c, [([src[:, 4 * g + k, :] for k in range(4)], chunk(dst, g), post) for g in range(CH)], ident)


def project(dst, w, xT, post=("copy",)):
    return [(chunk(dst, k), [(w, chunk(xT, k))], post) for k in range(CH)]


def value_jobs(V, w, row, ones, xT):
    n = w.shape[1]
    parts = -(-n // BANK)
    s = n // parts
    return [(V[:, t, k * s:k * s + s], [(tok(xT, t), w[:, k * s:k * s + s]), (ones[0:1, 0:P], row[0:1, k * s:k * s + s])],
             ("copy",)) for t in range(NT) for k in range(parts)]


def stage_mla(c, x, K):
    with ExitStack() as ctx:
        W = load_stage(c, ctx, ["A_kvd", "A_ku", "A_q", "A_qr", "A_qrs", "A_kr", "A_krs", "A_vu", "A_vrow", "A_wo",
                                "A_cos", "A_sin"])
        O = c.sbuf(ctx, "O", [P, NT, P])
        QT, KT = c.sbuf(ctx, "QT", [P, 1, N]), c.sbuf(ctx, "KT", [P, 1, N])
        with ExitStack() as inner:
            xT, ckvT = c.sbuf(inner, "xT", [P, N]), c.sbuf(inner, "ckvT", [P, N])
            QR, KR = c.sbuf(inner, "QR", [P, N]), c.sbuf(inner, "KR", [P, N])
            QRs, KRs = c.sbuf(inner, "QRs", [P, N]), c.sbuf(inner, "KRs", [P, N])
            V = c.sbuf(inner, "V", [P, NT, H * 9])
            turn_tokens(c, xT, x, K["ident"])
            cos, sin = ("mul", W["A_cos"][:]), ("mul", W["A_sin"][:])
            products(c, project(ckvT, W["A_kvd"][:], xT) + project(QT[:, 0, :], W["A_q"][:], xT)
                     + project(QR, W["A_qr"][:], xT, cos) + project(QRs, W["A_qrs"][:], xT, sin))
            products(c, project(KT[:, 0, :], W["A_ku"][:], ckvT) + project(KR, W["A_kr"][:], ckvT, cos)
                     + project(KRs, W["A_krs"][:], ckvT, sin) + value_jobs(V, W["A_vu"], W["A_vrow"], K["ones"], ckvT))
            add_pairs(c, [(QR[:], QRs[:]), (KR[:], KRs[:])])
            names = ("query", "key", "rotary_query", "rotary_key")
            own_parts = [c.nc.dram_tensor(f"own_{k}_parts_A", (LEVELS, P, N), BF16).ap() for k in names]
            split_features(c, feature_groups(QT, own_parts[0]) + feature_groups(KT, own_parts[1])
                           + [(QR[:], own_parts[2]), (KR[:], own_parts[3])])
            self_attention(c, own_parts[0], own_parts[1], V, O, K, 8, "causal", 40 ** -0.5,
                                  (own_parts[2], own_parts[3], 32))
        OT = QT
        turn_tokens(c, OT[:, 0, :], O, K["ident"])
        summed = c.sbuf(ctx, "summed", [P, NT, P])
        sum_and_norm(c, lambda t: [(tok(OT[:, 0, :], t), W["A_wo"][:])], summed, x, [x])


def stage_self_and_cross(c, x, K):
    with ExitStack() as ctx:
        W = load_stage(c, ctx, ["B_q", "B_k", "B_cq", "B_bq", "B_bk", "B_bcq", "B_v", "B_vrow", "B_wk", "B_wv",
                                "B_wp", "B_bp"])
        O = c.sbuf(ctx, "O", [P, NT, P])
        QcT = c.sbuf(ctx, "QcT", [P, 1, N])
        with ExitStack() as inner:
            xT = c.sbuf(inner, "xT", [P, N])
            QT, KT = c.sbuf(inner, "QT", [P, 1, N]), c.sbuf(inner, "KT", [P, 1, N])
            V = c.sbuf(inner, "V", [P, NT, H * 9])
            turn_tokens(c, xT, x, K["ident"])
            products(c, project(QT[:, 0, :], W["B_q"][:], xT, ("bias", W["B_bq"][:, 0:1]))
                     + project(KT[:, 0, :], W["B_k"][:], xT, ("bias", W["B_bk"][:, 0:1]))
                     + project(QcT[:, 0, :], W["B_cq"][:], xT, ("bias", W["B_bcq"][:, 0:1]))
                     + value_jobs(V, W["B_v"], W["B_vrow"], K["ones"], xT))
            own_parts = [c.nc.dram_tensor(f"own_{k}_parts_B", (LEVELS, P, N), BF16).ap() for k in ("query", "key")]
            query_parts = c.nc.dram_tensor("query_parts_B", (LEVELS, P, N), BF16).ap()
            split_features(c, feature_groups(QT, own_parts[0]) + feature_groups(KT, own_parts[1])
                           + feature_groups(QcT, query_parts))
            self_attention(c, *own_parts, V, O, K, 8, "causal", 8 ** -0.5)
        cross_attention(c, query_parts, O, W["B_wk"], W["B_wv"], c.ins["ctxT"], c.ins["ctx"], K, 8, True, 8 ** -0.5)
        OT = QcT[:, 0, :]
        turn_tokens(c, OT, O, K["ident"])
        summed = c.sbuf(ctx, "summed", [P, NT, P])
        sum_and_norm(c, lambda t: [(tok(OT, t), W["B_wp"][:]), (K["ones"][0:1, 0:P], W["B_bp"][0:1, :])], summed, x, [x])



E1, CAP1, F1 = 8, 512, 512
E2, CAP2, ADAPTERS = 32, 80, 16
BIG = 65536.0


def zero_rows(c, ctx, array):
    nc = c.nc
    zeros = c.sbuf(ctx, "zeros", [P, 2048])
    cleared, filled = c.sem("cleared"), c.sem("filled")
    step = 2048 // array.shape[1] * P
    with nc.Block() as block:
        @block.vector
        def _(dve):
            dve.memset(zeros[:], 0.0).then_inc(cleared, 1)

        @block.sync
        def _(sp):
            sp.wait_ge(cleared, 1)
            for r in range(0, array.shape[0], step):
                sp.dma_start(array[r:r + step, :].rearrange("(p k) d -> p (k d)", p=P), zeros[:]).then_inc(filled, 16)
    return filled, 16 * (array.shape[0] // step)


def choose_two(c, ctx, logit_terms, E, iota):
    nc = c.nc
    gates = c.sbuf(ctx, "gates", [P, NT, E])
    top = c.sbuf(ctx, "top", [P, NT, 8])
    hot = [c.sbuf(ctx, f"hot{k}", [P, NT, E]) for k in range(2)]
    with ExitStack() as inner:
        acc = c.psum(inner, "logits", [P, NT, E])
        row_max, row_sum = c.sbuf(inner, "row_max", [P, NT]), c.sbuf(inner, "row_sum", [P, NT])
        index = c.sbuf(inner, "index", [P, NT, 8], U32)
        indexf = c.sbuf(inner, "indexf", [P, NT, 8])
        logits_ready, shifted, powers = c.sem("logits_ready"), c.sem("logits_shifted"), c.sem("powers")
        block = inner.enter_context(nc.Block())

        @block.tensor
        def _(pe):
            for t in range(NT):
                lhsT, rhs = logit_terms(t)
                op = pe.matmul(acc[:, t, :], lhsT, rhs, start=True, stop=True)
            op.then_inc(logits_ready, 1)

        @block.scalar
        def _(act):
            act.wait_ge(shifted, 1)
            act.activation(gates[:], gates[:], ACT.Exp).then_inc(powers, 1)

        @block.vector
        def _(dve):
            dve.wait_ge(logits_ready, 1)
            dve.tensor_reduce(row_max[:], acc[:], AX_X, ALU.max)
            dve.drain()
            dve.tensor_tensor(gates[:], acc[:], row_max[:].unsqueeze(2).to_broadcast([P, NT, E]), ALU.subtract)\
               .then_inc(shifted, 1)
            dve.wait_ge(powers, 1)
            dve.tensor_reduce(row_sum[:], gates[:], AX_X, ALU.add)
            dve.drain()
            dve.reciprocal(row_max[:], row_sum[:])
            dve.drain()
            dve.tensor_tensor(gates[:], gates[:], row_max[:].unsqueeze(2).to_broadcast([P, NT, E]), ALU.mult)
            dve.drain()
            for t in range(NT):
                dve.max(top[:, t, :], gates[:, t, :])
            dve.drain()
            for t in range(NT):
                dve.max_index(index[:, t, :], top[:, t, :], gates[:, t, :])
            dve.drain()
            dve.tensor_copy(indexf[:], index[:])
            dve.drain()
            for k in range(2):
                dve.tensor_tensor(hot[k][:], iota[:].unsqueeze(1).to_broadcast([P, NT, E]),
                                  indexf[:, :, k:k + 1].to_broadcast([P, NT, E]), ALU.is_equal)
    return gates, top, hot


def stage_moe(c, x, K):
    nc = c.nc
    rows = nc.dram_tensor("expert_rows", (E1 * CAP1, P), F32).ap()
    results = nc.dram_tensor("expert_results", (E1 * CAP1, P), F32).ap()
    with ExitStack() as ctx:
        W = load_stage(c, ctx, ["C_q", "C_qs", "C_k", "C_ks", "C_v", "C_vrow", "C_proj", "C_g1", "C_s1", "C_g2", "C_s2",
                                "C_gate", "C_b1", "C_b2", "C_cos", "C_sin", "iota8", "slot_base", "upto", "all_ones"])
        y = c.sbuf(ctx, "y", [P, NT, P])
        yhat = c.sbuf(ctx, "yhat", [P, NT, P])
        with ExitStack() as inner:
            O = c.sbuf(inner, "O", [P, NT, P])
            hT = c.sbuf(inner, "hT", [P, N])
            QT, KT = c.sbuf(inner, "QT", [P, 1, N]), c.sbuf(inner, "KT", [P, 1, N])
            V = c.sbuf(inner, "V", [P, NT, H * 9])
            with ExitStack() as part:
                Qs, Ks = c.sbuf(part, "Qs", [P, N]), c.sbuf(part, "Ks", [P, N])
                sum_and_norm(c, None, None, yhat, [x])
                turn_tokens(c, hT, yhat, K["ident"], (W["C_g1"][:, 0:1], W["C_s1"][:, 0:1]))
                cos, sin = ("mul", W["C_cos"][:]), ("mul", W["C_sin"][:])
                products(c, project(QT[:, 0, :], W["C_q"][:], hT, cos) + project(Qs, W["C_qs"][:], hT, sin)
                         + project(KT[:, 0, :], W["C_k"][:], hT, cos) + project(Ks, W["C_ks"][:], hT, sin)
                         + value_jobs(V, W["C_v"], W["C_vrow"], K["ones"], hT))
                add_pairs(c, [(QT[:, 0, :], Qs[:]), (KT[:, 0, :], Ks[:])])
            own_parts = [c.nc.dram_tensor(f"own_{k}_parts_C", (LEVELS, P, N), BF16).ap() for k in ("query", "key")]
            split_features(c, feature_groups(QT, own_parts[0]) + feature_groups(KT, own_parts[1]))
            self_attention(c, *own_parts, V, O, K, 8, "causal", 8 ** -0.5)
            turn_tokens(c, hT, O, K["ident"])
            sum_and_norm(c, lambda t: [(tok(hT, t), W["C_proj"][:])], y, yhat, [x])
        h2T = c.sbuf(ctx, "h2T", [P, N])
        turn_tokens(c, h2T, yhat, K["ident"], (W["C_g2"][:, 0:1], W["C_s2"][:, 0:1]))
        zeroed = zero_rows(c, ctx, rows)
        gates, top, hot = choose_two(c, ctx, lambda t: (tok(h2T, t), W["C_gate"][:]), E1, W["iota8"])

        place = [c.sbuf(ctx, f"place{k}", [P, NT], I32) for k in range(2)]
        source = [c.sbuf(ctx, f"source{k}", [P, NT], I32) for k in range(2)]
        weight = [c.sbuf(ctx, f"weight{k}", [P, NT]) for k in range(2)]
        with ExitStack() as inner:
            acc = c.psum(inner, "counts", [P, 2, BANK])
            chosen = c.sbuf(inner, "chosen", [P, NT, E1])
            sums = [c.sbuf(inner, f"sums{k}", [P, NT, E1]) for k in range(2)]
            slot, keep, pick = (c.sbuf(inner, n, [P, NT, E1]) for n in ("slot", "keep", "pick"))
            at, kept, scratch = (c.sbuf(inner, n, [P, NT]) for n in ("at", "kept", "scratch"))
            chosen_ready, counted = c.sem("chosen_ready"), c.sem("counted")
            places_ready, scattered = c.sem("places_ready"), c.sem("scattered", True)
            block = inner.enter_context(nc.Block())

            @block.tensor
            def _(pe):
                pe.wait_ge(chosen_ready, 1)
                flat = chosen[:].rearrange("p t e -> p (t e)")
                pe.matmul(acc[:, 0, 0:NT * E1], W["upto"][:], flat, start=True, stop=True)
                pe.matmul(acc[:, 1, 0:NT * E1], W["all_ones"][:], flat, start=True, stop=True).then_inc(counted, 1)

            @block.vector
            def _(dve):
                dve.tensor_tensor(chosen[:], hot[0][:], hot[1][:], ALU.add).then_inc(chosen_ready, 1)
                dve.wait_ge(counted, 1)
                within = acc[:, 0, 0:NT * E1].rearrange("p (t e) -> p t e", t=NT)
                totals = acc[:, 1, 0:NT * E1].rearrange("p (t e) -> p t e", t=NT)
                dve.tensor_copy(sums[0][:], totals)
                step, now = 1, 0
                while step < NT:
                    dve.drain()
                    a, b_ = sums[now], sums[1 - now]
                    dve.tensor_copy(b_[:, 0:step, :], a[:, 0:step, :])
                    dve.tensor_tensor(b_[:, step:, :], a[:, step:, :], a[:, 0:NT - step, :], ALU.add)
                    step, now = 2 * step, 1 - now
                dve.drain()
                dve.tensor_tensor(slot[:], sums[now][:], totals, ALU.subtract)
                dve.drain()
                dve.tensor_tensor(slot[:], slot[:], within, ALU.add)
                dve.drain()
                dve.tensor_scalar(keep[:], slot[:], CAP1 + 0.5, None, ALU.is_lt)
                dve.tensor_tensor(sums[0][:], slot[:], W["slot_base"][:].unsqueeze(1).to_broadcast([P, NT, E1]), ALU.add)
                for k in range(2):
                    dve.drain()
                    dve.tensor_tensor(pick[:], hot[k][:], sums[0][:], ALU.mult)
                    dve.tensor_tensor(slot[:], hot[k][:], keep[:], ALU.mult)
                    dve.drain()
                    dve.tensor_reduce(at[:], pick[:], AX_X, ALU.add)
                    dve.tensor_reduce(kept[:], slot[:], AX_X, ALU.add)
                    dve.drain()
                    dve.tensor_tensor(weight[k][:], top[:, :, k], kept[:], ALU.mult)
                    dve.tensor_tensor(source[k][:], at[:], kept[:], ALU.mult)
                    dve.tensor_scalar(scratch[:], kept[:], -BIG, BIG, ALU.mult, ALU.add)
                    dve.drain()
                    dve.tensor_tensor(place[k][:], at[:], scratch[:], ALU.add)
                dve.drain().then_inc(places_ready, 1)

            @block.gpsimd
            def _(pool):
                pool.wait_ge(*zeroed)
                pool.wait_ge(places_ready, 1)
                for t in range(NT):
                    for k in range(2):
                        pool.indirect_dma_start(rows, bass.IndirectOffsetOnAxis(place[k][:, t:t + 1], 0), yhat[:, t, :],
                                                None, bounds_check=E1 * CAP1 - 1, oob_is_err=False)\
                            .then_inc(scattered, 16)
                pool.wait_ge(scattered, 16 * 2 * NT)

        moe_experts(c, W, K, rows, results)

        back = [c.sbuf(ctx, f"back{k}", [P, NT, P]) for k in range(2)]
        gathered = [c.sem(f"gathered{g}", True) for g in range(CH)]
        with nc.Block() as block:
            @block.gpsimd
            def _(pool):
                for t in range(NT):
                    for k in range(2):
                        pool.indirect_dma_start(back[k][:, t, :], None, results,
                                                bass.IndirectOffsetOnAxis(source[k][:, t:t + 1], 0))\
                            .then_inc(gathered[t // 4], 16)

            @block.vector
            def _(dve):
                dve.tensor_tensor(y[:], y[:], x[:], ALU.add)
                for g, k in [(g, k) for g in range(CH) for k in range(2)]:
                    dve.wait_ge(gathered[g], 16 * 2 * 4)
                    dve.drain()
                    for t in range(4 * g, 4 * g + 4):
                        dve.scalar_tensor_tensor(out=y[:, t, :], in0=back[k][:, t, :], scalar=weight[k][:, t:t + 1],
                                                 in1=y[:, t, :], op0=ALU.mult, op1=ALU.add)
        sum_and_norm(c, None, None, x, [y])


def moe_experts(c, W, K, rows, results):
    nc = c.nc
    NF, NS = F1 // P, CAP1 // P
    with ExitStack() as ctx:
        turned = c.psum(ctx, "turned", [P, BANK])
        wide = c.psum(ctx, "wide", [P, NF, BANK])
        back = c.psum(ctx, "back", [P, NS, P])
        xe = c.sbuf(ctx, "expert_rows", [P, 2, NS, P])
        w1, w2 = c.sbuf(ctx, "w1", [P, 2, F1]), c.sbuf(ctx, "w2", [P, 2, NF, P])
        xeT = c.sbuf(ctx, "expert_rowsT", [P, CAP1])
        hid = c.sbuf(ctx, "hidden", [P, NF, CAP1])
        res = c.sbuf(ctx, "result_rows", [P, 2, NS, P])
        loaded = [c.sem("expert_loaded0"), c.sem("expert_loaded1")]
        turned_ready, turned_copied = c.sem("turned_ready"), c.sem("turned_copied")
        wide_ready, hidden_ready = c.sem("wide_ready"), c.sem("hidden_ready")
        back_ready, back_copied = c.sem("back_ready"), c.sem("back_copied")
        stored = [c.sem("stored0"), c.sem("stored1")]
        block = ctx.enter_context(nc.Block())

        @block.sync
        def _(sp):
            def load(e, s):
                sp.wait_ge(back_ready, e + 1)
                sp.dma_start(xe[:, s, :, :], rows[bass.ds(e * CAP1, CAP1), :].rearrange("(s p) d -> p s d", p=P))\
                  .then_inc(loaded[s], 16)
                sp.dma_start(w1[:, s, :], c.ins["C_w1"][bass.ds(e, 1), :, :].rearrange("o p f -> (o p) f"))\
                  .then_inc(loaded[s], 16)
                sp.dma_start(w2[:, s, :, :], c.ins["C_w2"][bass.ds(e, 1), :, :, :].rearrange("o p f d -> (o p) f d"))\
                  .then_inc(loaded[s], 16)

            def store(e, s):
                sp.wait_ge(back_copied, e + 2)
                sp.dma_start(results[bass.ds(e * CAP1, CAP1), :].rearrange("(s p) d -> p s d", p=P), res[:, s, :, :])\
                  .then_inc(stored[s], 16)

            for s in range(2):
                sp.sem_inc(stored[s], 16)
                load(s, s)
            with sp.Fori(1, E1 // 2, 1) as i:
                for s in range(2):
                    load(i * 2 + s, s)
                    store(i * 2 + s - 2, s)
            for s in range(2):
                store(E1 - 2 + s, s)
            for s in range(2):
                sp.wait_ge(stored[s], 16 + 16 * (E1 // 2))

        @block.tensor
        def _(pe):
            pe.sem_inc(back_ready, 2)
            with pe.Fori(0, E1 // 2, 1) as i:
                for s in range(2):
                    e = i * 2 + s
                    pe.wait_ge(loaded[s], i * 48 + 48)
                    pe.wait_ge(turned_copied, e + 1)
                    for k in range(NS):
                        op = pe.transpose(turned[:, k * P:k * P + P], xe[:, s, k, :], K["ident"][:])
                    op.then_inc(turned_ready, 1)
                    pe.wait_ge(turned_copied, e + 2)
                    for f in range(NF):
                        pe.wait_ge(hidden_ready, e * NF + f + 1)
                        pe.matmul(wide[:, f, :], w1[:, s, f * P:f * P + P], xeT[:], start=True, stop=True)\
                          .then_inc(wide_ready, 1)
                    pe.wait_ge(hidden_ready, e * NF + 2 * NF)
                    pe.wait_ge(back_copied, e + 1)
                    for k in range(NS):
                        for f in range(NF):
                            pe.matmul(back[:, k, :], hid[:, f, k * P:k * P + P], w2[:, s, f, :], start=f == 0, stop=False)
                        op = pe.matmul(back[:, k, :], K["ones"][0:1, 0:P], W["C_b2"][0:1, bass.ds(e * P, P)],
                                       start=False, stop=True)
                    op.then_inc(back_ready, 1)

        @block.scalar
        def _(act):
            act.sem_inc(hidden_ready, NF)
            with act.Fori(0, E1 // 2, 1) as i:
                for s in range(2):
                    e = i * 2 + s
                    for f in range(NF):
                        act.wait_ge(wide_ready, e * NF + f + 1)
                        if f == 0:
                            act.wait_ge(back_ready, e + 2)
                        act.activation(hid[:, f, :], wide[:, f, :], ACT.Gelu, bias=W["C_b1"][:, bass.ds(e * NF + f, 1)])\
                           .then_inc(hidden_ready, 1)

        @block.vector
        def _(dve):
            dve.sem_inc(turned_copied, 1)
            dve.sem_inc(back_copied, 1)
            with dve.Fori(0, E1 // 2, 1) as i:
                for s in range(2):
                    e = i * 2 + s
                    dve.wait_ge(turned_ready, e + 1)
                    dve.tensor_scalar(xeT[:], turned[:], W["C_g2"][:, 0:1], W["C_s2"][:, 0:1], ALU.mult, ALU.add)\
                       .then_inc(turned_copied, 1)
                    dve.wait_ge(stored[s], i * 16 + 16)
                    dve.wait_ge(back_ready, e + 3)
                    dve.tensor_copy(res[:, s, :, :], back[:]).then_inc(back_copied, 1)


def stage_single_head(c, x, K):
    with ExitStack() as ctx:
        W = load_stage(c, ctx, ["D_q", "D_k", "D_v", "D_vrow"])
        O = c.sbuf(ctx, "O", [P, NT, P])
        xT = c.sbuf(ctx, "xT", [P, N])
        QT, KT = c.sbuf(ctx, "QT", [P, N]), c.sbuf(ctx, "KT", [P, N])
        V = c.sbuf(ctx, "V", [P, NT, P + 1])
        turn_tokens(c, xT, x, K["ident"])
        products(c, project(QT, W["D_q"][:], xT) + project(KT, W["D_k"][:], xT)
                 + value_jobs(V, W["D_v"], W["D_vrow"], K["ones"], xT))
        single_head_attention(c, QT, KT, V, O, K, P ** -0.5)
        add_pairs(c, [(O[:], x[:])])
        sum_and_norm(c, None, None, x, [O])


def feed_forward(c, W, K, name, xo, others, out):
    nc = c.nc
    NF = 4
    with ExitStack() as ctx:
        hat, hatT = c.sbuf(ctx, "hat", [P, NT, P]), c.sbuf(ctx, "hatT", [P, N])
        wide = c.sbuf(ctx, "wide", [P, NF, N])
        sum_and_norm(c, None, None, hat, [xo])
        turn_tokens(c, hatT, hat, K["ident"], (W[name + "_g3"][:, 0:1], W[name + "_s3"][:, 0:1]))
        products(c, [(chunk(wide[:, f, :], k), [(W[name + "_w2"][:, f * P:f * P + P], chunk(hatT, k))],
                      ("gelu", W[name + "_b2"][:, f:f + 1])) for k in range(CH) for f in range(NF)])
        sum_and_norm(c, lambda t: [(tok(wide[:, f, :], t), W[name + "_w3"][:, f, :]) for f in range(NF)]
                     + [(K["ones"][0:1, 0:P], W[name + "_b3"][0:1, :])], out, None, others + [xo])


def turn_wide(c, dst, src, K):
    transpose_tiles(c, [([src[:, 4 * g + k, w * P:w * P + P] for k in range(4)], chunk(dst[:, w, :], g), None)
                        for w in range(4) for g in range(CH)], K["ident"])


def norm_context(c, W, K, dst, plain):
    nc = c.nc
    full, rest = CTX // P, CTX % P
    with ExitStack() as ctx:
        raw = c.sbuf(ctx, "raw", [P, 2, NKT, CC])
        hat = c.sbuf(ctx, "hat", [P, 2, NKT, CC])
        stats, moments = c.sbuf(ctx, "stats", [P, NKT, 6]), c.sbuf(ctx, "moments", [P, NKT, 2])
        deviation, rstd = c.sbuf(ctx, "deviation", [P, NKT]), c.sbuf(ctx, "rstd", [P, NKT])
        eps = c.sbuf(ctx, "eps", [P, 1])
        out = c.sbuf(ctx, "out", [CC, CTX_PAD])
        turned = c.psum(ctx, "turned", [P, 4, BANK])
        cleared = c.sem("cleared")
        loaded = [c.sem("raw_loaded0"), c.sem("raw_loaded1")]
        variances, deviations = c.sem("variances"), c.sem("deviations")
        normed, turned_ready, copied, stored = c.sem("normed"), c.sem("turned_ready"), c.sem("copied"), c.sem("stored")
        plain_stored = [c.sem("plain_stored0"), c.sem("plain_stored1")]
        block = ctx.enter_context(nc.Block())

        @block.sync
        def _(sp):
            def store_plain(b, s):
                rows = plain[bass.ds(b, 1), :, :].rearrange("o k d -> (o k) d")
                sp.dma_start(rows[0:full * P, :].rearrange("(t p) d -> p t d", p=P), hat[:, s, 0:full, :])\
                  .then_inc(plain_stored[s], 16)
                sp.dma_start(rows[full * P:CTX, :], hat[0:rest, s, full, :]).then_inc(plain_stored[s], 16)

            def load(b, s):
                src = c.ins["ctx"][bass.ds(b, 1), :, :].rearrange("o k d -> (o k) d")
                sp.dma_start(raw[:, s, 0:full, :], src[0:full * P, :].rearrange("(t p) d -> p t d", p=P))\
                  .then_inc(loaded[s], 16)
                sp.dma_start(raw[0:rest, s, full, :], src[full * P:CTX, :]).then_inc(loaded[s], 16)

            def store(b):
                sp.wait_ge(copied, b * 4 + 8)
                sp.dma_start(dst[bass.ds(b, 1), :, :].rearrange("o c k -> (o c) k"), out[:, 0:CTX]).then_inc(stored, 16)

            sp.wait_ge(cleared, 1)
            sp.sem_inc(stored, 16)
            for s in range(2):
                sp.sem_inc(plain_stored[s], 32)
                load(s, s)
            with sp.Fori(1, B // 2, 1) as i:
                for s in range(2):
                    b = i * 2 + s
                    sp.wait_ge(normed, b - 1)
                    sp.sem_inc(c.seen, 1)
                    load(b, s)
                    store_plain(b - 2, s)
                    store(b - 2)
            for b in range(B - 2, B):
                sp.wait_ge(normed, b + 1)
                store_plain(b, b % 2)
                store(b)
            sp.wait_ge(stored, 16 + 16 * B)
            for s in range(2):
                sp.wait_ge(plain_stored[s], 32 + 32 * (B // 2))

        @block.tensor
        def _(pe):
            with pe.Fori(0, B // 2, 1) as i:
                for s in range(2):
                    b = i * 2 + s
                    pe.wait_ge(normed, b + 1)
                    for g in range(4):
                        pe.wait_ge(copied, b * 4 + g + 1)
                        pe.sem_inc(c.seen, 1)
                        for t in range(4 * g, min(4 * g + 4, NKT)):
                            op = pe.transpose(turned[0:CC, g, (t % 4) * P:(t % 4) * P + P], hat[:, s, t, :], K["ident"][:])
                        op.then_inc(turned_ready, 1)

        @block.scalar
        def _(act):
            act.sem_inc(copied, 4)
            with act.Fori(0, B, 1) as b:
                act.wait_ge(variances, b + 1)
                act.activation(deviation[:], moments[:, :, 1], ACT.Sqrt, bias=eps[:, 0:1]).then_inc(deviations, 1)
                act.wait_ge(stored, b * 16 + 16)
                for g in range(4):
                    act.wait_ge(turned_ready, b * 4 + g + 1)
                    cols = min(BANK, CTX_PAD - g * BANK)
                    act.activation(out[:, g * BANK:g * BANK + cols], turned[0:CC, g, 0:cols], ACT.Copy)\
                       .then_inc(copied, 1)

        @block.vector
        def _(dve):
            dve.memset(eps[:], EPS)
            dve.memset(raw[:], 0.0).then_inc(cleared, 1)
            with dve.Fori(0, B // 2, 1) as i:
                for s in range(2):
                    b = i * 2 + s
                    dve.wait_ge(loaded[s], i * 32 + 32)
                    for t in range(NKT):
                        dve.bn_stats(stats[:, t, :], raw[:, s, t, :])
                    dve.drain()
                    for t in range(NKT):
                        op = dve.bn_aggr(moments[:, t, :], stats[:, t, :])
                    op.then_inc(variances, 1)
                    dve.wait_ge(deviations, b + 1)
                    dve.reciprocal(rstd[:], deviation[:])
                    dve.drain()
                    dve.wait_ge(plain_stored[s], i * 32 + 32)
                    if s == 0:
                        dve.wait_ge(copied, b * 4 + 4)
                    for t in range(NKT):
                        dve.tensor_scalar(hat[:, s, t, :], raw[:, s, t, :], moments[:, t, 0:1], rstd[:, t:t + 1],
                                          ALU.subtract, ALU.mult)
                    dve.drain()
                    dve.tensor_tensor(hat[:, s, :, :], hat[:, s, :, :],
                                      W["a2_gain_row"][:].unsqueeze(1).to_broadcast([P, NKT, CC]), ALU.mult)
                    dve.drain()
                    dve.tensor_tensor(hat[:, s, :, :], hat[:, s, :, :],
                                      W["a2_shift_row"][:].unsqueeze(1).to_broadcast([P, NKT, CC]), ALU.add)\
                       .then_inc(normed, 1)
                    dve.drain()


def stage_two_blocks(c, x, K):
    nc = c.nc
    normed_ctx = nc.dram_tensor("normed_context_turned", (B, CC, CTX), F32).ap()
    plain_ctx = nc.dram_tensor("normed_context", (B, CTX, CC), F32).ap()
    with ExitStack() as ctx:
        x1 = c.sbuf(ctx, "x1", [P, NT, P])
        with ExitStack() as first:
            W = load_stage(c, first, ["*E_g1", "*E_s1", "*E_g2", "*E_s2", "a1_q", "a1_k", "a1_v", "a1_vrow", "a1_li1",
                                      "a1_b1", "a1_xg", "a1_xs", "a1_yg", "a1_ys", "a1_g3", "a1_s3", "a1_w2", "a1_b2",
                                      "a1_w3", "a1_b3"])
            sum_and_norm(c, None, None, x1, [x], W["E_g1"], W["E_s1"])
            own_parts = [nc.dram_tensor(f"own_{k}_parts_E", (LEVELS, 4 * P, N), BF16).ap() for k in ("query", "key")]
            O = c.sbuf(first, "O", [P, NT, 4 * P])
            with ExitStack() as part:
                V = c.sbuf(part, "V", [P, NT, H * 33])
                with ExitStack() as proj:
                    QT = c.sbuf(proj, "QT", [P, 4, N])
                    hat, hatT = c.sbuf(proj, "hat", [P, NT, P]), c.sbuf(proj, "hatT", [P, N])
                    sum_and_norm(c, None, None, hat, [x1])
                    turn_tokens(c, hatT, hat, K["ident"], (W["a1_xg"][:, 0:1], W["a1_xs"][:, 0:1]))
                    products(c, [j for g in range(4) for j in project(QT[:, g, :], W["a1_q"][:, g * P:g * P + P], hatT)])
                    split_features(c, feature_groups(QT, own_parts[0]))
                    turn_tokens(c, hatT, hat, K["ident"], (W["a1_yg"][:, 0:1], W["a1_ys"][:, 0:1]))
                    products(c, [j for g in range(4) for j in project(QT[:, g, :], W["a1_k"][:, g * P:g * P + P], hatT)]
                             + value_jobs(V, W["a1_v"], W["a1_vrow"], K["ones"], hatT))
                    split_features(c, feature_groups(QT, own_parts[1]))
                self_attention(c, *own_parts, V, O, K, 32, "future", 32 ** -0.5)
            OT = c.sbuf(first, "OT", [P, 4, N])
            turn_wide(c, OT, O, K)
            xo = c.sbuf(first, "xo", [P, NT, P])
            sum_and_norm(c, lambda t: [(tok(OT[:, g, :], t), W["a1_li1"][:, g, :]) for g in range(4)]
                         + [(K["ones"][0:1, 0:P], W["a1_b1"][0:1, :])], xo, None, [x1])
            feed_forward(c, W, K, "a1", xo, [x1], x1)
            sum_and_norm(c, None, None, x1, [x1], W["E_g2"], W["E_s2"])
        c.end_stage()
        with ExitStack() as second:
            W = load_stage(c, second, ["a2_q", "a2_wk", "a2_wv", "a2_li1", "a2_b1", "a2_xg", "a2_xs", "*a2_gain_row", "*a2_shift_row",
                                       "a2_g3", "a2_s3", "a2_w2", "a2_b2", "a2_w3", "a2_b3"])
            norm_context(c, W, K, normed_ctx, plain_ctx)
            query_parts = nc.dram_tensor("query_parts_E", (LEVELS, 4 * P, N), BF16).ap()
            with ExitStack() as inner:
                QT = c.sbuf(inner, "QT", [P, 4, N])
                hat, hatT = c.sbuf(inner, "hat", [P, NT, P]), c.sbuf(inner, "hatT", [P, N])
                sum_and_norm(c, None, None, hat, [x1])
                turn_tokens(c, hatT, hat, K["ident"], (W["a2_xg"][:, 0:1], W["a2_xs"][:, 0:1]))
                products(c, [j for g in range(4) for j in project(QT[:, g, :], W["a2_q"][:, g * P:g * P + P], hatT)])
                split_features(c, feature_groups(QT, query_parts))
            O = c.sbuf(second, "O", [P, NT, 4 * P])
            cross_attention(c, query_parts, O, W["a2_wk"], W["a2_wv"], normed_ctx, plain_ctx, K, 32, False,
                            32 ** -0.5)
            OT = c.sbuf(second, "OT", [P, 4, N])
            turn_wide(c, OT, O, K)
            xo = c.sbuf(second, "xo", [P, NT, P])
            sum_and_norm(c, lambda t: [(tok(OT[:, g, :], t), W["a2_li1"][:, g, :]) for g in range(4)]
                         + [(K["ones"][0:1, 0:P], W["a2_b1"][0:1, :])], xo, None, [x1])
            feed_forward(c, W, K, "a2", xo, [x1, x], x1)
        sum_and_norm(c, None, None, x, [x1])


def stage_routed(c, x, K):
    nc = c.nc
    ROW = P + 2 * E2
    table = nc.dram_tensor("token_table", (N, ROW), F32).ap()
    results = nc.dram_tensor("slot_results", (2 * N, P), F32).ap()
    with ExitStack() as ctx:
        W = load_stage(c, ctx, ["F_r1", "F_r1s", "F_b1", "F_r2", "iota32", "double_token"])
        zeroed = zero_rows(c, ctx, results)
        rows = c.sbuf(ctx, "rows", [P, NT, ROW])
        indexT = c.sbuf(ctx, "indexT", [CAP2, E2], I32)
        with ExitStack() as inner:
            xT = c.sbuf(inner, "xT", [P, N])
            st = c.sbuf(inner, "st", [P, NT, 6])
            stT = c.sbuf(inner, "stT", [6, N])
            hT = c.sbuf(inner, "hT", [64, N])
            token_statistics(c, x, st)
            turn_tokens(c, xT, x, K["ident"])
            turn_tokens(c, stT, st, K["ident"])
            products(c, [(hT[:, k * BANK:k * BANK + BANK], [(W["F_r1"][:], chunk(xT, k)), (W["F_r1s"][:], stT[:, k * BANK:k * BANK + BANK])],
                          ("gelu", W["F_b1"][:, 0:1])) for k in range(CH)])
            probs, top, hot = choose_two(c, inner, lambda t: (hT[:, t * P:t * P + P], W["F_r2"][:]), E2, W["iota32"])
            score = c.sbuf(inner, "score", [P, NT, E2])
            wsum, wnorm = c.sbuf(inner, "wsum", [P, NT]), c.sbuf(inner, "wnorm", [P, 2, NT])
            routed, tmp = c.sbuf(inner, "routed", [P, NT, E2]), c.sbuf(inner, "tmp", [P, NT, E2])
            with nc.Block() as block:
                @block.vector
                def _(dve):
                    dve.tensor_copy(rows[:, :, 0:P], x[:])
                    dve.tensor_tensor(wsum[:], top[:, :, 0], top[:, :, 1], ALU.add)
                    dve.tensor_tensor(routed[:], hot[0][:], hot[1][:], ALU.add)
                    dve.drain()
                    dve.reciprocal(wsum[:], wsum[:])
                    dve.tensor_tensor(score[:], probs[:], routed[:], ALU.mult)
                    dve.drain()
                    for k in range(2):
                        dve.tensor_tensor(wnorm[:, k, :], top[:, :, k], wsum[:], ALU.mult)
                    dve.scalar_tensor_tensor(out=score[:], in0=routed[:], scalar=-1.0, in1=score[:], op0=ALU.add, op1=ALU.add)
                    dve.scalar_tensor_tensor(out=tmp[:], in0=routed[:], scalar=-BIG, in1=hot[1][:], op0=ALU.mult, op1=ALU.add)
                    dve.drain()
                    dve.tensor_tensor(rows[:, :, P + E2:ROW], tmp[:], W["double_token"][:].unsqueeze(2).to_broadcast([P, NT, E2]),
                                      ALU.add)
                    dve.tensor_tensor(rows[:, :, P:P + E2], hot[0][:], wnorm[:, 0, :].unsqueeze(2).to_broadcast([P, NT, E2]),
                                      ALU.mult)
                    dve.tensor_tensor(routed[:], hot[1][:], wnorm[:, 1, :].unsqueeze(2).to_broadcast([P, NT, E2]), ALU.mult)
                    dve.drain()
                    dve.tensor_tensor(rows[:, :, P:P + E2], rows[:, :, P:P + E2], routed[:], ALU.add)
            scoreT = [c.sbuf(inner, f"scoreT{k}", [E2, N]) for k in range(2)]
            turn_tokens(c, scoreT[0], score, K["ident"])
            choose_tokens(c, scoreT, indexT, table, rows, K)
        routed_experts(c, K, table, results, indexT, zeroed)
        back = c.sbuf(ctx, "back", [P, NT, 2, P])
        came = c.sem("results_loaded")
        total = c.sbuf(ctx, "total", [P, NT, P])
        with nc.Block() as block:
            @block.sync
            def _(sp):
                sp.dma_start(back[:].rearrange("p t k d -> p t (k d)"), results.rearrange("(t p k) d -> p t (k d)", p=P, k=2))\
                  .then_inc(came, 16)

            @block.vector
            def _(dve):
                dve.wait_ge(came, 16)
                dve.tensor_tensor(total[:], back[:, :, 0, :], back[:, :, 1, :], ALU.add)
                dve.drain()
                dve.tensor_tensor(total[:], total[:], x[:], ALU.add)
        sum_and_norm(c, None, None, x, [total])


def token_statistics(c, x, st):
    nc = c.nc
    with ExitStack() as ctx:
        stats, moments = c.sbuf(ctx, "stats", [P, NT, 6]), c.sbuf(ctx, "moments", [P, NT, 2])
        roots, near = c.sbuf(ctx, "roots", [P, 2, NT]), c.sbuf(ctx, "near", [P, NT, P])
        zeros = c.sem("near_zeros")
        squares, rooted = c.sem("squares"), c.sem("rooted")
        block = ctx.enter_context(nc.Block())

        @block.vector
        def _(dve):
            for t in range(NT):
                dve.bn_stats(stats[:, t, :], x[:, t, :])
            dve.drain()
            for t in range(NT):
                dve.bn_aggr(moments[:, t, :], stats[:, t, :])
            dve.drain()
            dve.tensor_scalar(roots[:, 0, :], moments[:, :, 1], P / (P - 1.0), None, ALU.mult)
            dve.tensor_tensor(roots[:, 1, :], moments[:, :, 0], moments[:, :, 0], ALU.mult)
            dve.drain()
            dve.tensor_tensor(roots[:, 1, :], roots[:, 1, :], moments[:, :, 1], ALU.add)
            dve.drain()
            dve.tensor_scalar(roots[:, 1, :], roots[:, 1, :], float(P), None, ALU.mult).then_inc(squares, 1)
            dve.tensor_copy(st[:, :, 0], moments[:, :, 0])
            dve.tensor_reduce(st[:, :, 2], x[:], AX_X, ALU.min)
            dve.tensor_reduce(st[:, :, 3], x[:], AX_X, ALU.max)
            dve.tensor_scalar(near[:], x[:], 1e-6, None, ALU.is_lt)
            dve.drain()
            dve.scalar_tensor_tensor(out=near[:], in0=x[:], scalar=-1e-6, in1=near[:], op0=ALU.is_gt, op1=ALU.mult)
            dve.drain()
            dve.tensor_reduce(st[:, :, 5], near[:], AX_X, ALU.add)
            dve.drain()
            dve.tensor_scalar(st[:, :, 5], st[:, :, 5], 1.0 / P, None, ALU.mult)
            dve.wait_ge(rooted, 1)
            dve.tensor_copy(st[:, :, 1], roots[:, 0, :])
            dve.tensor_copy(st[:, :, 4], roots[:, 1, :])

        @block.scalar
        def _(act):
            act.wait_ge(squares, 1)
            act.activation(roots[:], roots[:], ACT.Sqrt).then_inc(rooted, 1)


def choose_tokens(c, scoreT, indexT, table, rows, K):
    nc = c.nc
    with ExitStack() as ctx:
        best = c.sbuf(ctx, "best", [E2, CAP2])
        index, indexf = c.sbuf(ctx, "index", [E2, CAP2], U32), c.sbuf(ctx, "indexf", [E2, CAP2])
        turned = c.psum(ctx, "turned", [CAP2, E2])
        stored, ready, turned_ready = c.sem("table_stored"), c.sem("index_ready"), c.sem("turned_ready")
        block = ctx.enter_context(nc.Block())

        @block.sync
        def _(sp):
            sp.dma_start(table.rearrange("(t p) w -> p t w", p=P), rows[:]).then_inc(stored, 16)
            sp.wait_ge(stored, 16)

        @block.vector
        def _(dve):
            for r in range(CAP2 // 8):
                now, then, eight = scoreT[r % 2], scoreT[1 - r % 2], slice(8 * r, 8 * r + 8)
                dve.max(best[:, eight], now[:])
                dve.drain()
                dve.max_index(index[:, eight], best[:, eight], now[:])
                dve.match_replace(then[:], best[:, eight], now[:], -2.0)
                dve.drain()
            dve.tensor_copy(indexf[:], index[:]).then_inc(ready, 1)
            dve.wait_ge(turned_ready, 1)
            dve.tensor_copy(indexT[:], turned[:])

        @block.tensor
        def _(pe):
            pe.wait_ge(ready, 1)
            pe.transpose(turned[:], indexf[:], K["ident"][0:E2, 0:E2]).then_inc(turned_ready, 1)


def routed_experts(c, K, table, results, indexT, zeroed):
    nc = c.nc
    ROW = table.shape[1]
    LOOPS = E2 // 4
    with ExitStack() as ctx:
        xg = c.sbuf(ctx, "token_rows", [CAP2, 4, ROW])
        which = c.sbuf(ctx, "which", [CAP2, 4], I32)
        target = c.sbuf(ctx, "target", [CAP2, 2], I32)
        xgT = c.sbuf(ctx, "tokenT", [P, 2, CAP2])
        wu, wd = c.sbuf(ctx, "w_up", [P, 2, 512]), c.sbuf(ctx, "w_down", [P, 2, 2, P])
        au, ad = c.sbuf(ctx, "a_up", [P, 2, 2 * P]), c.sbuf(ctx, "a_down", [P, 2, P])
        gate = c.sbuf(ctx, "gate", [P, 2, 3 * CAP2])
        hid = c.sbuf(ctx, "hidden", [P, 2, 3 * CAP2])
        res = c.sbuf(ctx, "result", [CAP2, 2, P])
        turned = c.psum(ctx, "turned", [P, 2, BANK])
        up = c.psum(ctx, "up", [P, 2, BANK])
        down = c.psum(ctx, "down", [P, 2, BANK])
        weights = [c.sem("weights0"), c.sem("weights1")]
        adapters = [c.sem("adapters0"), c.sem("adapters1")]
        which_ready, gathered = c.sem("which_ready"), [c.sem(f"gathered{k}", True) for k in range(4)]
        turned_ready, token_ready = c.sem("turned_ready"), c.sem("token_ready")
        up_ready, gate_ready, hidden_ready = c.sem("up_ready"), c.sem("gate_ready"), c.sem("hidden_ready")
        down_ready, result_ready = c.sem("down_ready"), c.sem("result_ready")
        scattered = [c.sem("scattered0", True), c.sem("scattered1", True)]
        block = ctx.enter_context(nc.Block())

        @block.sync
        def _(sp):
            with sp.Fori(0, LOOPS, 1) as i:
                for k in range(4):
                    e, s, p = i * 4 + k, k % 2, k // 2
                    sp.wait_ge(down_ready, e + 3)
                    sp.sem_inc(c.seen, 1)
                    if s == 0:
                        pair = i * 2 + p
                        sp.dma_start(au[:, p, :], c.ins["F_aup"][bass.ds(pair, 1), :, :].rearrange("o p j -> (o p) j"))\
                          .then_inc(adapters[p], 16)
                        sp.dma_start(ad[:, p, :], c.ins["F_adown"][bass.ds(pair, 1), :, :].rearrange("o p j -> (o p) j"))\
                          .then_inc(adapters[p], 16)
                    sp.dma_start(wu[:, s, :], c.ins["F_up"][bass.ds(e, 1), :, :].rearrange("o p j -> (o p) j"))\
                      .then_inc(weights[s], 16)
                    sp.dma_start(wd[:, s, :, :], c.ins["F_down"][bass.ds(e, 1), :, :, :].rearrange("o p j d -> (o p) j d"))\
                      .then_inc(weights[s], 16)

        def over_bodies(eng, body):
            body(0, True, False)
            with eng.Fori(1, LOOPS - 1, 1) as i:
                body(i, False, False)
            body(LOOPS - 1, False, True)

        @block.gpsimd
        def _(pool):
            def gather(e, k):
                pool.wait_ge(which_ready, e + 1)
                pool.sem_inc(c.seen, 1)
                pool.indirect_dma_start(xg[:, k, :], None, table, bass.IndirectOffsetOnAxis(which[:, k:k + 1], 0))\
                    .then_inc(gathered[k], 16)

            def body(i, first, last):
                for p in range(2):
                    if not (last and p == 1):
                        for s in range(2):
                            gather(i * 4 + 2 * p + s + 2, (2 * p + s + 2) % 4)
                    for s in range(2):
                        pool.wait_ge(result_ready, i * 4 + 2 * p + s + 1)
                        pool.sem_inc(c.seen, 1)
                        pool.indirect_dma_start(results, bass.IndirectOffsetOnAxis(target[:, s:s + 1], 0), res[:, s, :], None,
                                                bounds_check=2 * N - 1, oob_is_err=False).then_inc(scattered[s], 16)

            for s in range(2):
                gather(s, s)
            pool.wait_ge(*zeroed)
            over_bodies(pool, body)
            for s in range(2):
                pool.wait_ge(scattered[s], 16 * (E2 // 2))

        @block.tensor
        def _(pe):
            pe.sem_inc(down_ready, 4)
            with pe.Fori(0, LOOPS, 1) as i:
                for p in range(2):
                    for s in range(2):
                        e, k = i * 4 + 2 * p + s, 2 * p + s
                        pe.wait_ge(gathered[k], i * 16 + 16)
                        pe.wait_ge(token_ready, e + 1)
                        pe.transpose(turned[:, s, 0:CAP2], xg[:, k, 0:P], K["ident"][0:CAP2, 0:CAP2]).then_inc(turned_ready, 1)
                    for s in range(2):
                        e = i * 4 + 2 * p + s
                        pe.wait_ge(weights[s], i * 64 + p * 32 + 32)
                        pe.wait_ge(adapters[p], i * 32 + 32)
                        pe.wait_ge(token_ready, e + 3)
                        pe.wait_ge(hidden_ready, e + 1)
                        for n, w in enumerate([wu[:, s, 0:P], wu[:, s, P:2 * P], au[:, p, 0:P], wu[:, s, 2 * P:3 * P],
                                               wu[:, s, 3 * P:4 * P], au[:, p, P:2 * P]]):
                            op = pe.matmul(up[:, s, n * CAP2:n * CAP2 + CAP2], w, xgT[:, s, :], start=True, stop=True)
                        op.then_inc(up_ready, 1)
                    for s in range(2):
                        e = i * 4 + 2 * p + s
                        pe.wait_ge(hidden_ready, e + 3)
                        for n, w in enumerate([wd[:, s, 0, :], wd[:, s, 1, :], ad[:, p, :]]):
                            op = pe.matmul(down[0:CAP2, s, 0:P], hid[:, s, n * CAP2:n * CAP2 + CAP2], w,
                                           start=n == 0, stop=n == 2)
                        op.then_inc(down_ready, 1)

        @block.scalar
        def _(act):
            with act.Fori(0, E2 // 2, 1) as i:
                for s in range(2):
                    e = i * 2 + s
                    act.wait_ge(up_ready, e + 1)
                    act.activation(gate[:, s, :], up[:, s, 0:3 * CAP2], ACT.Silu).then_inc(gate_ready, 1)

        @block.vector
        def _(dve):
            dve.sem_inc(token_ready, 2)
            dve.sem_inc(hidden_ready, 2)

            def choose(e, k):
                dve.tensor_copy(which[:, k:k + 1], indexT[:, bass.ds(e, 1)]).then_inc(which_ready, 1)

            def pair(i, p, first, last):
                for s in range(2):
                    e, k = i * 4 + 2 * p + s, 2 * p + s
                    dve.wait_ge(turned_ready, e + 1)
                    dve.tensor_copy(xgT[:, s, :], turned[:, s, 0:CAP2]).then_inc(token_ready, 1)
                if not last:
                    for s in range(2):
                        choose(i * 4 + 2 * p + s + 2, (2 * p + s + 2) % 4)
                for s in range(2):
                    e = i * 4 + 2 * p + s
                    dve.wait_ge(gate_ready, e + 1)
                    dve.tensor_tensor(hid[:, s, 0:2 * CAP2], gate[:, s, 0:2 * CAP2], up[:, s, 3 * CAP2:5 * CAP2], ALU.mult)
                    dve.scalar_tensor_tensor(out=hid[:, s, 2 * CAP2:], in0=gate[:, s, 2 * CAP2:], scalar=0.05,
                                             in1=up[:, s, 5 * CAP2:6 * CAP2], op0=ALU.mult, op1=ALU.mult)\
                       .then_inc(hidden_ready, 1)
                for s in range(2):
                    e, k = i * 4 + 2 * p + s, 2 * p + s
                    if not first:
                        dve.wait_ge(scattered[s], i * 32 + p * 16)
                    dve.tensor_copy(target[:, s:s + 1], xg[:, k, bass.ds(e + P + E2, 1)])
                    dve.wait_ge(down_ready, e + 5)
                    dve.tensor_scalar(res[:, s, :], down[0:CAP2, s, 0:P], xg[:, k, bass.ds(e + P, 1)], None, ALU.mult)\
                       .then_inc(result_ready, 1)
                dve.drain()

            def body(i, first, last):
                for p in range(2):
                    pair(i, p, first and p == 0, last and p == 1)

            for s in range(2):
                choose(s, s)
            over_bodies(dve, body)


STAGES = [stage_mla, stage_self_and_cross, stage_moe, stage_single_head, stage_two_blocks, stage_routed]


def build_program(nc, ins, out, stages=STAGES):
    with ExitStack() as ctx:
        c = Core(nc, ctx, ins)
        x = c.sbuf(ctx, "x", [P, NT, P])
        K = load_stage(c, ctx, ["ident", "identb", "causal_bias", "future_mask", "row_pickers", "ones"])
        came = c.sem("x_loaded")
        with nc.Block() as block:
            @block.sync
            def _(sp):
                sp.dma_start(x[:], ins["x"].rearrange("(t p) d -> p t d", p=P)).then_inc(came, 16)
                sp.wait_ge(came, 16)
        c.end_stage()
        for stage in stages:
            stage(c, x, K)
            c.end_stage()
        gone = c.sem("out_stored")
        with nc.Block() as block:
            @block.sync
            def _(sp):
                sp.dma_start(out.rearrange("(t p) d -> p t d", p=P), x[:]).then_inc(gone, 16)
                sp.wait_ge(gone, 16)


def constants():
    import numpy as np
    f = np.float32
    K = {}
    K["ident"] = np.eye(P, dtype=f)
    K["identb"] = np.eye(P).astype(mybir.dt.np(BF16))
    q, k = np.arange(P)[:, None], np.arange(P)[None, :]
    bias = np.zeros((P, T), f)
    bias[:, P:] = np.where(k <= q, 0.0, -1e30)
    K["causal_bias"] = bias.astype(mybir.dt.np(BF16))
    K["future_mask"] = (k > q).astype(f)
    pick = np.zeros((P, 2 * P), f)
    pick[:, 96] = pick[:, P + 97] = 1
    K["row_pickers"] = pick.astype(mybir.dt.np(BF16))
    K["ones"] = np.ones((1, P), f)
    K["all_ones"] = np.ones((P, P), f)
    K["upto"] = (q <= k).astype(f)
    K["iota8"] = np.tile(np.arange(E1, dtype=f), (P, 1))
    K["iota32"] = np.tile(np.arange(E2, dtype=f), (P, 1))
    K["slot_base"] = np.tile(np.arange(E1, dtype=f) * CAP1 - 1, (P, 1))
    K["double_token"] = (2 * (np.arange(NT)[None, :] * P + np.arange(P)[:, None]) + BIG).astype(f)

    def rope(width, rows):
        inv = (f(1.0) / f(10000.0) ** (np.arange(0, width, 2, dtype=f) / f(width))).astype(f)
        ang = np.outer(np.arange(T, dtype=f), inv).astype(f)
        i = np.arange(P)
        cos, sin = np.cos(ang)[:, i % (width // 2)].T, np.sin(ang)[:, i % (width // 2)].T
        sin = sin * np.where(i % width < width // 2, -1, 1)[:, None]
        cos, sin = cos.astype(f), sin.astype(f)
        return np.tile(cos, (1, 2)), np.tile(sin, (1, 2))

    K["A_cos"], K["A_sin"] = rope(32, 32)
    K["C_cos"], K["C_sin"] = rope(8, P)
    return K


def layouts(I):
    import numpy as np
    f = np.float32
    I = {k: np.asarray(v) for k, v in I.items()}
    L = {"x": np.ascontiguousarray(I["x"].reshape(N, P))}

    def pad_cols(w, n):
        z = np.zeros((w.shape[0], n), f)
        z[:, :w.shape[1]] = w
        return z

    def values(w, bias, d):
        wz = np.zeros((w.shape[0], H, d + 1), f)
        wz[:, :, :d] = w.reshape(w.shape[0], H, d)
        row = np.zeros((1, H, d + 1), f)
        row[0, :, :d] = 0 if bias is None else bias.reshape(H, d)
        row[0, :, d] = 1
        return wz.reshape(w.shape[0], -1), row.reshape(1, -1)

    def halves_swapped(w, width):
        n = w.shape[1] // width
        return w.reshape(w.shape[0], n, 2, width // 2)[:, :, ::-1].reshape(w.shape[0], -1)

    p = "L0_attn_"
    L["A_kvd"], L["A_ku"], L["A_q"], L["A_wo"] = (I[p + k] for k in ("W_kv_down", "W_k_up", "W_q", "W_o"))
    L["A_vu"], L["A_vrow"] = values(I[p + "W_v_up"], None, 8)
    for k, w in (("A_qr", "W_q_rope"), ("A_kr", "W_k_rope")):
        L[k] = pad_cols(I[p + w], P)
        L[k + "s"] = pad_cols(halves_swapped(I[p + w], 32), P)

    def context_keys(w, bias):
        return np.concatenate([w, np.zeros((1, w.shape[1]), f) if bias is None else bias.reshape(1, -1)])

    def context_values(w, bias, d):
        wz, row = values(w, bias, d)
        z = np.zeros((P, wz.shape[1]), f)
        z[:CC], z[CC] = wz, row[0]
        return z

    p = "L0_xattn_"
    L["B_q"], L["B_k"], L["B_cq"], L["B_wp"] = (I[p + k] for k in ("Wq", "Wk", "Wcq", "Wp"))
    L["B_bq"], L["B_bk"], L["B_bcq"] = (I[p + k].reshape(P, 1) for k in ("bq", "bk", "bcq"))
    L["B_bp"] = I[p + "bp"].reshape(1, P)
    L["B_v"], L["B_vrow"] = values(I[p + "Wv"], I[p + "bv"], 8)
    L["B_wk"] = context_keys(I[p + "Wck"], I[p + "bck"])
    L["B_wv"] = context_values(I[p + "Wcv"], I[p + "bcv"], 8)
    L["ctxT"] = I["ctx_512"].transpose(0, 2, 1)
    L["ctx"] = I["ctx_512"]

    p = "L0_ffn_"
    qkv = I[p + "Wqkv"].reshape(P, H, 3, 8)
    L["C_q"], L["C_k"] = (qkv[:, :, k].reshape(P, P) for k in range(2))
    L["C_qs"], L["C_ks"] = halves_swapped(L["C_q"], 8), halves_swapped(L["C_k"], 8)
    L["C_v"], L["C_vrow"] = values(qkv[:, :, 2].reshape(P, P), None, 8)
    L["C_proj"], L["C_gate"] = I[p + "Wproj"], I[p + "Wgate"]
    for n, k in (("C_g1", "ln1_g"), ("C_s1", "ln1_b"), ("C_g2", "ln2_g"), ("C_s2", "ln2_b")):
        L[n] = I[p + k].reshape(P, 1)
    L["C_w1"] = I[p + "W1"]
    L["C_w2"] = I[p + "W2"].reshape(E1, F1 // P, P, P).transpose(0, 2, 1, 3)
    L["C_b1"] = I[p + "b1"].reshape(E1 * F1 // P, P).T
    L["C_b2"] = I[p + "b2"].reshape(1, E1 * P)

    L["D_q"], L["D_k"] = I["L1_attn_Wq"].T, I["L1_attn_Wk"].T
    L["D_v"] = pad_cols(I["L1_attn_Wv"].T, P + 1)
    L["D_vrow"] = np.zeros((1, P + 1), f)
    L["D_vrow"][0, P] = 1

    p = "L1_xattn_"
    for n, k in (("E_g1", "ln1_g"), ("E_s1", "ln1_b"), ("E_g2", "ln2_g"), ("E_s2", "ln2_b")):
        L[n] = I[p + k].reshape(1, P)
    for a in ("a1_", "a2_"):
        by_head = lambda w: w.transpose(1, 0, 2).reshape(w.shape[1], -1)
        L[a + "q"] = by_head(I[p + a + "wq"])
        wk, wv = by_head(I[p + a + "wk"]), by_head(I[p + a + "wv"])
        if a == "a1_":
            L["a1_k"] = wk
            L["a1_v"], L["a1_vrow"] = values(wv, None, 32)
        else:
            L["a2_wk"], L["a2_wv"] = context_keys(wk, None), context_values(wv, None, 32)
        L[a + "li1"] = I[p + a + "li1_w"].reshape(4, P, P).transpose(1, 0, 2)
        L[a + "b1"] = I[p + a + "li1_b"].reshape(1, P)
        for n, k in (("xg", "lnx_g"), ("xs", "lnx_b"), ("yg", "lny_g"), ("ys", "lny_b"), ("g3", "ln3_g"), ("s3", "ln3_b")):
            L[a + n] = I[p + a + k].reshape(-1, 1)
        L[a + "w2"] = I[p + a + "li2_w"]
        L[a + "b2"] = I[p + a + "li2_b"].reshape(4, P).T
        L[a + "w3"] = I[p + a + "li3_w"].reshape(4, P, P).transpose(1, 0, 2)
        L[a + "b3"] = I[p + a + "li3_b"].reshape(1, P)

    L["a2_gain_row"], L["a2_shift_row"] = (I[p + "a2_" + k].reshape(1, -1) for k in ("lny_g", "lny_b"))

    p = "L1_ffn_"
    L["F_r1"], L["F_r1s"] = I[p + "r1_w"][:, :P].T, I[p + "r1_w"][:, P:].T
    L["F_b1"], L["F_r2"] = I[p + "r1_b"].reshape(64, 1), I[p + "r2_w"].T
    L["F_up"] = I[p + "w_up"].transpose(0, 2, 1)
    L["F_down"] = I[p + "w_down"].transpose(0, 2, 1).reshape(E2, 2, P, P).transpose(0, 2, 1, 3)
    L["F_aup"], L["F_adown"] = I[p + "a_up"].transpose(0, 2, 1), I[p + "a_down"].transpose(0, 2, 1)
    return {k: np.ascontiguousarray(v) for k, v in L.items()}


def launch_arrays(inputs):
    arrays = layouts(inputs)
    arrays.update(constants())
    return {f"in_{k}": v for k, v in arrays.items()}


def make(nc, arrays, stages=STAGES):
    from concourse import mybir as _mybir
    ins = {k[3:]: nc.dram_tensor(k, v.shape, _mybir.dt.from_np(v.dtype), kind="ExternalInput").ap()
           for k, v in arrays.items()}
    out = nc.dram_tensor("out", (N, P), F32, kind="ExternalOutput").ap()
    build_program(nc, ins, out, stages)


def kernel(**inputs):
    import concourse.bacc as _bacc
    from concourse.bass_utils import run_bass_kernel_spmd as _run
    arrays = launch_arrays(inputs)
    nc = _bacc.Bacc("TRN2", target_bir_lowering=False, num_devices=1)
    make(nc, arrays)
    r = _run(nc, [arrays], core_ids=[0])
    return r.results[0]["out"].reshape(B, T, P)
```
